# Optimizing a Trainium2 kernel written in Bass

```python
import numpy as np
import jax
import jax.numpy as jnp

def _softmax(x, axis=-1):
    return jax.nn.softmax(x, axis=axis)

def _gelu(x):
    return jax.nn.gelu(x, approximate=True)

def _silu(x):
    return jax.nn.silu(x)

def _sigmoid(x):
    return jax.nn.sigmoid(x)

def _layernorm(x, axis=-1, eps=1e-05):
    m = jnp.mean(x, axis=axis, keepdims=True)
    v = jnp.var(x, axis=axis, keepdims=True)
    return (x - m) / jnp.sqrt(v + eps)

def _scatter_add(tgt, idx, src, axis=0):
    return tgt.at[idx].add(src)

def _segment_sum(src, seg, n):
    return jax.ops.segment_sum(src, seg, n)
kernel_name = 'mk_hybrid_d1_jaxref_r8_27f811'

def setup_inputs(seed: int=0):
    np.random.seed(seed)
    _w = jnp.asarray

    def _L0_attn_a_setup():
        import jax, jax.numpy as jnp
        import numpy as np
        HIDDEN = 128
        NUM_HEADS = 16
        B, S = (2, 256)

        def _mha(x, w_in, b_in, w_out, b_out, num_heads):
            lead = x.shape[:-2]
            L, E = (x.shape[-2], x.shape[-1])
            dh = E // num_heads
            qkv = x @ w_in.T + b_in
            q, k, v = jnp.split(qkv, 3, axis=-1)
            q = q.reshape(lead + (L, num_heads, dh)) * dh ** (-0.5)
            k = k.reshape(lead + (L, num_heads, dh))
            v = v.reshape(lead + (L, num_heads, dh))
            scores = jnp.einsum('...qhd,...khd->...hqk', q, k)
            probs = jax.nn.softmax(scores, axis=-1)
            out = jnp.einsum('...hqk,...khd->...qhd', probs, v).reshape(lead + (L, E))
            return out @ w_out.T + b_out
        key = jax.random.key(seed)
        ks = jax.random.split(key, 12)
        E = HIDDEN
        s_in = 1.0 / np.sqrt(E)
        inp = {'x': jax.random.normal(ks[0], (B, S, E), dtype=jnp.float32), 'w_in_g': jax.random.normal(ks[1], (3 * E, E), dtype=jnp.float32) * s_in, 'b_in_g': jnp.zeros((3 * E,), dtype=jnp.float32), 'w_out_g': jax.random.normal(ks[2], (E, E), dtype=jnp.float32) * s_in, 'b_out_g': jnp.zeros((E,), dtype=jnp.float32), 'w_in_l': jax.random.normal(ks[3], (3 * E, E), dtype=jnp.float32) * s_in, 'b_in_l': jnp.zeros((3 * E,), dtype=jnp.float32), 'w_out_l': jax.random.normal(ks[4], (E, E), dtype=jnp.float32) * s_in, 'b_out_l': jnp.zeros((E,), dtype=jnp.float32), 'w_f': jax.random.normal(ks[5], (E, 2 * E), dtype=jnp.float32) * (1.0 / np.sqrt(2 * E)), 'b_f': jnp.zeros((E,), dtype=jnp.float32)}
        return inp
    _L0_attn_a_in = _L0_attn_a_setup()

    def _L0_attn_b_setup():
        import jax, jax.numpy as jnp
        import numpy as np
        NUM_HEADS = 8
        SCALE_BASE = 512.0
        GN_EPS = 1e-05

        def rotate_every_two(x):
            x1 = x[..., ::2]
            x2 = x[..., 1::2]
            return jnp.stack([-x2, x1], axis=-1).reshape(x.shape)

        def xpos_apply(x, downscale):
            L, D = (x.shape[1], x.shape[2])
            half = D // 2
            scale_vec = (jnp.arange(0, D, 2, dtype=jnp.float32) + 0.4 * D) / (1.4 * D)
            pos = jnp.arange(L, dtype=jnp.float32)
            scale = scale_vec[None, :] ** (pos[:, None] / SCALE_BASE)
            inv_freq = 1.0 / 10000.0 ** (jnp.arange(half, dtype=jnp.float32) / half)
            sinusoid = pos[:, None] * inv_freq[None, :]
            sin, cos = (jnp.sin(sinusoid), jnp.cos(sinusoid))
            if downscale:
                scale = 1.0 / scale
            sin_s = jnp.repeat(sin * scale, 2, axis=-1)
            cos_s = jnp.repeat(cos * scale, 2, axis=-1)
            return x * cos_s + rotate_every_two(x) * sin_s

        def decay_mask_fn(T, num_heads):
            s, e = (np.log(1.0 / 32.0), np.log(1.0 / 512.0))
            gamma = 1.0 - jnp.exp(jnp.linspace(s, e, num_heads).astype(jnp.float32))
            log_decay = jnp.log(gamma)
            idx = jnp.arange(T)
            expo = (idx[:, None] - idx[None, :]).astype(jnp.float32)
            tri = idx[:, None] >= idx[None, :]
            expo_safe = jnp.where(tri, expo, 0.0)
            mask = jnp.exp(log_decay[:, None, None] * expo_safe) * tri
            scale = jnp.sqrt(mask.sum(axis=-1, keepdims=True))
            return mask / scale

        def _reference_tuple_inner(hidden_states, w_qkv, b_qkv, w_g, b_g, w_p, b_p):
            B, T, E = hidden_states.shape
            H = NUM_HEADS
            V = 2 * E
            dk, dv = (E // H, V // H)
            qkv = hidden_states @ w_qkv + b_qkv
            q, k, v = (qkv[..., :E], qkv[..., E:2 * E], qkv[..., 2 * E:])
            q = xpos_apply(q, downscale=False)
            k = xpos_apply(k, downscale=True)
            q = q.reshape(B, T, H, dk).transpose(0, 2, 1, 3)
            k = k.reshape(B, T, H, dk).transpose(0, 2, 1, 3)
            v = v.reshape(B, T, H, dv).transpose(0, 2, 1, 3)
            mask = decay_mask_fn(T, H)
            retention = jnp.einsum('bhid,bhjd->bhij', q, k) * dk ** (-0.5)
            retention = retention * mask[None]
            out = jnp.einsum('bhij,bhjv->bhiv', retention, v)
            curr_kv = jnp.einsum('hj,bhjk,bhjv->bhkv', mask[:, -1, :], k, v)
            retention_out = out.transpose(0, 2, 1, 3).reshape(B, T, V)
            g = retention_out.reshape(B * T, H, dv)
            mu = g.mean(axis=-1, keepdims=True)
            var = ((g - mu) ** 2).mean(axis=-1, keepdims=True)
            normed = ((g - mu) / jnp.sqrt(var + GN_EPS)).reshape(B, T, V)
            gated = jax.nn.silu(hidden_states @ w_g + b_g) * normed
            proj = gated @ w_p + b_p
            return (proj, curr_kv)
        key = jax.random.key(seed)
        ks = jax.random.split(key, 4)
        B, T, E = (2, 256, 128)
        V = 2 * E
        return {'hidden_states': jax.random.normal(ks[0], (B, T, E), dtype=jnp.float32), 'w_qkv': jax.random.normal(ks[1], (E, 2 * E + V), dtype=jnp.float32) * 0.02, 'b_qkv': jnp.zeros((2 * E + V,), dtype=jnp.float32), 'w_g': jax.random.normal(ks[2], (E, V), dtype=jnp.float32) * 0.02, 'b_g': jnp.zeros((V,), dtype=jnp.float32), 'w_p': jax.random.normal(ks[3], (V, E), dtype=jnp.float32) * 0.02, 'b_p': jnp.zeros((E,), dtype=jnp.float32)}
    _L0_attn_b_in = _L0_attn_b_setup()

    def _L0_ffn_setup():
        import jax, jax.numpy as jnp
        import numpy as np
        B, S, DIM = (4, 512, 128)
        BASE_COUPLING = 0.1
        NUM_CYCLES = 3

        def _gelu(x):
            return jax.nn.gelu(x, approximate=False)

        def _coupling_net(h, w1, b1, w2, b2, w3, b3, w4, b4):
            h = _gelu(h @ w1 + b1)
            h = _gelu(h @ w2 + b2)
            h = _gelu(h @ w3 + b3)
            return jax.nn.sigmoid(h @ w4 + b4)

        def _global_net(h, w1, b1, w2, b2, w3, b3):
            h = _gelu(h @ w1 + b1)
            h = _gelu(h @ w2 + b2)
            return jax.nn.sigmoid(h @ w3 + b3)

        def _twist(x):
            o_r, o_i, p_r, p_i = jnp.split(x, 4, axis=-1)
            return jnp.concatenate([p_r, -p_i, -o_r, o_i], axis=-1)
        key = jax.random.key(seed)
        ks = jax.random.split(key, 9)
        d = DIM

        def w(k, fan_in, fan_out):
            return jax.random.normal(k, (fan_in, fan_out), dtype=jnp.float32) / np.sqrt(fan_in).astype(np.float32)
        inp = {'x': jax.random.normal(ks[0], (B, S, d), dtype=jnp.float32)}
        cn_dims = [(d, d), (d, d // 2), (d // 2, d // 4), (d // 4, 1)]
        for i, (a, b) in enumerate(cn_dims):
            inp[f'cn_w{i + 1}'] = w(ks[1 + i], a, b)
            inp[f'cn_b{i + 1}'] = jnp.zeros((b,), dtype=jnp.float32)
        gc_dims = [(d, d // 2), (d // 2, d // 4), (d // 4, 1)]
        for i, (a, b) in enumerate(gc_dims):
            inp[f'gc_w{i + 1}'] = w(ks[5 + i], a, b)
            inp[f'gc_b{i + 1}'] = jnp.zeros((b,), dtype=jnp.float32)
        inp['adaptive_range'] = jnp.full((1,), 0.2, dtype=jnp.float32)
        return inp
    _L0_ffn_in = _L0_ffn_setup()
    _d = {'L0_attn_a_x': _L0_attn_a_in['x'], 'L0_attn_a_w_in_g': _L0_attn_a_in['w_in_g'], 'L0_attn_a_b_in_g': _L0_attn_a_in['b_in_g'], 'L0_attn_a_w_out_g': _L0_attn_a_in['w_out_g'], 'L0_attn_a_b_out_g': _L0_attn_a_in['b_out_g'], 'L0_attn_a_w_in_l': _L0_attn_a_in['w_in_l'], 'L0_attn_a_b_in_l': _L0_attn_a_in['b_in_l'], 'L0_attn_a_w_out_l': _L0_attn_a_in['w_out_l'], 'L0_attn_a_b_out_l': _L0_attn_a_in['b_out_l'], 'L0_attn_a_w_f': _L0_attn_a_in['w_f'], 'L0_attn_a_b_f': _L0_attn_a_in['b_f'], 'L0_attn_b_w_qkv': _L0_attn_b_in['w_qkv'], 'L0_attn_b_b_qkv': _L0_attn_b_in['b_qkv'], 'L0_attn_b_w_g': _L0_attn_b_in['w_g'], 'L0_attn_b_b_g': _L0_attn_b_in['b_g'], 'L0_attn_b_w_p': _L0_attn_b_in['w_p'], 'L0_attn_b_b_p': _L0_attn_b_in['b_p'], 'L0_ffn_cn_w1': _L0_ffn_in['cn_w1'], 'L0_ffn_cn_b1': _L0_ffn_in['cn_b1'], 'L0_ffn_cn_w2': _L0_ffn_in['cn_w2'], 'L0_ffn_cn_b2': _L0_ffn_in['cn_b2'], 'L0_ffn_cn_w3': _L0_ffn_in['cn_w3'], 'L0_ffn_cn_b3': _L0_ffn_in['cn_b3'], 'L0_ffn_cn_w4': _L0_ffn_in['cn_w4'], 'L0_ffn_cn_b4': _L0_ffn_in['cn_b4'], 'L0_ffn_gc_w1': _L0_ffn_in['gc_w1'], 'L0_ffn_gc_b1': _L0_ffn_in['gc_b1'], 'L0_ffn_gc_w2': _L0_ffn_in['gc_w2'], 'L0_ffn_gc_b2': _L0_ffn_in['gc_b2'], 'L0_ffn_gc_w3': _L0_ffn_in['gc_w3'], 'L0_ffn_gc_b3': _L0_ffn_in['gc_b3'], 'L0_ffn_adaptive_range': _L0_ffn_in['adaptive_range']}
    _x0 = _d['L0_attn_a_x']
    _d['L0_attn_a_x'] = jax.random.normal(jax.random.fold_in(jax.random.key(seed), 1), (8, 256, 128), dtype=_x0.dtype)
    del _x0
    return _d

def reference(L0_attn_a_x, L0_attn_a_w_in_g, L0_attn_a_b_in_g, L0_attn_a_w_out_g, L0_attn_a_b_out_g, L0_attn_a_w_in_l, L0_attn_a_b_in_l, L0_attn_a_w_out_l, L0_attn_a_b_out_l, L0_attn_a_w_f, L0_attn_a_b_f, L0_attn_b_w_qkv, L0_attn_b_b_qkv, L0_attn_b_w_g, L0_attn_b_b_g, L0_attn_b_w_p, L0_attn_b_b_p, L0_ffn_cn_w1, L0_ffn_cn_b1, L0_ffn_cn_w2, L0_ffn_cn_b2, L0_ffn_cn_w3, L0_ffn_cn_b3, L0_ffn_cn_w4, L0_ffn_cn_b4, L0_ffn_gc_w1, L0_ffn_gc_b1, L0_ffn_gc_w2, L0_ffn_gc_b2, L0_ffn_gc_w3, L0_ffn_gc_b3, L0_ffn_adaptive_range):

    def _L0_attn_a_ref(x, w_in_g, b_in_g, w_out_g, b_out_g, w_in_l, b_in_l, w_out_l, b_out_l, w_f, b_f):
        import jax, jax.numpy as jnp
        import numpy as np
        HIDDEN = 128
        NUM_HEADS = 16
        B, S = (2, 256)

        def _mha(x, w_in, b_in, w_out, b_out, num_heads):
            lead = x.shape[:-2]
            L, E = (x.shape[-2], x.shape[-1])
            dh = E // num_heads
            qkv = x @ w_in.T + b_in
            q, k, v = jnp.split(qkv, 3, axis=-1)
            q = q.reshape(lead + (L, num_heads, dh)) * dh ** (-0.5)
            k = k.reshape(lead + (L, num_heads, dh))
            v = v.reshape(lead + (L, num_heads, dh))
            scores = jnp.einsum('...qhd,...khd->...hqk', q, k)
            probs = jax.nn.softmax(scores, axis=-1)
            out = jnp.einsum('...hqk,...khd->...qhd', probs, v).reshape(lead + (L, E))
            return out @ w_out.T + b_out
        Bn, Sn, E = x.shape
        g = _mha(x, w_in_g, b_in_g, w_out_g, b_out_g, NUM_HEADS)
        sub_len = NUM_HEADS
        sub_num = Sn // sub_len
        xb = x.reshape(Bn, sub_num, sub_len, E)
        l = _mha(xb, w_in_l, b_in_l, w_out_l, b_out_l, NUM_HEADS).reshape(Bn, Sn, E)
        fused = jnp.concatenate([g, l], axis=-1)
        return fused @ w_f.T + b_f

    def _L0_attn_b_ref(hidden_states, w_qkv, b_qkv, w_g, b_g, w_p, b_p):
        import jax, jax.numpy as jnp
        import numpy as np
        NUM_HEADS = 8
        SCALE_BASE = 512.0
        GN_EPS = 1e-05

        def rotate_every_two(x):
            x1 = x[..., ::2]
            x2 = x[..., 1::2]
            return jnp.stack([-x2, x1], axis=-1).reshape(x.shape)

        def xpos_apply(x, downscale):
            L, D = (x.shape[1], x.shape[2])
            half = D // 2
            scale_vec = (jnp.arange(0, D, 2, dtype=jnp.float32) + 0.4 * D) / (1.4 * D)
            pos = jnp.arange(L, dtype=jnp.float32)
            scale = scale_vec[None, :] ** (pos[:, None] / SCALE_BASE)
            inv_freq = 1.0 / 10000.0 ** (jnp.arange(half, dtype=jnp.float32) / half)
            sinusoid = pos[:, None] * inv_freq[None, :]
            sin, cos = (jnp.sin(sinusoid), jnp.cos(sinusoid))
            if downscale:
                scale = 1.0 / scale
            sin_s = jnp.repeat(sin * scale, 2, axis=-1)
            cos_s = jnp.repeat(cos * scale, 2, axis=-1)
            return x * cos_s + rotate_every_two(x) * sin_s

        def decay_mask_fn(T, num_heads):
            s, e = (np.log(1.0 / 32.0), np.log(1.0 / 512.0))
            gamma = 1.0 - jnp.exp(jnp.linspace(s, e, num_heads).astype(jnp.float32))
            log_decay = jnp.log(gamma)
            idx = jnp.arange(T)
            expo = (idx[:, None] - idx[None, :]).astype(jnp.float32)
            tri = idx[:, None] >= idx[None, :]
            expo_safe = jnp.where(tri, expo, 0.0)
            mask = jnp.exp(log_decay[:, None, None] * expo_safe) * tri
            scale = jnp.sqrt(mask.sum(axis=-1, keepdims=True))
            return mask / scale

        def _reference_tuple_inner(hidden_states, w_qkv, b_qkv, w_g, b_g, w_p, b_p):
            B, T, E = hidden_states.shape
            H = NUM_HEADS
            V = 2 * E
            dk, dv = (E // H, V // H)
            qkv = hidden_states @ w_qkv + b_qkv
            q, k, v = (qkv[..., :E], qkv[..., E:2 * E], qkv[..., 2 * E:])
            q = xpos_apply(q, downscale=False)
            k = xpos_apply(k, downscale=True)
            q = q.reshape(B, T, H, dk).transpose(0, 2, 1, 3)
            k = k.reshape(B, T, H, dk).transpose(0, 2, 1, 3)
            v = v.reshape(B, T, H, dv).transpose(0, 2, 1, 3)
            mask = decay_mask_fn(T, H)
            retention = jnp.einsum('bhid,bhjd->bhij', q, k) * dk ** (-0.5)
            retention = retention * mask[None]
            out = jnp.einsum('bhij,bhjv->bhiv', retention, v)
            curr_kv = jnp.einsum('hj,bhjk,bhjv->bhkv', mask[:, -1, :], k, v)
            retention_out = out.transpose(0, 2, 1, 3).reshape(B, T, V)
            g = retention_out.reshape(B * T, H, dv)
            mu = g.mean(axis=-1, keepdims=True)
            var = ((g - mu) ** 2).mean(axis=-1, keepdims=True)
            normed = ((g - mu) / jnp.sqrt(var + GN_EPS)).reshape(B, T, V)
            gated = jax.nn.silu(hidden_states @ w_g + b_g) * normed
            proj = gated @ w_p + b_p
            return (proj, curr_kv)
        return _reference_tuple_inner(hidden_states, w_qkv, b_qkv, w_g, b_g, w_p, b_p)[0]

    def _L0_ffn_ref(x, cn_w1, cn_b1, cn_w2, cn_b2, cn_w3, cn_b3, cn_w4, cn_b4, gc_w1, gc_b1, gc_w2, gc_b2, gc_w3, gc_b3, adaptive_range):
        import jax, jax.numpy as jnp
        import numpy as np
        B, S, DIM = (4, 512, 128)
        BASE_COUPLING = 0.1
        NUM_CYCLES = 3

        def _gelu(x):
            return jax.nn.gelu(x, approximate=False)

        def _coupling_net(h, w1, b1, w2, b2, w3, b3, w4, b4):
            h = _gelu(h @ w1 + b1)
            h = _gelu(h @ w2 + b2)
            h = _gelu(h @ w3 + b3)
            return jax.nn.sigmoid(h @ w4 + b4)

        def _global_net(h, w1, b1, w2, b2, w3, b3):
            h = _gelu(h @ w1 + b1)
            h = _gelu(h @ w2 + b2)
            return jax.nn.sigmoid(h @ w3 + b3)

        def _twist(x):
            o_r, o_i, p_r, p_i = jnp.split(x, 4, axis=-1)
            return jnp.concatenate([p_r, -p_i, -o_r, o_i], axis=-1)
        global_context = x.mean(axis=1, keepdims=True)
        gf = _global_net(global_context, gc_w1, gc_b1, gc_w2, gc_b2, gc_w3, gc_b3)
        out = x
        for _ in range(NUM_CYCLES):
            tf = _coupling_net(out, cn_w1, cn_b1, cn_w2, cn_b2, cn_w3, cn_b3, cn_w4, cn_b4)
            combined = 0.7 * gf + 0.3 * tf
            coupling = BASE_COUPLING + adaptive_range * (combined - 0.5) * 2.0
            out = out + coupling * _twist(out)
        return out
    x = L0_attn_a_x
    x = x + _L0_attn_a_ref(_layernorm(x, axis=-1), L0_attn_a_w_in_g, L0_attn_a_b_in_g, L0_attn_a_w_out_g, L0_attn_a_b_out_g, L0_attn_a_w_in_l, L0_attn_a_b_in_l, L0_attn_a_w_out_l, L0_attn_a_b_out_l, L0_attn_a_w_f, L0_attn_a_b_f)
    x = x + _L0_ffn_ref(_layernorm(x, axis=-1), L0_ffn_cn_w1, L0_ffn_cn_b1, L0_ffn_cn_w2, L0_ffn_cn_b2, L0_ffn_cn_w3, L0_ffn_cn_b3, L0_ffn_cn_w4, L0_ffn_cn_b4, L0_ffn_gc_w1, L0_ffn_gc_b1, L0_ffn_gc_w2, L0_ffn_gc_b2, L0_ffn_gc_w3, L0_ffn_gc_b3, L0_ffn_adaptive_range)
    x = x + _L0_attn_b_ref(_layernorm(x, axis=-1), L0_attn_b_w_qkv, L0_attn_b_b_qkv, L0_attn_b_w_g, L0_attn_b_b_g, L0_attn_b_w_p, L0_attn_b_b_p)
    x = x + _L0_ffn_ref(_layernorm(x, axis=-1), L0_ffn_cn_w1, L0_ffn_cn_b1, L0_ffn_cn_w2, L0_ffn_cn_b2, L0_ffn_cn_w3, L0_ffn_cn_b3, L0_ffn_cn_w4, L0_ffn_cn_b4, L0_ffn_gc_w1, L0_ffn_gc_b1, L0_ffn_gc_w2, L0_ffn_gc_b2, L0_ffn_gc_w3, L0_ffn_gc_b3, L0_ffn_adaptive_range)
    return x

_drawn_inputs = setup_inputs


def setup_inputs(seed=0):
    import zlib

    import numpy as np

    out = dict(_drawn_inputs(seed))
    spreads = {'L0_attn_a_b_in_g': (0.0, 0.1),
     'L0_attn_a_b_out_g': (0.0, 0.1),
     'L0_attn_a_b_in_l': (0.0, 0.1),
     'L0_attn_a_b_out_l': (0.0, 0.1),
     'L0_attn_a_b_f': (0.0, 0.1),
     'L0_attn_b_b_qkv': (0.0, 0.482),
     'L0_attn_b_b_g': (0.0, 0.8),
     'L0_attn_b_b_p': (0.0, 0.1),
     'L0_ffn_cn_b1': (0.0, 0.8),
     'L0_ffn_cn_b2': (0.0, 2.0),
     'L0_ffn_cn_b3': (0.0, 2.0),
     'L0_ffn_gc_b1': (0.0, 0.8),
     'L0_ffn_gc_b2': (0.0, 0.8)}
    factors = {'L0_attn_b_w_qkv': 3.079,
     'L0_attn_b_w_g': 3.212,
     'L0_attn_b_w_p': 2.977,
     'L0_ffn_cn_w1': 5.039,
     'L0_ffn_cn_w2': 4.154,
     'L0_ffn_cn_w3': 3.61,
     'L0_ffn_gc_w1': 8.0,
     'L0_ffn_gc_w2': 4.962,
     'L0_ffn_gc_w3': 8.0}
    for name, (base, spread) in spreads.items():
        noise = np.random.default_rng([zlib.crc32(name.encode()), seed]).standard_normal(out[name].shape)
        drawn = base * np.exp(spread * noise) if base else spread * noise
        out[name] = jnp.asarray(drawn.astype(out[name].dtype))
    for name, factor in factors.items():
        out[name] = (out[name] * factor).astype(out[name].dtype)
    return out
```

```python
from contextlib import ExitStack

import concourse.bass as bass
from concourse import mybir

F32 = mybir.dt.float32
F32R = mybir.dt.float32r
ALU = mybir.AluOpType
ACT = mybir.ActivationFunctionType
AX_X = mybir.AxisListType.X

P = 128
BATCH, SEQ, E = 8, 256, 128
TOK = BATCH * SEQ
TILES = TOK // P
UT = 512
UNITS = TOK // UT
TPU = UT // P
EPS = 1e-5

AH, AD = 16, 8
AG, AJ = 4, 4
WIN = 16
A_SCALE = float(AD) ** -0.5
FAR = 2.0 ** 100

RH, RK, RV = 8, 16, 32


def columns(spec):
    at, out = 0, {}
    for name, width in spec:
        out[name] = (at, width)
        at += width
    return out, at


W_ATT, W_ATT_N = columns([
    ("in_g", 3 * E), ("in_l", 3 * E), ("out_g", E), ("out_l", E), ("f_g", E), ("f_l", E),
    ("b_in_g", 3), ("b_in_l", 3), ("b_v_g", 1), ("b_v_l", 1), ("b_out_g", 1), ("b_out_l", 1), ("b_f", E)])
W_REST, W_REST_N = columns([
    ("c1", E), ("c1p", E), ("c2", E // 2), ("c3", E // 2), ("c4r", 2 * E),
    ("b1", 1), ("b2", 1), ("b3", 1), ("b4", 1), ("range", 1),
    ("g1", E // 2), ("g2", E // 4), ("g3r", E), ("gb1", 1), ("gb2", 1), ("gb3", 1),
    ("q", E), ("k", E), ("qs", E), ("ks", E), ("v", 2 * E), ("gate", 2 * E), ("p0", E), ("p1", E),
    ("bq", 1), ("bk", 1), ("bqs", 1), ("bks", 1), ("bg", 2), ("b_v", 2 * E), ("b_p", E)])
CONST, CONST_N = columns([
    ("ident", P), ("cos_q", SEQ), ("sin_q", SEQ), ("cos_k", SEQ), ("sin_k", SEQ),
    ("heads", 2 * E), ("causal", P), ("mean", P), ("sign", 1)])


class Chain:

    def __init__(self, eng, sem):
        self.eng, self.sem, self.n = eng, sem, 0

    def after(self, ins):
        self.n += 1
        ins.then_inc(self.sem, 1)
        self.eng.wait_ge(self.sem, self.n)


def attention_events():
    n_units = 2 * UNITS
    chunks = [16 if u % 2 == 0 else 8 for u in range(n_units)]
    banks = [32 if u % 2 == 0 else 16 for u in range(n_units)]
    ev = [("xt", p) for p in range(UNITS)]
    ev += [("proj", 0), ("load", 0), ("proj", 1), ("load", 1)]
    ev += [("max", 0, n) for n in range(banks[0])] + [("shift", 0)]
    for u in range(n_units):
        spread = []
        if u + 1 < n_units:
            spread = [("max", u + 1, n) for n in range(banks[u + 1])]
        ev.append(("st", u, 0))
        first = 3 if chunks[u] == 16 else 2
        last = chunks[u] - 1
        for c in range(chunks[u]):
            if c + 1 < chunks[u]:
                ev.append(("st", u, c + 1))
            ev.append(("pv", u, c))
            if c == first - 1 and u > 0:
                ev.append(("norm", u - 1))
            if c == first + 1 and u > 0:
                ev.append(("outproj", u - 1))
            if c == first + 2 and u > 0 and u % 2 == 0:
                ev.append(("fuse", u // 2 - 1))
            if c >= first:
                done = (c - first + 1) * len(spread) // (last - first)
                before = (c - first) * len(spread) // (last - first)
                ev += spread[before:done]
            if c == last - 1:
                if u + 1 < n_units:
                    ev.append(("shift", u + 1))
                if u + 2 < n_units:
                    ev.append(("proj", u + 2))
        ev.append(("evac", u))
        if u + 2 < n_units:
            ev.append(("load", u + 2))
    ev += [("norm", n_units - 1), ("outproj", n_units - 1), ("fuse", UNITS - 1)]
    return ev, chunks, banks


def attention_stage(nc, mem, dram, x_in):
    events, chunks, banks = attention_events()
    n_units = 2 * UNITS
    first_chunk = [sum(chunks[:u]) for u in range(n_units + 1)]

    use = {}
    for e in events:
        if e[0] == "proj":
            for part in ("k", "q", "v"):
                use[("proj", e[1], part)] = len(use)
        elif e[0] in ("xt", "max", "shift", "outproj", "fuse"):
            use[e] = len(use)

    by_use = list(use)

    with ExitStack() as ctx:
        def sb(name, shape, dt=F32):
            return ctx.enter_context(nc.sbuf_tensor(name, shape, dt))

        def ps(name, shape):
            return ctx.enter_context(nc.psum_tensor(name, shape, F32))

        def sem(name):
            return ctx.enter_context(nc.semaphore(name))

        x_res, wa, const = mem["x_res"], mem["w_att"], mem["const"]
        xn = sb("a_xn", [P, TILES, E])
        xt = sb("a_xt", [P, TOK])
        stats = sb("a_stats", [P, TILES, 6])
        mv = sb("a_mv", [P, TILES, 2])
        std = sb("a_std", [P, TILES])
        rstd = sb("a_rstd", [P, TILES])
        eps = sb("a_eps", [P, 1])
        qbd = [sb(f"a_qbd{i}", [P, AG, AJ, UT], F32R) for i in range(2)]
        kst = [sb(f"a_kst{i}", [P, AG, UT], F32R) for i in range(2)]
        vx = [sb(f"a_vx{i}", [P, TPU, AH, 32]) for i in range(3)]
        probs = [sb(f"a_probs{i}", [P, 1024]) for i in range(4)]
        hi = {k: sb(f"a_{k}hi", [P, UT], F32R) for k in "kq"}
        lo = {k: sb(f"a_{k}lo", [P, UT], F32R) for k in "kq"}
        mx = sb("a_mx", [P, TPU * AJ, AG])
        ml = sb("a_ml", [P, TPU * AJ, 2, AG], F32R)
        mrow = sb("a_mrow", [32, UT], F32R)
        o_raw = sb("a_o_raw", [P, 2, UT])
        o_val = sb("a_o_val", [P, UT])
        o_den = sb("a_o_den", [P, UT])
        o_inv = sb("a_o_inv", [P, UT])
        o_nrm = sb("a_o_nrm", [P, UT])
        heads_out = [[sb(f"a_out{i}{k}", [P, UT]) for k in "gl"] for i in range(2)]

        st = [ps(f"a_st{i}", [P, 2, 512]) for i in range(2)]
        work = [ps(f"a_work{i}", [P, 512]) for i in range(2)]
        pv_bank = [ps(f"a_pv{i}", [P, 512]) for i in range(2)]

        x_loaded = [sem(f"x_loaded{p}") for p in range(UNITS)]
        w_loaded, aux_set = sem("w_loaded"), sem("aux_set")
        zeroed = sem("zeroed")
        var_ready = sem("var_ready")
        std_ready = sem("std_ready")
        xn_ready = sem("xn_ready")
        bias_added = sem("bias_added")
        xt_ready = sem("xt_ready")
        work_ready = sem("work_ready")
        max_done = sem("max_done")
        hi_ready, lo_ready = sem("hi_ready"), sem("lo_ready")
        parts_stored = sem("parts_stored")
        qk_loaded = [sem(f"qk_loaded_{k}") for k in "gl"]
        v_ready = sem("v_ready")
        ml_ready = sem("ml_ready")
        mrow_ready = sem("mrow_ready")
        mrow_placed = sem("mrow_placed")
        st_ready = sem("st_ready")
        probs_ready = sem("probs_ready")
        pv_done = sem("pv_done")
        o_evacuated = sem("o_evacuated")
        o_stored, o_loaded = sem("o_stored"), sem("o_loaded")
        o_scaled = sem("o_scaled")
        o_ready = sem("o_ready")
        out_ready = sem("out_ready")
        x_done = sem("x_done")
        dve_chain = sem("a_dve_chain")
        pool_chain = sem("a_pool_chain")

        block = ctx.enter_context(nc.Block())
        col = lambda name: slice(W_ATT[name][0], sum(W_ATT[name]))
        ident = const[:, CONST["ident"][0]:CONST["ident"][0] + P]
        KIND = ["g", "l"]

        def in_bank(eng, key):
            eng.wait_ge(work_ready, use[key] + 1)
            return work[use[key] % 2]

        def read(key):
            kind, u = key[0], key[1]
            return {"xt": lambda: (xt_ready, u + 1), "shift": lambda: (mrow_ready, u + 1),
                    "outproj": lambda: (out_ready, u + 1), "fuse": lambda: (x_done, u + 1),
                    "max": lambda: (max_done, sum(banks[:u]) + key[2] + 1),
                    "proj": lambda: {"k": (lo_ready, 2 * u + 1), "q": (lo_ready, 2 * u + 2),
                                     "v": (v_ready, u + 1)}[key[2]]}[kind]()

        @block.sync
        def _(sp):
            for p in range(UNITS):
                sp.dma_start(x_res[:, TPU * p:TPU * (p + 1), :],
                             x_in.rearrange("(i p) e -> p i e", p=P)[:, TPU * p:TPU * (p + 1), :]
                             ).then_inc(x_loaded[p], 16)
            sp.dma_start(const[:, :], dram["const"]).then_inc(w_loaded, 16)
            sp.dma_start(wa[:, :], dram["w_att"]).then_inc(w_loaded, 16)
            for kind in range(2):
                for which in range(2):
                    dst = dram["parts"][kind][which].rearrange("(h r) t -> h r t", r=32)[:, 24:32, :]
                    src = dram["aux"][kind, which]
                    sp.dma_start(dst, bass.AP(src.tensor, src.offset, [[0, AH], [UT, 8], [1, UT]])
                                 ).then_inc(aux_set, 16)
            sp.dma_start(mem["w_rest"][:, :], dram["w_rest"]).then_inc(mem["rest_loaded"], 16)
            for e in events:
                if e[0] == "proj":
                    u = e[1]
                    if u >= 2:
                        sp.wait_ge(qk_loaded[u % 2], 80 * (u // 2))
                    for n, (k, where) in enumerate([("k", [("hi", 0), ("lo", 1), ("hi", 2)]),
                                                    ("q", [("hi", 0), ("hi", 1), ("lo", 2)])]):
                        sp.wait_ge(hi_ready, 2 * u + n + 1)
                        sp.wait_ge(lo_ready, 2 * u + n + 1)
                        scratch = dram["parts"][u % 2][n].rearrange("(h r) t -> h r t", r=32)
                        for part, r in where:
                            src = (hi if part == "hi" else lo)[k]
                            sp.dma_start(scratch[:, 8 * r:8 * r + 8, :], src[:, :].bitcast(F32)
                                         ).then_inc(parts_stored, 16)
                elif e[0] == "load":
                    u = e[1]
                    sp.wait_ge(parts_stored, 96 * (u + 1))
                    if u < 2:
                        sp.wait_ge(aux_set, 64)
                        sp.wait_ge(zeroed, u + 1)
                    else:
                        sp.wait_ge(st_ready, first_chunk[u - 1])
                    sp.dma_start(kst[u % 2][:, :, :].bitcast(F32),
                                 dram["parts"][u % 2][0].rearrange("(g p) t -> p g t", p=P)
                                 ).then_inc(qk_loaded[u % 2], 16)
                    for j in range(AJ):
                        sp.dma_start(qbd[u % 2][32 * j:32 * j + 32, :, j, :].bitcast(F32),
                                     dram["parts"][u % 2][1].rearrange(
                                         "(g j r) t -> j r g t", g=AG, j=AJ)[j]).then_inc(qk_loaded[u % 2], 16)
                elif e[0] == "shift":
                    u = e[1]
                    sp.wait_ge(mrow_ready, u + 1)
                    for j in range(AJ):
                        sp.dma_start(qbd[u % 2][32 * j + 24:32 * j + 26, :, j, :].bitcast(F32),
                                     mrow[8 * j:8 * j + 8, :].bitcast(F32)).then_inc(mrow_placed, 16)
                elif e[0] == "evac":
                    u = e[1]
                    sp.wait_ge(o_evacuated, u + 1)
                    if u >= 1:
                        sp.wait_ge(o_loaded, 112 * u)
                    sp.dma_start(dram["o"].rearrange("a p t -> p a t"), o_raw[:, :, :]
                                 ).then_inc(o_stored, 16)
                    sp.wait_ge(o_stored, 16 * (u + 1))
                    if u >= 1:
                        sp.wait_ge(o_scaled, u)
                    o = dram["o"].tensor
                    loads = [(o_val[0:96, :], 0, [[32 * UT, AJ], [UT, 24]]),
                             (o_val[96:P, :], P * UT, [[32 * UT, AJ], [UT, 8]]),
                             (o_den[96:P, :], (P + 8) * UT, [[32 * UT, AJ], [0, 8]])]
                    loads += [(o_den[24 * j:24 * j + 24, :], (32 * j + 24) * UT, [[UT, 3], [0, 8]])
                              for j in range(AJ)]
                    for dst, first, rows in loads:
                        sp.dma_start(dst, bass.AP(o, first, rows + [[1, UT]])).then_inc(o_loaded, 16)

        @block.gpsimd
        def _(pool):
            nc.gpsimd.memset(eps[:, :], EPS).then_inc(pool_chain, 1)
            for i in range(2):
                nc.gpsimd.memset(qbd[i][:, :, :, :].bitcast(F32), 0.0).then_inc(zeroed, 1)
            for i in range(3):
                nc.gpsimd.memset(vx[i][:, :, :, :], 0.0).then_inc(pool_chain, 1)
                pool.wait_ge(pool_chain, 2 + i)
                for g in range(AG):
                    one = 24 + g if g < 3 else 8
                    last = nc.gpsimd.memset(vx[i][:, :, 4 * g:4 * g + 4, one], 1.0)
                last.then_inc(zeroed, 1)
            pool.wait_ge(xn_ready, TILES)
            pool.wait_ge(w_loaded, 32)
            for i in range(TILES):
                ins = nc.gpsimd.tensor_tensor(x_res[:, i, :], x_res[:, i, :], wa[:, col("b_f")], ALU.add)
            ins.then_inc(bias_added, 1)
            for e in events:
                if e[0] == "norm":
                    u = e[1]
                    pool.wait_ge(o_scaled, u + 1)
                    at = W_ATT["b_v_" + KIND[u % 2]][0]
                    nc.gpsimd.tensor_scalar(o_nrm[:, :], o_inv[:, :], wa[:, at:at + 1], None, ALU.add
                                            ).then_inc(o_ready, 1)

        @block.vector
        def _(dve):
            chain = Chain(dve, dve_chain)
            for i in range(TILES):
                if i % TPU == 0:
                    dve.wait_ge(x_loaded[i // TPU], 16)
                last = nc.vector.bn_stats(stats[:, i, :], x_res[:, i, :])
            chain.after(last)
            for i in range(TILES):
                last = nc.vector.bn_aggr(mv[:, i, :], stats[:, i, :])
            last.then_inc(var_ready, 1)
            dve.wait_ge(std_ready, 1)
            chain.after(nc.vector.reciprocal(rstd[:, :], std[:, :]))
            for i in range(TILES):
                nc.vector.tensor_scalar(xn[:, i, :], x_res[:, i, :], mv[:, i, 0:1], rstd[:, i:i + 1],
                                        ALU.subtract, ALU.mult).then_inc(xn_ready, 1)
            for e in events:
                if e[0] == "proj":
                    u = e[1]
                    for n, k in enumerate("kq"):
                        bank = in_bank(dve, ("proj", u, k))
                        dve.wait_ge(hi_ready, 2 * u + n + 1)
                        if u >= 1:
                            dve.wait_ge(parts_stored, 96 * u)
                        at = W_ATT["b_in_" + KIND[u % 2]][0] + (1 if k == "k" else 0)
                        ins = nc.vector.scalar_tensor_tensor(
                            out=lo[k][:, :], in0=bank[:, :], scalar=wa[:, at:at + 1],
                            in1=hi[k][:, :].bitcast(F32), op0=ALU.add, op1=ALU.subtract)
                        ins.then_inc(lo_ready, 1)
                elif e[0] == "max":
                    _, u, n = e
                    bank = in_bank(dve, e)
                    if u % 2 == 0:
                        qt, pair = n // 8, n % 8
                        g, j = pair // 2, 2 * (pair % 2)
                        ins = nc.vector.tensor_reduce(mx[:, AJ * qt + j:AJ * qt + j + 2, g],
                                                      bank[:, :].rearrange("p (h k) -> p h k", h=2), AX_X, ALU.max)
                    else:
                        qt, g = n // AG, n % AG
                        ins = nc.vector.tensor_reduce(mx[:, AJ * qt:AJ * qt + AJ, g],
                                                      bank[:, :].rearrange("p (h k) -> p h k", h=4), AX_X, ALU.max)
                    ins.then_inc(max_done, 1)
                elif e[0] == "shift":
                    u = e[1]
                    dve.wait_ge(max_done, sum(banks[:u + 1]))
                    if u >= 1:
                        dve.wait_ge(mrow_ready, u)
                    chain.after(nc.vector.tensor_scalar(ml[:, :, 0, :], mx[:, :, :], -1.0, None, ALU.mult))
                    nc.vector.scalar_tensor_tensor(out=ml[:, :, 1, :], in0=mx[:, :, :], scalar=-1.0,
                                                   in1=ml[:, :, 0, :].bitcast(F32), op0=ALU.mult,
                                                   op1=ALU.subtract).then_inc(ml_ready, 1)
                    dve.wait_ge(ml_ready, u + 1)
                elif e[0] == "norm":
                    u = e[1]
                    dve.wait_ge(o_loaded, 112 * (u + 1))
                    if u >= 1:
                        dve.wait_ge(o_ready, u)
                    chain.after(nc.vector.reciprocal(o_inv[:, :], o_den[:, :]))
                    nc.vector.tensor_tensor(o_inv[:, :], o_val[:, :], o_inv[:, :], ALU.mult).then_inc(o_scaled, 1)
                elif e[0] == "fuse":
                    p = e[1]
                    bank = in_bank(dve, e)
                    dve.wait_ge(bias_added, 1)
                    xs = x_res[:, TPU * p:TPU * (p + 1), :].rearrange("p i e -> p (i e)")
                    ins = nc.vector.tensor_tensor(xs, bank[:, :], xs, ALU.add)
                    ins.then_inc(x_done, 1)

        @block.scalar
        def _(act):
            act.wait_ge(var_ready, 1)
            act.wait_ge(pool_chain, 1)
            nc.scalar.activation(std[:, :], mv[:, :, 1], ACT.Sqrt, bias=eps[:, 0:1]).then_inc(std_ready, 1)
            for e in events:
                if e[0] == "xt":
                    bank = in_bank(act, e)
                    ins = nc.scalar.copy(xt[:, UT * e[1]:UT * (e[1] + 1)], bank[:, :])
                    ins.then_inc(xt_ready, 1)
                elif e[0] == "proj":
                    u = e[1]
                    for n, k in enumerate("kq"):
                        bank = in_bank(act, ("proj", u, k))
                        if u == 0:
                            act.wait_ge(w_loaded, 32)
                        else:
                            act.wait_ge(parts_stored, 96 * u)
                            act.wait_ge(lo_ready, 2 * u)
                        at = W_ATT["b_in_" + KIND[u % 2]][0] + (1 if k == "k" else 0)
                        nc.scalar.activation(hi[k][:, :], bank[:, :], ACT.Identity, bias=wa[:, at:at + 1]
                                             ).then_inc(hi_ready, 1)
                    bank = in_bank(act, ("proj", u, "v"))
                    act.wait_ge(zeroed, 5)
                    if u >= 3:
                        act.wait_ge(pv_done, first_chunk[u - 2])
                    for g in range(AG):
                        off = 8 * g if g < 3 else 0
                        for t in range(TPU):
                            ins = nc.scalar.copy(
                                vx[u % 3][:, t, 4 * g:4 * g + 4, off:off + 8],
                                bank[:, P * t + 32 * g:P * t + 32 * g + 32].rearrange("p (j d) -> p j d", j=AJ))
                    ins.then_inc(v_ready, 1)
                elif e[0] == "shift":
                    u = e[1]
                    bank = in_bank(act, e)
                    if u >= 1:
                        act.wait_ge(mrow_placed, 64 * u)
                    ins = nc.scalar.copy(mrow[:, :], bank[0:32, :])
                    ins.then_inc(mrow_ready, 1)
                elif e[0] == "pv":
                    _, u, c = e
                    n = first_chunk[u] + c
                    act.wait_ge(st_ready, n + 1)
                    if n >= 4:
                        act.wait_ge(pv_done, n - 3)
                    nc.scalar.activation(probs[n % 4][:, :], st[n % 2][:, :, :].rearrange("p a b -> p (a b)"),
                                         ACT.Exp, scale=A_SCALE).then_inc(probs_ready, 1)
                elif e[0] == "evac":
                    u = e[1]
                    act.wait_ge(pv_done, first_chunk[u + 1])
                    if u >= 1:
                        act.wait_ge(o_stored, 16 * u)
                    nc.scalar.copy(o_raw[:, 0, :], pv_bank[0][:, :])
                    nc.scalar.copy(o_raw[:, 1, :], pv_bank[1][:, :]).then_inc(o_evacuated, 1)
                elif e[0] == "outproj":
                    u = e[1]
                    bank = in_bank(act, e)
                    p = u // 2
                    if p >= 2:
                        act.wait_ge(x_done, p - 1)
                    at = W_ATT["b_out_" + KIND[u % 2]][0]
                    ins = nc.scalar.activation(heads_out[p % 2][u % 2][:, :], bank[:, :], ACT.Identity,
                                               bias=wa[:, at:at + 1])
                    ins.then_inc(out_ready, 1)

        @block.tensor
        def _(pe):
            def fill(key):
                n = use[key]
                if n >= 2:
                    pe.wait_ge(*read(by_use[n - 2]))
                return work[n % 2]

            def scores(u, c):
                n = first_chunk[u] + c
                if c == 0:
                    pe.wait_ge(mrow_placed, 64 * (u + 1))
                if n >= 2:
                    pe.wait_ge(probs_ready, n - 1)
                q, k = qbd[u % 2], kst[u % 2]
                for half in range(2):
                    if u % 2 == 0:
                        b, kt, g = c // 8, c // 4 % 2, c % 4
                        keys = k[:, g, SEQ * b + P * kt:SEQ * b + P * kt + P]
                        queries = q[:, g, 2 * half:2 * half + 2, SEQ * b:SEQ * (b + 1)]
                        out = st[n % 2][:, half, :].rearrange("p (j q) -> p j q", j=2)
                    else:
                        t, g = c // 2, 2 * (c % 2) + half
                        keys = k[:, g, P * t:P * (t + 1)]
                        queries = q[:, g, :, P * t:P * (t + 1)]
                        out = st[n % 2][:, half, :].rearrange("p (j q) -> p j q", j=4)
                    ins = pe.matmul(out, keys, queries, start=True, stop=True)
                ins.then_inc(st_ready, 1)

            def outputs(u, c):
                n = first_chunk[u] + c
                pe.wait_ge(probs_ready, n + 1)
                if c == 0:
                    pe.wait_ge(v_ready, u + 1)
                    if u >= 1:
                        pe.wait_ge(o_evacuated, u)
                pr, v = probs[n % 4], vx[u % 3]
                if u % 2 == 0:
                    b, kt, g = c // 8, c // 4 % 2, c % 4
                    bank, cols = pv_bank[g // 3], slice(SEQ * b, SEQ * (b + 1))
                    for j in range(AJ):
                        ins = pe.matmul(bank[32 * j:32 * j + 32, cols], v[:, 2 * b + kt, 4 * g + j, :],
                                        pr[:, SEQ * j:SEQ * (j + 1)],
                                        start=(kt == 0 and g in (0, 3)), stop=(kt == 1 and g in (2, 3)))
                else:
                    t = c // 2
                    for half in range(2):
                        g = 2 * (c % 2) + half
                        for j in range(AJ):
                            at = 512 * half + P * j
                            ins = pe.matmul(pv_bank[g // 3][32 * j:32 * j + 32, P * t:P * (t + 1)],
                                            v[:, t, 4 * g + j, :], pr[:, at:at + P],
                                            start=(g in (0, 3)), stop=(g in (2, 3)))
                ins.then_inc(pv_done, 1)

            pe.wait_ge(w_loaded, 32)
            for e in events:
                if e[0] == "xt":
                    bank = fill(e)
                    pe.wait_ge(xn_ready, TPU * (e[1] + 1))
                    for t in range(TPU):
                        ins = pe.transpose(bank[:, P * t:P * (t + 1)], xn[:, TPU * e[1] + t, :], ident)
                    ins.then_inc(work_ready, 1)
                elif e[0] == "proj":
                    u = e[1]
                    at = W_ATT["in_" + KIND[u % 2]][0]
                    pe.wait_ge(xt_ready, u // 2 + 1)
                    cols = slice(UT * (u // 2), UT * (u // 2 + 1))
                    for k, off in (("k", E), ("q", 0)):
                        bank = fill(("proj", u, k))
                        pe.matmul(bank[:, :], wa[:, at + off:at + off + E], xt[:, cols], start=True, stop=True
                                  ).then_inc(work_ready, 1)
                    bank = fill(("proj", u, "v"))
                    for t in range(TPU):
                        ins = pe.matmul(bank[:, P * t:P * (t + 1)], xt[:, cols.start + P * t:cols.start + P * (t + 1)],
                                        wa[:, at + 2 * E:at + 3 * E], start=True, stop=True)
                    ins.then_inc(work_ready, 1)
                elif e[0] == "max":
                    _, u, n = e
                    bank = fill(e)
                    if n == 0:
                        pe.wait_ge(qk_loaded[u % 2], 80 * (u // 2 + 1))
                    q, k = qbd[u % 2], kst[u % 2]
                    if u % 2 == 0:
                        qt, pair = n // 8, n % 8
                        g, j, b = pair // 2, 2 * (pair % 2), qt // 2
                        for i in range(2):
                            ins = pe.matmul(bank[:, SEQ * i:SEQ * (i + 1)], q[:, g, j + i, P * qt:P * (qt + 1)],
                                            k[:, g, SEQ * b:SEQ * (b + 1)], start=True, stop=True)
                    else:
                        qt, g = n // AG, n % AG
                        for j in range(AJ):
                            ins = pe.matmul(bank[:, P * j:P * (j + 1)], q[:, g, j, P * qt:P * (qt + 1)],
                                            k[:, g, P * qt:P * (qt + 1)], start=True, stop=True)
                    ins.then_inc(work_ready, 1)
                elif e[0] == "shift":
                    u = e[1]
                    bank = fill(e)
                    pe.wait_ge(ml_ready, u + 1)
                    for t in range(TPU):
                        src = ml[:, AJ * t:AJ * (t + 1), :, :].rearrange("p j r g -> p (j r g)").bitcast(F32)
                        ins = pe.transpose(bank[0:32, P * t:P * (t + 1)], src, ident)
                    ins.then_inc(work_ready, 1)
                elif e[0] == "st":
                    scores(e[1], e[2])
                elif e[0] == "pv":
                    outputs(e[1], e[2])
                elif e[0] == "outproj":
                    u = e[1]
                    bank = fill(e)
                    pe.wait_ge(o_ready, u + 1)
                    pe.matmul(bank[:, :], wa[:, col("out_" + KIND[u % 2])], o_nrm[:, :], start=True, stop=True
                              ).then_inc(work_ready, 1)
                elif e[0] == "fuse":
                    p = e[1]
                    bank = fill(e)
                    pe.wait_ge(out_ready, 2 * p + 2)
                    for t in range(TPU):
                        for i, name in enumerate(("f_g", "f_l")):
                            ins = pe.matmul(bank[:, P * t:P * (t + 1)], heads_out[p % 2][i][:, P * t:P * (t + 1)],
                                            wa[:, col(name)], start=(i == 0), stop=(i == 1))
                    ins.then_inc(work_ready, 1)


class LayerNorm:

    def __init__(self, nc, ctx, mem, tag, banks):
        def sb(name, shape):
            return ctx.enter_context(nc.sbuf_tensor(f"{tag}_{name}", shape, F32))

        def sem(name):
            return ctx.enter_context(nc.semaphore(f"{tag}_{name}"))

        self.nc, self.x_res, self.banks = nc, mem["x_res"], banks
        self.ident = mem["const"][:, CONST["ident"][0]:CONST["ident"][0] + P]
        self.xn, self.xt = sb("xn", [P, TILES, E]), sb("xt", [P, TOK])
        self.stats, self.mv = sb("stats", [P, TILES, 6]), sb("mv", [P, TILES, 2])
        self.std, self.rstd, self.eps = sb("std", [P, TILES]), sb("rstd", [P, TILES]), sb("eps", [P, 1])
        self.eps_set = sem("eps_set")
        self.var_ready = sem("var_ready")
        self.std_ready = sem("std_ready")
        self.xn_ready = sem("xn_ready")
        self.turned = sem("turned")
        self.xt_ready = sem("xt_ready")

    def on_pool(self):
        self.nc.gpsimd.memset(self.eps[:, :], EPS).then_inc(self.eps_set, 1)

    def on_vector(self, dve, chain):
        nc = self.nc
        for i in range(TILES):
            last = nc.vector.bn_stats(self.stats[:, i, :], self.x_res[:, i, :])
        chain.after(last)
        for i in range(TILES):
            last = nc.vector.bn_aggr(self.mv[:, i, :], self.stats[:, i, :])
        last.then_inc(self.var_ready, 1)
        dve.wait_ge(self.std_ready, 1)
        chain.after(nc.vector.reciprocal(self.rstd[:, :], self.std[:, :]))
        for i in range(TILES):
            nc.vector.tensor_scalar(self.xn[:, i, :], self.x_res[:, i, :], self.mv[:, i, 0:1],
                                    self.rstd[:, i:i + 1], ALU.subtract, ALU.mult).then_inc(self.xn_ready, 1)

    def on_scalar(self, act):
        act.wait_ge(self.var_ready, 1)
        act.wait_ge(self.eps_set, 1)
        self.nc.scalar.activation(self.std[:, :], self.mv[:, :, 1], ACT.Sqrt, bias=self.eps[:, 0:1]
                                  ).then_inc(self.std_ready, 1)

    def turn(self, pe, u):
        pe.wait_ge(self.xn_ready, TPU * (u + 1))
        for t in range(TPU):
            ins = pe.transpose(self.banks[u][:, P * t:P * (t + 1)], self.xn[:, TPU * u + t, :], self.ident)
        ins.then_inc(self.turned, 1)

    def copy(self, act, u):
        act.wait_ge(self.turned, u + 1)
        self.nc.scalar.copy(self.xt[:, UT * u:UT * (u + 1)], self.banks[u][:, :]).then_inc(self.xt_ready, 1)


def coupled_stage(nc, mem, tag, out):
    CYCLES, PAIRS = 3, UNITS // 2
    with ExitStack() as ctx:
        def sb(name, shape):
            return ctx.enter_context(nc.sbuf_tensor(f"{tag}_{name}", shape, F32))

        def ps(name, shape):
            return ctx.enter_context(nc.psum_tensor(f"{tag}_{name}", shape, F32))

        def sem(name):
            return ctx.enter_context(nc.semaphore(f"{tag}_{name}"))

        x_res, w, const = mem["x_res"], mem["w_rest"], mem["const"]
        wcol = lambda name: w[:, W_REST[name][0]:sum(W_REST[name])]
        each = lambda name, shape=(P, UT): [sb(f"{name}{t}", list(shape)) for t in range(UNITS)]
        a_sb, b_sb, h_sb, g_sb, t_sb = each("a"), each("b"), each("h"), each("g"), each("t")
        g1 = each("g1")
        g2 = [sb(f"g2{i}", [P, UT]) for i in range(PAIRS)]
        g3 = [sb(f"g3{i}", [64, UT]) for i in range(PAIRS)]
        cc = [each(f"c{n}_") for n in range(CYCLES)]
        txn = sb("txn", [P, TILES, E])
        c1s = sb("c1s", [P, E])
        ctx_sum, gh1, gh2 = sb("ctx", [P, BATCH]), sb("gh1", [64, BATCH]), sb("gh2", [32, BATCH])
        tg, k0 = sb("tg", [P, BATCH]), sb("k0", [P, BATCH])
        k1, k7, hb4, hg3 = sb("k1", [P, 1]), sb("k7", [P, 1]), sb("hb4", [P, 1]), sb("hg3", [P, 1])
        ct = [sb(f"ct{i}", [P, CYCLES, 2 * TPU]) for i in range(PAIRS)]
        ab = [sb(f"ab{i}", [P, 6, 2 * TPU]) for i in range(PAIRS)]
        pa = [ps(f"pa{t}", [P, UT]) for t in range(UNITS)]
        p2 = [ps(f"p2{i}", [P, UT]) for i in range(PAIRS)]
        p3 = [ps(f"p3{i}", [P, UT]) for i in range(PAIRS)]
        pb = [p2[0], p3[0], p2[1], p3[1]]
        ln = LayerNorm(nc, ctx, mem, tag, pa)

        small_ready = sem("small_ready")
        ctx_ready = sem("ctx_ready")
        glob_mm = sem("glob_mm")
        glob_act = sem("glob_act")
        k0_ready = sem("k0_ready")
        a_mm, b_mm = sem("a_mm"), sem("b_mm")
        a_ready, b_ready = sem("a_ready"), sem("b_ready")
        g1_ready = sem("g1_ready")
        l2_mm, l3_mm = sem("l2_mm"), sem("l3_mm")
        g2_ready, g3_ready = sem("g2_ready"), sem("g3_ready")
        z_mm = sem("z_mm")
        t_ready = sem("t_ready")
        c_ready = sem("c_ready")
        h_ready = sem("h_ready")
        g_ready = sem("g_ready")
        txn_ready = sem("txn_ready")
        ct_mm, ct_ready = sem("ct_mm"), sem("ct_ready")
        x_done = sem("x_done")
        stored = sem("stored")
        dve_chain, pool_chain = sem("dve_chain"), sem("pool_chain")
        block = ctx.enter_context(nc.Block())

        if out is not None:
            @block.sync
            def _(sp):
                for i in range(PAIRS):
                    sp.wait_ge(x_done, i + 1)
                    tiles = slice(2 * TPU * i, 2 * TPU * (i + 1))
                    sp.dma_start(out.rearrange("(i p) e -> p i e", p=P)[:, tiles, :], x_res[:, tiles, :]
                                 ).then_inc(stored, 16)
                sp.wait_ge(stored, 16 * PAIRS)

        @block.gpsimd
        def _(pool):
            ln.on_pool()
            chain = Chain(pool, pool_chain)
            pool.wait_ge(mem["rest_loaded"], 16)
            for t in range(UNITS):
                pool.wait_ge(c_ready, t + 1)
                pool.wait_ge(a_ready, t + 1)
                pool.wait_ge(b_ready, t + 1)
                chain.after(nc.gpsimd.tensor_tensor(g_sb[t][:, :], cc[0][t][:, :], a_sb[t][:, :], ALU.mult))
                nc.gpsimd.tensor_tensor(g_sb[t][:, :], b_sb[t][:, :], g_sb[t][:, :], ALU.subtract
                                        ).then_inc(g_ready, 1)
            for block_out, (block_in, sign) in enumerate([(2, 1.0), (3, -1.0), (0, -1.0), (1, 1.0)]):
                ins = nc.gpsimd.tensor_scalar(txn[:, :, 32 * block_out:32 * block_out + 32],
                                              ln.xn[:, :, 32 * block_in:32 * block_in + 32],
                                              sign, None, ALU.mult)
                ins.then_inc(txn_ready, 1)

        @block.vector
        def _(dve):
            chain = Chain(dve, dve_chain)
            dve.wait_ge(mem["rest_loaded"], 16)
            for dst, src, by in ((k1, "range", 0.3), (k7, "range", 0.7), (hb4, "b4", 0.5), (hg3, "gb3", 0.5)):
                nc.vector.tensor_scalar(dst[:, :], wcol(src), by, None, ALU.mult)
            nc.vector.tensor_scalar(c1s[:, :], wcol("c1p"), const[:, CONST["sign"][0]:CONST["sign"][0] + 1],
                                    None, ALU.mult).then_inc(small_ready, 1)
            ln.on_vector(dve, chain)
            for t in range(UNITS):
                dve.wait_ge(ln.xt_ready, t + 1)
                ins = nc.vector.tensor_reduce(ctx_sum[:, 2 * t:2 * t + 2],
                                              ln.xt[:, UT * t:UT * (t + 1)].rearrange("p (b t) -> p b t", b=2),
                                              AX_X, ALU.add)
            ins.then_inc(ctx_ready, 1)
            for t in range(UNITS):
                dve.wait_ge(g1_ready, t + 1)
                nc.vector.tensor_copy(a_sb[t][:, :], pa[t][:, :]).then_inc(a_ready, 1)
            dve.wait_ge(glob_act, 3)
            nc.vector.tensor_scalar(k0[:, :], tg[:, :], k7[:, 0:1], 0.1, ALU.mult, ALU.add).then_inc(k0_ready, 1)
            dve.wait_ge(k0_ready, 1)
            for n in range(CYCLES):
                for t in range(UNITS):
                    dve.wait_ge(t_ready, UNITS * n + t + 1)
                    for b in range(2):
                        cols = slice(SEQ * b, SEQ * (b + 1))
                        ins = nc.vector.tensor_scalar(cc[n][t][:, cols], t_sb[t][:, cols], k1[:, 0:1],
                                                      k0[:, 2 * t + b:2 * t + b + 1], ALU.mult, ALU.add)
                    ins.then_inc(c_ready, 1)
                    if n < CYCLES - 1:
                        dve.wait_ge(c_ready, UNITS * n + t + 1)
                        if n == 0:
                            dve.wait_ge(b_ready, t + 1)
                            dve.wait_ge(a_ready, t + 1)
                        else:
                            dve.wait_ge(g_ready, t + 1)
                        step, base = (b_sb, a_sb) if n == 0 else (g_sb, h_sb)
                        chain.after(nc.vector.tensor_tensor(t_sb[t][:, :], cc[n][t][:, :], step[t][:, :], ALU.mult))
                        nc.vector.tensor_tensor(h_sb[t][:, :], t_sb[t][:, :], base[t][:, :], ALU.add
                                                ).then_inc(h_ready, 1)
            dve.wait_ge(txn_ready, 4)
            for i in range(PAIRS):
                c, s = ct[i], ab[i]
                dve.wait_ge(ct_mm, i + 1)
                nc.vector.tensor_copy(c[:, :, :].rearrange("p n t -> p (n t)"),
                                      p2[i][:, 0:CYCLES * 2 * TPU]).then_inc(ct_ready, 1)
                dve.wait_ge(ct_ready, i + 1)
                TT, TS = nc.vector.tensor_tensor, nc.vector.tensor_scalar
                TT(s[:, 0, :], c[:, 0, :], c[:, 1, :], ALU.mult)
                chain.after(TT(s[:, 1, :], c[:, 0, :], c[:, 1, :], ALU.add))
                chain.after(TS(s[:, 2, :], s[:, 0, :], -1.0, 1.0, ALU.mult, ALU.add))
                TT(s[:, 3, :], c[:, 2, :], s[:, 1, :], ALU.mult)
                chain.after(TT(s[:, 0, :], c[:, 2, :], s[:, 2, :], ALU.mult))
                TT(s[:, 4, :], s[:, 2, :], s[:, 3, :], ALU.subtract)
                chain.after(TT(s[:, 5, :], s[:, 1, :], s[:, 0, :], ALU.add))
                for src, k in ((ln.xn, 4), (txn, 5)):
                    for t in range(2 * TPU):
                        n = 2 * TPU * i + t
                        ins = nc.vector.scalar_tensor_tensor(
                            out=x_res[:, n, :], in0=src[:, n, :], scalar=s[:, k, t:t + 1], in1=x_res[:, n, :],
                            op0=ALU.mult, op1=ALU.add)
                    if k == 4:
                        chain.after(ins)
                ins.then_inc(x_done, 1)

        @block.scalar
        def _(act):
            ln.on_scalar(act)
            act.wait_ge(mem["rest_loaded"], 16)
            act.wait_ge(small_ready, 1)
            for t in range(UNITS):
                ln.copy(act, t)
            gelu = lambda dst, src, bias, scale=1.0: nc.scalar.activation(dst, src, ACT.Gelu, bias=bias, scale=scale)
            for t in range(UNITS):
                act.wait_ge(a_mm, t + 1)
                gelu(g1[t][:, :], pa[t][:, :], wcol("b1")).then_inc(g1_ready, 1)
                act.wait_ge(b_mm, t + 1)
                nc.scalar.copy(b_sb[t][:, :], pb[t][:, :]).then_inc(b_ready, 1)
            for n in range(CYCLES):
                if n > 0:
                    for t in range(UNITS):
                        act.wait_ge(h_ready, UNITS * (n - 1) + t + 1)
                        gelu(g1[t][:, :], h_sb[t][:, :], wcol("b1")).then_inc(g1_ready, 1)
                for i in range(PAIRS):
                    act.wait_ge(l2_mm, PAIRS * n + i + 1)
                    gelu(g2[i][:, :], p2[i][:, :], wcol("b2")).then_inc(g2_ready, 1)
                for i in range(PAIRS):
                    act.wait_ge(l3_mm, PAIRS * n + i + 1)
                    gelu(g3[i][:, :], p3[i][0:64, :], wcol("b3")[0:64]).then_inc(g3_ready, 1)
                if n == 0:
                    act.wait_ge(glob_mm, 1)
                    gelu(gh1[:, :], p3[0][0:64, 0:BATCH], wcol("gb1")[0:64], 1.0 / SEQ).then_inc(glob_act, 1)
                    act.wait_ge(glob_mm, 2)
                    gelu(gh2[:, :], p3[0][0:32, BATCH:2 * BATCH], wcol("gb2")[0:32]).then_inc(glob_act, 1)
                    act.wait_ge(glob_mm, 3)
                    nc.scalar.activation(tg[:, :], p3[0][:, 2 * BATCH:3 * BATCH], ACT.Tanh, bias=hg3[:, 0:1],
                                         scale=0.5).then_inc(glob_act, 1)
                for t in range(UNITS):
                    act.wait_ge(z_mm, UNITS * n + t + 1)
                    if n > 0:
                        act.wait_ge(h_ready, UNITS * (n - 1) + t + 1)
                    nc.scalar.activation(t_sb[t][:, :], pa[t][:, :], ACT.Tanh, bias=hb4[:, 0:1], scale=0.5
                                         ).then_inc(t_ready, 1)

        @block.tensor
        def _(pe):
            for t in range(UNITS):
                ln.turn(pe, t)
            pe.wait_ge(mem["rest_loaded"], 16)
            pe.wait_ge(small_ready, 1)
            for t in range(UNITS):
                cols = slice(UT * t, UT * (t + 1))
                pe.wait_ge(ln.xt_ready, t + 1)
                pe.matmul(pa[t][:, :], wcol("c1"), ln.xt[:, cols], start=True, stop=True).then_inc(a_mm, 1)
                pe.matmul(pb[t][:, :], c1s[:, :], ln.xt[:, cols], start=True, stop=True).then_inc(b_mm, 1)
            for n in range(CYCLES):
                for i in range(PAIRS):
                    pe.wait_ge(g1_ready, UNITS * n + 2 * i + 2)
                    pe.wait_ge(b_ready, 2 * i + 2)
                    if n > 0:
                        pe.wait_ge(g2_ready, PAIRS * (n - 1) + i + 1)
                    for e in range(2):
                        ins = pe.matmul(p2[i][64 * e:64 * e + 64, :], wcol("c2"), g1[2 * i + e][:, :],
                                        start=True, stop=True)
                    ins.then_inc(l2_mm, 1)
                for i in range(PAIRS):
                    pe.wait_ge(g2_ready, PAIRS * n + i + 1)
                    pe.matmul(p3[i][0:64, :], wcol("c3"), g2[i][:, :], start=True, stop=True).then_inc(l3_mm, 1)
                if n == 0:
                    pe.wait_ge(ctx_ready, 1)
                    pe.wait_ge(g3_ready, 2)
                    pe.matmul(p3[0][0:64, 0:BATCH], wcol("g1"), ctx_sum[:, :], start=True, stop=True).then_inc(glob_mm, 1)
                    pe.wait_ge(glob_act, 1)
                    pe.matmul(p3[0][0:32, BATCH:2 * BATCH], wcol("g2")[0:64], gh1[:, :], start=True, stop=True
                              ).then_inc(glob_mm, 1)
                    pe.wait_ge(glob_act, 2)
                    pe.matmul(p3[0][:, 2 * BATCH:3 * BATCH], wcol("g3r")[0:32], gh2[:, :], start=True, stop=True
                              ).then_inc(glob_mm, 1)
                for t in range(UNITS):
                    pe.wait_ge(g3_ready, PAIRS * n + t // 2 + 1)
                    pe.wait_ge(a_ready, t + 1)
                    pe.matmul(pa[t][:, :], wcol("c4r")[0:64, P * (t % 2):P * (t % 2 + 1)], g3[t // 2][:, :],
                              start=True, stop=True).then_inc(z_mm, 1)
            for i in range(PAIRS):
                pe.wait_ge(c_ready, UNITS * (CYCLES - 1) + 2 * i + 2)
                for n in range(CYCLES):
                    for t in range(2 * TPU):
                        col = 2 * TPU * n + t
                        src = cc[n][2 * i + t // TPU][0:1, P * (t % TPU):P * (t % TPU + 1)]
                        ins = pe.transpose(p2[i][:, col:col + 1], src, ln.ident[0:1, 0:1])
                ins.then_inc(ct_mm, 1)


def retention_stage(nc, mem):
    HG = 2
    with ExitStack() as ctx:
        def sb(name, shape):
            return ctx.enter_context(nc.sbuf_tensor(f"r_{name}", shape, F32))

        def ps(name, shape):
            return ctx.enter_context(nc.psum_tensor(f"r_{name}", shape, F32))

        def sem(name):
            return ctx.enter_context(nc.semaphore(f"r_{name}"))

        x_res, w, const = mem["x_res"], mem["w_rest"], mem["const"]
        wcol = lambda name: w[:, W_REST[name][0]:sum(W_REST[name])]
        ccol = lambda name: const[:, CONST[name][0]:sum(CONST[name])]

        def again(ap, n):
            return bass.AP(ap.tensor, ap.offset, [list(ap.ap[0]), [0, n], list(ap.ap[1])])

        rot = {k: sb(f"{k}r", [P, TOK]) for k in "qk"}
        turned = [[sb(f"{k}{i}", [P, UT]) for i in range(2)] for k in "qk"]
        qbd = [sb(f"qbd{i}", [P, RH, UT]) for i in range(2)]
        val = sb("val", [P, TILES, 2 * E])
        gate = sb("gate", [P, HG, TOK])
        ktok = [sb(f"ktok{i}", [P, 2, P]) for i in range(2)]
        kv = [sb(f"kv{i}", [P, 2, 2 * E]) for i in range(2)]
        masked = [sb(f"masked{i}", [P, 4, P]) for i in range(4)]
        o_sb = [sb(f"o{i}", [P, UT]) for i in range(HG)]
        cen = [sb(f"cen{i}", [P, UT]) for i in range(HG)]
        sq = [sb(f"sq{i}", [P, UT]) for i in range(HG)]
        std = [sb(f"sd{i}", [P, UT]) for i in range(HG)]
        gated = [sb(f"gated{i}", [P, UT]) for i in range(HG)]

        work = [ps(f"work{i}", [P, 512]) for i in range(4)]
        s_bank = [ps(f"s{i}", [P, 512]) for i in range(2)]
        o_bank = [ps(f"ob{i}", [P, 512]) for i in range(HG)]
        ln = LayerNorm(nc, ctx, mem, "r", work)

        keys = []
        for u in range(UNITS):
            keys += [(k, u) for k in ("q", "qs", "k", "ks")]
            keys += [("v", u, 0), ("v", u, 1), ("g", u, 0), ("g", u, 1)]
        for u in range(UNITS):
            keys += [("kt", u), ("u", u)]
            keys += [(k, u, hg) for k in ("mean", "var") for hg in range(HG)] + [("proj", u)]
        use = {k: n + UNITS for n, k in enumerate(keys)}

        zeroed = sem("zeroed")
        work_mm = sem("work_mm")
        part_ready = sem("part_ready")
        rot_ready = sem("rot_ready")
        val_ready = sem("val_ready")
        gate_ready = sem("gate_ready")
        qbd_loaded = [sem(f"qbd_loaded{i}") for i in range(2)]
        ktok_ready = sem("ktok_ready")
        kv_ready = sem("kv_ready")
        s_mm = sem("s_mm")
        masked_ready = sem("masked_ready")
        o_mm = sem("o_mm")
        o_ready = sem("o_ready")
        cen_ready = sem("cen_ready")
        sq_ready = sem("sq_ready")
        std_ready = sem("sd_ready")
        norm_ready = sem("norm_ready")
        gated_ready = sem("gated_ready")
        bias_added = sem("bias_added")
        x_done = sem("x_done")
        dve_chain = sem("dve_chain")
        block = ctx.enter_context(nc.Block())

        def in_bank(eng, key):
            eng.wait_ge(work_mm, use[key] - UNITS + 1)
            return work[use[key] % 4]

        def read(n):
            if n < UNITS:
                return ln.xt_ready, n + 1
            key = keys[n - UNITS]
            kind, u = key[0], key[1]
            if kind in ("q", "qs", "k", "ks"):
                return part_ready, 4 * u + ("q", "qs", "k", "ks").index(kind) + 1
            return {"v": lambda: (val_ready, 2 * u + key[2] + 1), "g": lambda: (gate_ready, 2 * u + key[2] + 1),
                    "kt": lambda: (ktok_ready, u + 1), "u": lambda: (kv_ready, u + 1),
                    "mean": lambda: (cen_ready, HG * u + key[2] + 1),
                    "var": lambda: (std_ready, HG * u + key[2] + 1), "proj": lambda: (x_done, u + 1)}[kind]()

        ITEMS = [(t, hg) for t in range(TPU) for hg in range(HG)]

        @block.sync
        def _(sp):
            for u in range(UNITS):
                sp.wait_ge(rot_ready, 2 * u + 1)
                if u < 2:
                    sp.wait_ge(zeroed, u + 1)
                else:
                    sp.wait_ge(s_mm, 8 * (u - 1))
                for h in range(RH):
                    sp.dma_start(qbd[u % 2][RK * h:RK * (h + 1), h, :],
                                 rot["q"][RK * h:RK * (h + 1), UT * u:UT * (u + 1)]).then_inc(qbd_loaded[u % 2], 16)

        @block.gpsimd
        def _(pool):
            ln.on_pool()
            for i in range(2):
                nc.gpsimd.memset(qbd[i][:, :, :], 0.0).then_inc(zeroed, 1)
            for u in range(UNITS):
                for n, k in enumerate("qk"):
                    pool.wait_ge(part_ready, 4 * u + 2 * n + 2)
                    nc.gpsimd.tensor_tensor(rot[k][:, UT * u:UT * (u + 1)], turned[n][0][:, :], turned[n][1][:, :],
                                            ALU.add).then_inc(rot_ready, 1)
            pool.wait_ge(ln.xn_ready, TILES)
            for i in range(TILES):
                ins = nc.gpsimd.tensor_tensor(x_res[:, i, :], x_res[:, i, :], wcol("b_p"), ALU.add)
            ins.then_inc(bias_added, 1)
            for u in range(UNITS):
                for hg in range(HG):
                    n = HG * u + hg + 1
                    pool.wait_ge(cen_ready, n)
                    nc.gpsimd.tensor_tensor(sq[hg][:, :], cen[hg][:, :], cen[hg][:, :], ALU.mult).then_inc(sq_ready, 1)
                for hg in range(HG):
                    n = HG * u + hg + 1
                    pool.wait_ge(norm_ready, n)
                    pool.wait_ge(gate_ready, n)
                    if u > 0:
                        pool.wait_ge(x_done, u)
                    nc.gpsimd.tensor_tensor(gated[hg][:, :], std[hg][:, :], gate[:, hg, UT * u:UT * (u + 1)],
                                            ALU.mult).then_inc(gated_ready, 1)

        @block.vector
        def _(dve):
            chain = Chain(dve, dve_chain)
            ln.on_vector(dve, chain)
            for u in range(UNITS):
                for n, k in enumerate("qk"):
                    if u > 0:
                        dve.wait_ge(rot_ready, 2 * (u - 1) + n + 1)
                    for i, (key, table) in enumerate([(k, "cos_" + k), (k + "s", "sin_" + k)]):
                        bank = in_bank(dve, (key, u))
                        nc.vector.scalar_tensor_tensor(
                            out=turned[n][i][:, :].rearrange("p (b t) -> p b t", b=2),
                            in0=bank[:, :].rearrange("p (b t) -> p b t", b=2), scalar=wcol("b" + key),
                            in1=again(ccol(table), 2), op0=ALU.add, op1=ALU.mult).then_inc(part_ready, 1)
                for half in range(2):
                    bank = in_bank(dve, ("v", u, half))
                    i = TPU * u + 2 * half
                    nc.vector.tensor_tensor(val[:, i:i + 2, :], bank[:, :].rearrange("p (t v) -> p t v", t=2),
                                            again(wcol("b_v"), 2), ALU.add).then_inc(val_ready, 1)
            for u in range(UNITS):
                bank = in_bank(dve, ("u", u))
                if u >= 2:
                    dve.wait_ge(o_mm, 8 * (u - 1))
                nc.vector.tensor_tensor(kv[u % 2][:, :, :], bank[:, :].rearrange("p (t v) -> p t v", t=2),
                                        again(ccol("heads"), 2), ALU.mult).then_inc(kv_ready, 1)
                for i in range(8):
                    n = 8 * u + i
                    dve.wait_ge(s_mm, n + 1)
                    if n >= 4:
                        dve.wait_ge(o_mm, n - 3)
                    nc.vector.tensor_tensor(masked[n % 4][:, :, :], s_bank[n % 2][:, :].rearrange("p (h i) -> p h i", h=4),
                                            again(ccol("causal"), 4), ALU.mult).then_inc(masked_ready, 1)
                for hg in range(HG):
                    n = HG * u + hg + 1
                    bank = in_bank(dve, ("mean", u, hg))
                    if u > 0:
                        dve.wait_ge(norm_ready, n - HG)
                    nc.vector.tensor_tensor(cen[hg][:, :], o_sb[hg][:, :], bank[:, :], ALU.subtract).then_inc(cen_ready, 1)
                for hg in range(HG):
                    n = HG * u + hg + 1
                    dve.wait_ge(std_ready, n)
                    dve.wait_ge(cen_ready, n)
                    chain.after(nc.vector.reciprocal(std[hg][:, :], std[hg][:, :]))
                    nc.vector.tensor_tensor(std[hg][:, :], std[hg][:, :], cen[hg][:, :], ALU.mult).then_inc(norm_ready, 1)
                bank = in_bank(dve, ("proj", u))
                dve.wait_ge(bias_added, 1)
                xs = x_res[:, TPU * u:TPU * (u + 1), :].rearrange("p i e -> p (i e)")
                nc.vector.tensor_tensor(xs, bank[:, :], xs, ALU.add).then_inc(x_done, 1)

        @block.scalar
        def _(act):
            ln.on_scalar(act)
            for u in range(UNITS):
                ln.copy(act, u)
            for u in range(UNITS):
                for hg in range(HG):
                    bank = in_bank(act, ("g", u, hg))
                    at = W_REST["bg"][0] + hg
                    nc.scalar.activation(gate[:, hg, UT * u:UT * (u + 1)], bank[:, :], ACT.Silu, bias=w[:, at:at + 1]
                                         ).then_inc(gate_ready, 1)
            for u in range(UNITS):
                bank = in_bank(act, ("kt", u))
                nc.scalar.copy(ktok[u % 2][:, :, :].rearrange("p a b -> p (a b)"), bank[:, 0:2 * P]).then_inc(ktok_ready, 1)
                for hg in range(HG):
                    act.wait_ge(o_mm, 8 * (u + 1) - (1 - hg))
                    if u > 0:
                        act.wait_ge(cen_ready, HG * (u - 1) + hg + 1)
                    nc.scalar.copy(o_sb[hg][:, :], o_bank[hg][:, :]).then_inc(o_ready, 1)
                for hg in range(HG):
                    bank = in_bank(act, ("var", u, hg))
                    if u > 0:
                        act.wait_ge(gated_ready, HG * (u - 1) + hg + 1)
                    nc.scalar.activation(std[hg][:, :], bank[:, :], ACT.Sqrt, bias=ln.eps[:, 0:1]).then_inc(std_ready, 1)

        @block.tensor
        def _(pe):
            def fill(key):
                pe.wait_ge(*read(use[key] - 4))
                return work[use[key] % 4]

            for u in range(UNITS):
                ln.turn(pe, u)
            for u in range(UNITS):
                cols = slice(UT * u, UT * (u + 1))
                pe.wait_ge(ln.xt_ready, u + 1)
                for k in ("q", "qs", "k", "ks"):
                    pe.matmul(fill((k, u))[:, :], wcol(k), ln.xt[:, cols], start=True, stop=True).then_inc(work_mm, 1)
                for half in range(2):
                    bank = fill(("v", u, half))
                    for t in range(2):
                        at = UT * u + P * (2 * half + t)
                        ins = pe.matmul(bank[:, 2 * E * t:2 * E * (t + 1)], ln.xt[:, at:at + P], wcol("v"),
                                        start=True, stop=True)
                    ins.then_inc(work_mm, 1)
                for hg in range(HG):
                    pe.matmul(fill(("g", u, hg))[:, :], wcol("gate")[:, P * hg:P * (hg + 1)], ln.xt[:, cols],
                              start=True, stop=True).then_inc(work_mm, 1)
            for u in range(UNITS):
                pe.wait_ge(rot_ready, 2 * u + 2)
                bank = fill(("kt", u))
                for b in range(2):
                    at = UT * u + SEQ * b
                    ins = pe.transpose(bank[:, P * b:P * (b + 1)], rot["k"][:, at:at + P], ln.ident)
                ins.then_inc(work_mm, 1)

                def scores(i):
                    n = 8 * u + i
                    t, hg = ITEMS[i]
                    if n >= 2:
                        pe.wait_ge(masked_ready, n - 1)
                    at = UT * u + P * t
                    pe.matmul(s_bank[n % 2][:, :].rearrange("p (h i) -> p h i", h=4), rot["k"][:, at:at + P],
                              qbd[u % 2][:, 4 * hg:4 * hg + 4, P * t:P * (t + 1)], start=True, stop=True
                              ).then_inc(s_mm, 1)

                pe.wait_ge(qbd_loaded[u % 2], 16 * RH * (u // 2 + 1))
                scores(0)
                bank = fill(("u", u))
                pe.wait_ge(ktok_ready, u + 1)
                pe.wait_ge(val_ready, 2 * u + 2)
                for b in range(2):
                    ins = pe.matmul(bank[:, 2 * E * b:2 * E * (b + 1)], ktok[u % 2][:, b, :], val[:, TPU * u + 2 * b, :],
                                    start=True, stop=True)
                ins.then_inc(work_mm, 1)
                for i, (t, hg) in enumerate(ITEMS):
                    if i + 1 < 8:
                        scores(i + 1)
                    out = o_bank[hg][:, P * t:P * (t + 1)]
                    if i < 2 and u > 0:
                        pe.wait_ge(o_ready, HG * (u - 1) + hg + 1)
                    if t % 2 == 1:
                        pe.wait_ge(kv_ready, u + 1)
                        at = UT * u + P * t
                        pe.matmul(out, kv[u % 2][:, t // 2, P * hg:P * (hg + 1)], rot["q"][:, at:at + P],
                                  start=True, stop=False)
                    pe.wait_ge(masked_ready, 8 * u + i + 1)
                    for j in range(4):
                        h = 4 * hg + j
                        ins = pe.matmul(out[32 * j:32 * j + 32, :], val[:, TPU * u + t, RV * h:RV * (h + 1)],
                                        masked[(8 * u + i) % 4][:, j, :], start=(t % 2 == 0), stop=True)
                    ins.then_inc(o_mm, 1)
                for hg in range(HG):
                    bank = fill(("mean", u, hg))
                    pe.wait_ge(o_ready, HG * u + hg + 1)
                    pe.matmul(bank[:, :], ccol("mean"), o_sb[hg][:, :], start=True, stop=True).then_inc(work_mm, 1)
                for hg in range(HG):
                    bank = fill(("var", u, hg))
                    pe.wait_ge(sq_ready, HG * u + hg + 1)
                    pe.matmul(bank[:, :], ccol("mean"), sq[hg][:, :], start=True, stop=True).then_inc(work_mm, 1)
                bank = fill(("proj", u))
                pe.wait_ge(gated_ready, HG * (u + 1))
                for t in range(TPU):
                    for hg in range(HG):
                        ins = pe.matmul(bank[:, P * t:P * (t + 1)], gated[hg][:, P * t:P * (t + 1)], wcol(f"p{hg}"),
                                        start=(hg == 0), stop=(hg == HG - 1))
                ins.then_inc(work_mm, 1)


def build(nc, ins, out):
    parts = nc.dram_tensor("scratch_parts", (2, 2, AH * 32, UT), F32, kind="Internal").ap()
    dram = dict(ins)
    dram["parts"] = [[parts[kind, which] for which in range(2)] for kind in range(2)]
    dram["o"] = nc.dram_tensor("scratch_o", (2, P, UT), F32, kind="Internal").ap()
    with ExitStack() as ctx:
        mem = {
            "x_res": ctx.enter_context(nc.sbuf_tensor("x_res", [P, TILES, E], F32)),
            "w_att": ctx.enter_context(nc.sbuf_tensor("w_att", [P, W_ATT_N], F32)),
            "w_rest": ctx.enter_context(nc.sbuf_tensor("w_rest", [P, W_REST_N], F32)),
            "const": ctx.enter_context(nc.sbuf_tensor("const", [P, CONST_N], F32)),
            "rest_loaded": ctx.enter_context(nc.semaphore("rest_loaded")),
        }
        attention_stage(nc, mem, dram, ins["x"])
        coupled_stage(nc, mem, "f0", None)
        retention_stage(nc, mem)
        coupled_stage(nc, mem, "f1", out)


def _constants():
    import numpy as np

    aux = np.zeros((2, 2, 8, UT), np.float32)
    aux[:, 0, 0:2] = 1.0
    window = np.arange(UT) % P // WIN
    for bit in range(3):
        on = (window >> bit & 1).astype(np.float32)
        aux[1, 1, 2 + 2 * bit], aux[1, 1, 3 + 2 * bit] = on, 1 - on
        aux[1, 0, 2 + 2 * bit], aux[1, 0, 3 + 2 * bit] = -FAR * (1 - on), -FAR * on

    f32 = np.float32
    pos = np.arange(SEQ, dtype=f32)
    half = E // 2
    scale_vec = (np.arange(0, E, 2, dtype=f32) + f32(0.4 * E)) / f32(1.4 * E)
    scale = scale_vec[None, :].astype(np.float64) ** (pos[:, None].astype(np.float64) / 512.0)
    inv_freq = (f32(1.0) / f32(10000.0) ** (np.arange(half, dtype=f32) / f32(half))).astype(f32)
    angle = (pos[:, None] * inv_freq[None, :]).astype(f32).astype(np.float64)
    gamma = f32(1.0) - np.exp(np.linspace(np.log(1 / 32), np.log(1 / 512), RH).astype(f32)).astype(f32)
    log_decay = np.log(gamma).astype(f32).astype(np.float64)
    decay = np.exp(log_decay[:, None, None] * np.maximum(pos[:, None] - pos[None, :], 0.0))
    norm = np.sqrt((decay * (pos[:, None] >= pos[None, :])).sum(-1))
    head = np.arange(E) // RK
    q_side = np.exp(log_decay[head][:, None] * pos[None, :]) / norm[head] * RK ** -0.5
    k_side = np.exp(-log_decay[head][:, None] * pos[None, :])
    sign = np.where(np.arange(E) % 2 == 0, -1.0, 1.0)[:, None]
    wide = lambda a: np.repeat(a, 2, axis=1).T
    const = np.zeros((P, CONST_N), np.float32)

    def put(name, a):
        at, n = CONST[name]
        const[:, at:at + n] = a

    put("ident", np.eye(P))
    put("cos_q", wide(np.cos(angle) * scale) * q_side)
    put("sin_q", wide(np.sin(angle) * scale) * q_side * sign)
    put("cos_k", wide(np.cos(angle) / scale) * k_side)
    put("sin_k", wide(np.sin(angle) / scale) * k_side * sign)
    put("heads", head[:, None] == (np.arange(2 * E) // RV)[None, :])
    put("causal", np.arange(P)[:, None] <= np.arange(P)[None, :])
    put("mean", (np.arange(P)[:, None] // RV == np.arange(P)[None, :] // RV) / RV)
    blocks = np.arange(P) // 32
    put("sign", np.where((blocks == 0) | (blocks == 3), -1.0, 1.0)[:, None])
    return aux, const


def _pack(spec, total, blocks):
    import numpy as np

    out = np.zeros((P, total), np.float32)
    for name, a in blocks.items():
        at, n = spec[name]
        a = np.asarray(a)
        out[:a.shape[0], at:at + n] = a
    return out


def kernel(**inputs):
    import numpy as np
    import concourse.bacc as _bacc
    from concourse.bass_utils import run_bass_kernel_spmd as _run

    a = {k.replace("L0_attn_a_", "a_").replace("L0_attn_b_", "r_").replace("L0_ffn_", "f_"): np.asarray(v)
         for k, v in inputs.items()}
    column = lambda v: v.reshape(-1, P).T
    spread = lambda v: np.broadcast_to(v[None, :], (P, v.shape[0]))
    order = np.arange(E).reshape(AG, AJ, AD)
    rows = np.concatenate([order[:3].transpose(1, 0, 2).reshape(-1), order[3].reshape(-1)])
    att = _pack(W_ATT, W_ATT_N, {
        "in_g": a["a_w_in_g"].T, "in_l": a["a_w_in_l"].T,
        "out_g": a["a_w_out_g"].T[rows], "out_l": a["a_w_out_l"].T[rows],
        "f_g": a["a_w_f"].T[:E], "f_l": a["a_w_f"].T[E:],
        "b_in_g": column(a["a_b_in_g"]), "b_in_l": column(a["a_b_in_l"]),
        "b_v_g": a["a_b_in_g"][2 * E:][rows][:, None], "b_v_l": a["a_b_in_l"][2 * E:][rows][:, None],
        "b_out_g": column(a["a_b_out_g"]), "b_out_l": column(a["a_b_out_l"]), "b_f": spread(a["a_b_f"])})

    swap = np.arange(E) ^ 1
    turn = (np.arange(E) + 64) % E
    w1 = a["f_cn_w1"]
    w_q, w_k, w_v = a["r_w_qkv"][:, :E], a["r_w_qkv"][:, E:2 * E], a["r_w_qkv"][:, 2 * E:]
    b_q, b_k, b_v = a["r_b_qkv"][:E], a["r_b_qkv"][E:2 * E], a["r_b_qkv"][2 * E:]
    c3 = np.zeros((P, E // 2), np.float32)
    c3[:64, :32], c3[64:, 32:] = a["f_cn_w3"], a["f_cn_w3"]
    c4 = np.zeros((64, 2 * E), np.float32)
    c4[:32, :E], c4[32:, E:] = a["f_cn_w4"], a["f_cn_w4"]
    tile = lambda v, n: np.concatenate([v] * n)[:, None]
    rest = _pack(W_REST, W_REST_N, {
        "c1": w1, "c1p": w1[turn], "c2": a["f_cn_w2"], "c3": c3, "c4r": c4,
        "b1": column(a["f_cn_b1"]), "b2": tile(a["f_cn_b2"], 2), "b3": tile(a["f_cn_b3"], 4),
        "b4": tile(a["f_cn_b4"], P), "range": tile(a["f_adaptive_range"], P),
        "g1": a["f_gc_w1"], "g2": a["f_gc_w2"], "g3r": np.broadcast_to(a["f_gc_w3"], (32, P)),
        "gb1": a["f_gc_b1"][:, None], "gb2": a["f_gc_b2"][:, None], "gb3": tile(a["f_gc_b3"], P),
        "q": w_q, "k": w_k, "qs": w_q[:, swap], "ks": w_k[:, swap], "v": w_v, "gate": a["r_w_g"],
        "p0": a["r_w_p"][:P], "p1": a["r_w_p"][P:],
        "bq": column(b_q), "bk": column(b_k), "bqs": column(b_q[swap]), "bks": column(b_k[swap]),
        "bg": column(a["r_b_g"]), "b_v": spread(b_v), "b_p": spread(a["r_b_p"])})
    aux, const = _constants()

    nc = _bacc.Bacc("TRN2", target_bir_lowering=False, num_devices=1)
    arrays = {"x": a["a_x"].reshape(TOK, E), "w_att": att, "w_rest": rest, "aux": aux, "const": const}
    ins = {n: nc.dram_tensor("in_" + n, v.shape, F32, kind="ExternalInput").ap() for n, v in arrays.items()}
    out = nc.dram_tensor("out_0", (TOK, E), F32, kind="ExternalOutput").ap()
    build(nc, ins, out)
    r = _run(nc, [{"in_" + n: np.ascontiguousarray(v) for n, v in arrays.items()}], core_ids=[0])
    return np.asarray(r.results[0]["out_0"]).reshape(a["a_x"].shape)
```

```python
from contextlib import ExitStack

import concourse.bass as bass
from concourse import mybir

F32 = mybir.dt.float32
F32R = mybir.dt.float32r
ALU = mybir.AluOpType
ACT = mybir.ActivationFunctionType
AX_X = mybir.AxisListType.X

P = 128
BATCH, SEQ, E = 8, 256, 128
TOK = BATCH * SEQ
TILES = TOK // P
UT = 512
UNITS = TOK // UT
TPU = UT // P
EPS = 1e-5

AH, AD = 16, 8
AG, AJ = 4, 4
WIN = 16
A_SCALE = float(AD) ** -0.5
FAR = 2.0 ** 100

RH, RK, RV = 8, 16, 32


def columns(spec):
    at, out = 0, {}
    for name, width in spec:
        out[name] = (at, width)
        at += width
    return out, at


W_ATT, W_ATT_N = columns([
    ("in_g", 3 * E), ("in_l", 3 * E), ("out_g", E), ("out_l", E), ("f_g", E), ("f_l", E),
    ("b_in_g", 2), ("b_in_l", 2), ("b_v_g", P), ("b_v_l", P), ("b_out_g", P), ("b_out_l", P), ("b_f", E)])
W_REST, W_REST_N = columns([
    ("c1", E), ("c1p", E), ("c2", E // 2), ("c3", E // 2), ("c4r", 2 * E),
    ("b1", 1), ("b2", 1), ("b3", 1), ("b4", 1), ("range", 1),
    ("g1", E // 2), ("g2", E // 4), ("g3r", E), ("gb1", 1), ("gb2", 1), ("gb3", 1),
    ("q", E), ("k", E), ("qs", E), ("ks", E), ("v", 2 * E), ("gate", 2 * E), ("p0", E), ("p1", E),
    ("bq", 1), ("bk", 1), ("bqs", 1), ("bks", 1), ("bg", 2), ("b_v", 2 * E), ("b_p", E)])
CONST, CONST_N = columns([
    ("ident", P), ("cos_q", SEQ), ("sin_q", SEQ), ("cos_k", SEQ), ("sin_k", SEQ),
    ("heads", 2 * E), ("causal", P), ("mean", P), ("sign", 1)])


class Chain:

    def __init__(self, eng, sem):
        self.eng, self.sem, self.n = eng, sem, 0

    def after(self, ins):
        self.n += 1
        ins.then_inc(self.sem, 1)
        self.eng.wait_ge(self.sem, self.n)


class LayerNorm:

    def __init__(self, nc, ctx, mem, tag, banks):
        def sb(name, shape):
            return ctx.enter_context(nc.sbuf_tensor(f"{tag}_{name}", shape, F32))

        def sem(name):
            return ctx.enter_context(nc.semaphore(f"{tag}_{name}"))

        self.nc, self.x_res, self.banks = nc, mem["x_res"], banks
        self.ident = mem["const"][:, CONST["ident"][0]:CONST["ident"][0] + P]
        self.xn, self.xt = sb("xn", [P, TILES, E]), sb("xt", [P, TOK])
        self.stats, self.mv = sb("stats", [P, TILES, 6]), sb("mv", [P, TILES, 2])
        self.std, self.rstd, self.eps = sb("std", [P, TILES]), sb("rstd", [P, TILES]), sb("eps", [P, 1])
        self.eps_set = sem("eps_set")
        self.var_ready = sem("var_ready")
        self.std_ready = sem("std_ready")
        self.xn_ready = sem("xn_ready")
        self.turned = sem("turned")
        self.xt_ready = sem("xt_ready")

    def on_pool(self):
        self.nc.gpsimd.memset(self.eps[:, :], EPS).then_inc(self.eps_set, 1)

    def on_vector(self, dve, chain, loaded=None):
        nc = self.nc
        for u in range(UNITS + 1):
            if u < UNITS:
                if loaded is not None:
                    dve.wait_ge(loaded[u], 16)
                for i in range(TPU * u, TPU * (u + 1)):
                    last = nc.vector.bn_stats(self.stats[:, i, :], self.x_res[:, i, :])
                chain.after(last)
                for i in range(TPU * u, TPU * (u + 1)):
                    last = nc.vector.bn_aggr(self.mv[:, i, :], self.stats[:, i, :])
                last.then_inc(self.var_ready, 1)
            if u > 0:
                tiles = slice(TPU * (u - 1), TPU * u)
                dve.wait_ge(self.std_ready, u)
                chain.after(nc.vector.reciprocal(self.rstd[:, tiles], self.std[:, tiles]))
                for i in range(TPU * (u - 1), TPU * u):
                    nc.vector.tensor_scalar(self.xn[:, i, :], self.x_res[:, i, :], self.mv[:, i, 0:1],
                                            self.rstd[:, i:i + 1], ALU.subtract, ALU.mult
                                            ).then_inc(self.xn_ready, 1)

    def on_scalar(self, act):
        act.wait_ge(self.eps_set, 1)
        for u in range(UNITS):
            tiles = slice(TPU * u, TPU * (u + 1))
            act.wait_ge(self.var_ready, u + 1)
            self.nc.scalar.activation(self.std[:, tiles], self.mv[:, tiles, 1], ACT.Sqrt, bias=self.eps[:, 0:1]
                                      ).then_inc(self.std_ready, 1)

    def turn(self, pe, u):
        pe.wait_ge(self.xn_ready, TPU * (u + 1))
        for t in range(TPU):
            ins = pe.transpose(self.banks[u][:, P * t:P * (t + 1)], self.xn[:, TPU * u + t, :], self.ident)
        ins.then_inc(self.turned, 1)

    def copy(self, act, u):
        act.wait_ge(self.turned, u + 1)
        self.nc.scalar.copy(self.xt[:, UT * u:UT * (u + 1)], self.banks[u][:, :]).then_inc(self.xt_ready, 1)


KINDS = "lg"
A_UNITS = 2 * UNITS
HALVES = 2 * A_UNITS
HT = UT // 2


def kind_of(u):
    return KINDS[u % 2]


def attention_events():
    chunks = [8 if kind_of(v // 2) == "g" else 4 for v in range(HALVES)]
    banks = [16 if kind_of(v // 2) == "g" else 8 for v in range(HALVES)]
    maxima = lambda v: [("max", v, n) for n in range(banks[v])] + [("shift", v)]
    ev = [("xt", 0), ("proj", 0), ("load", 0), ("load", 1), ("proj", 1), ("load", 2)]
    ev += [("xt", p) for p in range(1, UNITS)] + [("weights", 0)]
    ev += maxima(0) + maxima(1)
    for v in range(HALVES):
        spread = maxima(v + 2)[:-1] if v + 2 < HALVES else []
        if v + 3 < HALVES:
            ev.append(("load", v + 3))
        ev.append(("st", v, 0))
        for c in range(chunks[v]):
            if c + 1 < chunks[v]:
                ev.append(("st", v, c + 1))
            ev += spread[c * len(spread) // chunks[v]:(c + 1) * len(spread) // chunks[v]]
            ev.append(("pv", v, c))
            if c == 0 and v % 2 == 0 and v // 2 + 2 < A_UNITS:
                ev.append(("proj", v // 2 + 2))
            if c == chunks[v] - 2 and v % 2 == 1 and v >= 3:
                ev.append(("norm", v // 2 - 1))
        if spread:
            ev.append(("shift", v + 2))
        if v % 2 == 1:
            ev.append(("evac", v // 2))
            if v % 4 == 1 and v >= 5:
                ev.append(("fuse", v // 4 - 1))
    ev += [("norm", A_UNITS - 1), ("fuse", UNITS - 1)]
    return ev, chunks, banks


def attention_stage(nc, mem, dram, x_in):
    events, chunks, banks = attention_events()
    first_chunk = [sum(chunks[:v]) for v in range(HALVES + 1)]
    first_bank = [sum(banks[:v]) for v in range(HALVES + 1)]

    keys = []
    for e in events:
        if e[0] == "proj":
            keys += [("proj", e[1], part) for part in ("k", "q", "v")]
        elif e[0] == "weights":
            keys += [("w", "g"), ("w", "l"), ("bias",)]
        elif e[0] in ("xt", "max", "shift", "fuse"):
            keys.append(e)
    use = {key: n for n, key in enumerate(keys)}
    mine = [key for key in keys if key[0] != "xt"]
    filled = {key: n + 1 for n, key in enumerate(mine)}

    with ExitStack() as ctx:
        def sb(name, shape, dt=F32):
            return ctx.enter_context(nc.sbuf_tensor(name, shape, dt))

        def ps(name, shape):
            return ctx.enter_context(nc.psum_tensor(name, shape, F32))

        def sem(name):
            return ctx.enter_context(nc.semaphore(name))

        x_res, wa, const = mem["x_res"], mem["w_att"], mem["const"]
        qbd = [sb(f"a_qbd{i}", [P, AG, AJ, UT], F32R) for i in range(2)]
        kst = [sb(f"a_kst{i}", [P, AG, UT], F32R) for i in range(2)]
        vx = [sb(f"a_vx{i}", [P, TPU, AH, 32]) for i in range(3)]
        probs = [sb(f"a_probs{i}", [P, 1024]) for i in range(4)]
        hi = {k: sb(f"a_{k}hi", [P, UT], F32R) for k in "kq"}
        lo = {k: sb(f"a_{k}lo", [P, UT], F32R) for k in "kq"}
        mx = sb("a_mx", [P, 2 * AJ, AG])
        ml = sb("a_ml", [P, 2 * AJ, 2, AG], F32R)
        mrow = sb("a_mrow", [32, HT], F32R)
        o_raw = sb("a_o_raw", [P, 2, UT])
        o_val = sb("a_o_val", [P, UT])
        o_den = sb("a_o_den", [P, UT])
        o_nrm = {k: sb(f"a_o_nrm_{k}", [P, UT]) for k in KINDS}
        w_out = {k: sb(f"a_w_out_{k}", [P, E]) for k in KINDS}
        bias = sb("a_bias", [P, E])

        st = [ps(f"a_st{i}", [P, 2, 512]) for i in range(2)]
        work = [ps(f"a_work{i}", [P, 512]) for i in range(2)]
        pv_bank = [ps(f"a_pv{i}", [P, 512]) for i in range(2)]
        ln = LayerNorm(nc, ctx, mem, "a", [work[p % 2] for p in range(UNITS)])
        xt = ln.xt

        x_loaded = [sem(f"x_loaded{p}") for p in range(UNITS)]
        w_loaded, aux_set = sem("w_loaded"), sem("aux_set")
        zeroed = sem("zeroed")
        w_ready = sem("w_ready")
        bias_ready = sem("bias_ready")
        bias_added = sem("bias_added")
        work_mm = sem("work_mm")
        max_done = sem("max_done")
        hi_ready, lo_ready = sem("hi_ready"), sem("lo_ready")
        parts_stored = sem("parts_stored")
        qk_loaded = [sem(f"qk_loaded{i}") for i in range(4)]
        v_ready = sem("v_ready")
        ml_ready = sem("ml_ready")
        mrow_ready = sem("mrow_ready")
        mrow_placed = sem("mrow_placed")
        st_ready = sem("st_ready")
        probs_ready = sem("probs_ready")
        pv_done = sem("pv_done")
        o_evacuated = sem("o_evacuated")
        o_stored, o_loaded = sem("o_stored"), sem("o_loaded")
        o_scaled = sem("o_scaled")
        x_done = sem("x_done")
        dve_chain, pool_chain = sem("a_dve_chain"), sem("a_pool_chain")

        block = ctx.enter_context(nc.Block())
        col = lambda name: slice(W_ATT[name][0], sum(W_ATT[name]))

        def in_bank(eng, key):
            eng.wait_ge(work_mm, filled[key])
            return work[use[key] % 2]

        def read(key):
            kind = key[0]
            if kind == "proj":
                _, u, part = key
                return {"k": (lo_ready, 2 * u + 1), "q": (lo_ready, 2 * u + 2), "v": (v_ready, u + 1)}[part]
            if kind == "w":
                return w_ready, 1 + "gl".index(key[1])
            if kind == "bias":
                return bias_ready, 1
            if kind == "max":
                return max_done, first_bank[key[1]] + key[2] + 1
            return {"xt": ln.xt_ready, "shift": mrow_ready, "fuse": x_done}[kind], key[1] + 1

        def max_step(v, n):
            if kind_of(v // 2) == "g":
                return n // 8, n % 8 // 2, 2 * (n % 2), 2
            return n // AG, n % AG, 0, 4

        @block.sync
        def _(sp):
            x_tiles = x_in.rearrange("(i p) e -> p i e", p=P)
            load_x = lambda p: sp.dma_start(x_res[:, TPU * p:TPU * (p + 1), :], x_tiles[:, TPU * p:TPU * (p + 1), :]
                                            ).then_inc(x_loaded[p], 16)
            load_x(0)
            sp.dma_start(const[:, :], dram["const"]).then_inc(w_loaded, 16)
            sp.dma_start(wa[:, :], dram["w_att"]).then_inc(w_loaded, 16)
            for p in range(1, UNITS):
                load_x(p)
            for kind in range(2):
                for which in range(2):
                    dst = dram["parts"][kind][which].rearrange("(h r) t -> h r t", r=32)[:, 24:32, :]
                    src = dram["aux"][kind, which]
                    sp.dma_start(dst, bass.AP(src.tensor, src.offset, [[0, AH], [UT, 8], [1, UT]])
                                 ).then_inc(aux_set, 16)
            for e in events:
                if e[0] == "proj":
                    u = e[1]
                    if u >= 2:
                        for b in range(2):
                            sp.wait_ge(qk_loaded[2 * (u % 2) + b], 80 * (u // 2))
                    for n, (k, where) in enumerate([("k", [("hi", 0), ("lo", 1), ("hi", 2)]),
                                                    ("q", [("hi", 0), ("hi", 1), ("lo", 2)])]):
                        sp.wait_ge(hi_ready, 2 * u + n + 1)
                        sp.wait_ge(lo_ready, 2 * u + n + 1)
                        scratch = dram["parts"][u % 2][n].rearrange("(h r) t -> h r t", r=32)
                        for part, r in where:
                            src = (hi if part == "hi" else lo)[k]
                            sp.dma_start(scratch[:, 8 * r:8 * r + 8, :], src[:, :].bitcast(F32)
                                         ).then_inc(parts_stored, 16)
                elif e[0] == "load":
                    v = e[1]
                    u, b = v // 2, v % 2
                    cols = slice(HT * b, HT * (b + 1))
                    sp.wait_ge(parts_stored, 96 * (u + 1))
                    if v < 4:
                        sp.wait_ge(aux_set, 64)
                        sp.wait_ge(zeroed, u + 1)
                    else:
                        sp.wait_ge(st_ready, first_chunk[v - 3])
                    sp.dma_start(kst[u % 2][:, :, cols].bitcast(F32),
                                 dram["parts"][u % 2][0].rearrange("(g p) t -> p g t", p=P)[:, :, cols]
                                 ).then_inc(qk_loaded[v % 4], 16)
                    queries = dram["parts"][u % 2][1].rearrange("(g j r) t -> j r g t", g=AG, j=AJ)
                    for j in range(AJ):
                        sp.dma_start(qbd[u % 2][32 * j:32 * j + 32, :, j, cols].bitcast(F32),
                                     queries[j][:, :, cols]).then_inc(qk_loaded[v % 4], 16)
                    if v == 2:
                        sp.dma_start(mem["w_rest"][:, :], dram["w_rest"]).then_inc(mem["rest_loaded"], 16)
                elif e[0] == "shift":
                    v = e[1]
                    cols = slice(HT * (v % 2), HT * (v % 2 + 1))
                    sp.wait_ge(mrow_ready, v + 1)
                    for j in range(AJ):
                        sp.dma_start(qbd[v // 2 % 2][32 * j + 24:32 * j + 26, :, j, cols].bitcast(F32),
                                     mrow[8 * j:8 * j + 8, :].bitcast(F32)).then_inc(mrow_placed, 16)
                elif e[0] == "evac":
                    u = e[1]
                    sp.wait_ge(o_evacuated, u + 1)
                    if u >= 1:
                        sp.wait_ge(o_loaded, 112 * u)
                    sp.dma_start(dram["o"].rearrange("a p t -> p a t"), o_raw[:, :, :]).then_inc(o_stored, 16)
                    sp.wait_ge(o_stored, 16 * (u + 1))
                    if u >= 1:
                        sp.wait_ge(o_scaled, u)
                    o = dram["o"].tensor
                    loads = [(o_val[0:96, :], 0, [[32 * UT, AJ], [UT, 24]]),
                             (o_val[96:P, :], P * UT, [[32 * UT, AJ], [UT, 8]]),
                             (o_den[96:P, :], (P + 8) * UT, [[32 * UT, AJ], [0, 8]])]
                    loads += [(o_den[24 * j:24 * j + 24, :], (32 * j + 24) * UT, [[UT, 3], [0, 8]])
                              for j in range(AJ)]
                    for dst, first, rows in loads:
                        sp.dma_start(dst, bass.AP(o, first, rows + [[1, UT]])).then_inc(o_loaded, 16)

        @block.gpsimd
        def _(pool):
            ln.on_pool()
            for i in range(2):
                nc.gpsimd.memset(qbd[i][:, :, :, :].bitcast(F32), 0.0).then_inc(zeroed, 1)
            for i in range(3):
                nc.gpsimd.memset(vx[i][:, :, :, :], 0.0).then_inc(pool_chain, 1)
                pool.wait_ge(pool_chain, 1 + i)
                for g in range(AG):
                    one = 24 + g if g < 3 else 8
                    last = nc.gpsimd.memset(vx[i][:, :, 4 * g:4 * g + 4, one], 1.0)
                last.then_inc(zeroed, 1)
            pool.wait_ge(bias_ready, 1)
            for p in range(UNITS):
                pool.wait_ge(ln.xn_ready, TPU * (p + 1))
                for i in range(TPU * p, TPU * (p + 1)):
                    ins = nc.gpsimd.tensor_tensor(x_res[:, i, :], x_res[:, i, :], bias[:, :], ALU.add)
                ins.then_inc(bias_added, 1)

        @block.vector
        def _(dve):
            chain = Chain(dve, dve_chain)
            ln.on_vector(dve, chain, x_loaded)
            for e in events:
                if e[0] == "proj":
                    u = e[1]
                    for n, k in enumerate("kq"):
                        bank = in_bank(dve, ("proj", u, k))
                        dve.wait_ge(hi_ready, 2 * u + n + 1)
                        if u >= 1:
                            dve.wait_ge(parts_stored, 96 * u)
                        at = W_ATT["b_in_" + kind_of(u)][0] + (1 if k == "k" else 0)
                        nc.vector.scalar_tensor_tensor(
                            out=lo[k][:, :], in0=bank[:, :], scalar=wa[:, at:at + 1],
                            in1=hi[k][:, :].bitcast(F32), op0=ALU.add, op1=ALU.subtract).then_inc(lo_ready, 1)
                elif e[0] == "weights":
                    bank = in_bank(dve, ("bias",))
                    nc.vector.tensor_tensor(bias[:, :], bank[:, 0:E], wa[:, col("b_f")], ALU.add).then_inc(bias_ready, 1)
                elif e[0] == "max":
                    _, v, n = e
                    bank = in_bank(dve, e)
                    qt, g, j, heads = max_step(v, n)
                    nc.vector.tensor_reduce(mx[:, AJ * qt + j:AJ * qt + j + heads, g],
                                            bank[:, :].rearrange("p (h k) -> p h k", h=heads), AX_X, ALU.max
                                            ).then_inc(max_done, 1)
                elif e[0] == "shift":
                    v = e[1]
                    dve.wait_ge(max_done, first_bank[v + 1])
                    if v >= 1:
                        dve.wait_ge(mrow_ready, v)
                    chain.after(nc.vector.tensor_scalar(ml[:, :, 0, :], mx[:, :, :], -1.0, None, ALU.mult))
                    nc.vector.scalar_tensor_tensor(out=ml[:, :, 1, :], in0=mx[:, :, :], scalar=-1.0,
                                                   in1=ml[:, :, 0, :].bitcast(F32), op0=ALU.mult,
                                                   op1=ALU.subtract).then_inc(ml_ready, 1)
                    dve.wait_ge(ml_ready, v + 1)
                elif e[0] == "norm":
                    u = e[1]
                    dve.wait_ge(o_loaded, 112 * (u + 1))
                    chain.after(nc.vector.reciprocal(o_den[:, :], o_den[:, :]))
                    nc.vector.tensor_tensor(o_nrm[kind_of(u)][:, :], o_val[:, :], o_den[:, :], ALU.mult
                                            ).then_inc(o_scaled, 1)
                elif e[0] == "fuse":
                    p = e[1]
                    bank = in_bank(dve, e)
                    dve.wait_ge(bias_added, p + 1)
                    xs = x_res[:, TPU * p:TPU * (p + 1), :].rearrange("p i e -> p (i e)")
                    nc.vector.tensor_tensor(xs, bank[:, :], xs, ALU.add).then_inc(x_done, 1)

        @block.scalar
        def _(act):
            ln.on_scalar(act)
            for e in events:
                if e[0] == "xt":
                    ln.copy(act, e[1])
                elif e[0] == "proj":
                    u = e[1]
                    for n, k in enumerate("kq"):
                        bank = in_bank(act, ("proj", u, k))
                        if u == 0:
                            act.wait_ge(w_loaded, 32)
                        else:
                            act.wait_ge(parts_stored, 96 * u)
                            act.wait_ge(lo_ready, 2 * u)
                        at = W_ATT["b_in_" + kind_of(u)][0] + (1 if k == "k" else 0)
                        nc.scalar.activation(hi[k][:, :], bank[:, :], ACT.Identity, bias=wa[:, at:at + 1]
                                             ).then_inc(hi_ready, 1)
                    bank = in_bank(act, ("proj", u, "v"))
                    act.wait_ge(zeroed, 5)
                    if u >= 3:
                        act.wait_ge(pv_done, first_chunk[2 * (u - 2)])
                    for g in range(AG):
                        off = 8 * g if g < 3 else 0
                        ins = nc.scalar.copy(
                            vx[u % 3][:, :, 4 * g:4 * g + 4, off:off + 8],
                            bank[:, :].rearrange("p (t g j d) -> p t g j d", t=TPU, g=AG, j=AJ)[:, :, g, :, :])
                    ins.then_inc(v_ready, 1)
                elif e[0] == "weights":
                    for n, k in enumerate("gl"):
                        bank = in_bank(act, ("w", k))
                        nc.scalar.copy(w_out[k][:, :], bank[:, 0:E]).then_inc(w_ready, 1)
                elif e[0] == "shift":
                    v = e[1]
                    bank = in_bank(act, e)
                    if v >= 1:
                        act.wait_ge(mrow_placed, 64 * v)
                    nc.scalar.copy(mrow[:, :], bank[0:32, 0:HT]).then_inc(mrow_ready, 1)
                elif e[0] == "pv":
                    _, v, c = e
                    n = first_chunk[v] + c
                    act.wait_ge(st_ready, n + 1)
                    if n >= 4:
                        act.wait_ge(pv_done, n - 3)
                    nc.scalar.activation(probs[n % 4][:, :], st[n % 2][:, :, :].rearrange("p a b -> p (a b)"),
                                         ACT.Exp, scale=A_SCALE).then_inc(probs_ready, 1)
                elif e[0] == "evac":
                    u = e[1]
                    act.wait_ge(pv_done, first_chunk[2 * u + 2])
                    if u >= 1:
                        act.wait_ge(o_stored, 16 * u)
                    nc.scalar.copy(o_raw[:, 0, :], pv_bank[0][:, :])
                    nc.scalar.copy(o_raw[:, 1, :], pv_bank[1][:, :]).then_inc(o_evacuated, 1)

        @block.tensor
        def _(pe):
            def fill(key):
                n = use[key]
                if n >= 2:
                    pe.wait_ge(*read(keys[n - 2]))
                return work[n % 2]

            def scores(v, c):
                u, b = v // 2, v % 2
                n = first_chunk[v] + c
                if c == 0:
                    pe.wait_ge(mrow_placed, 64 * (v + 1))
                if n >= 2:
                    pe.wait_ge(probs_ready, n - 1)
                q, k = qbd[u % 2], kst[u % 2]
                for half in range(2):
                    out = st[n % 2][:, half, :]
                    if kind_of(u) == "g":
                        kt, g = c // 4, c % 4
                        at = HT * b + P * kt
                        pairs = q[:, g, 2 * half:2 * half + 2, HT * b:HT * (b + 1)]
                        ins = pe.matmul(out.rearrange("p (j q) -> p j q", j=2), k[:, g, at:at + P], pairs,
                                        start=True, stop=True)
                    else:
                        g, at = 2 * (c % 2) + half, HT * b + P * (c // 2)
                        ins = pe.matmul(out.rearrange("p (j q) -> p j q", j=4), k[:, g, at:at + P],
                                        q[:, g, :, at:at + P], start=True, stop=True)
                ins.then_inc(st_ready, 1)

            def outputs(v, c):
                u, b = v // 2, v % 2
                n = first_chunk[v] + c
                pe.wait_ge(probs_ready, n + 1)
                if c == 0 and b == 0:
                    pe.wait_ge(v_ready, u + 1)
                    if u >= 1:
                        pe.wait_ge(o_evacuated, u)
                pr, val = probs[n % 4], vx[u % 3]
                if kind_of(u) == "g":
                    kt, g = c // 4, c % 4
                    for j in range(AJ):
                        ins = pe.matmul(pv_bank[g // 3][32 * j:32 * j + 32, HT * b:HT * (b + 1)],
                                        val[:, 2 * b + kt, 4 * g + j, :], pr[:, HT * j:HT * (j + 1)],
                                        start=(kt == 0 and g in (0, 3)), stop=(kt == 1 and g in (2, 3)))
                else:
                    t = 2 * b + c // 2
                    for half in range(2):
                        g = 2 * (c % 2) + half
                        for j in range(AJ):
                            at = 512 * half + P * j
                            ins = pe.matmul(pv_bank[g // 3][32 * j:32 * j + 32, P * t:P * (t + 1)],
                                            val[:, t, 4 * g + j, :], pr[:, at:at + P],
                                            start=(g in (0, 3)), stop=(g in (2, 3)))
                ins.then_inc(pv_done, 1)

            pe.wait_ge(w_loaded, 32)
            for e in events:
                if e[0] == "xt":
                    fill(e)
                    ln.turn(pe, e[1])
                elif e[0] == "proj":
                    u = e[1]
                    at = W_ATT["in_" + kind_of(u)][0]
                    pe.wait_ge(ln.xt_ready, u // 2 + 1)
                    first = UT * (u // 2)
                    for k, off in (("k", E), ("q", 0)):
                        bank = fill(("proj", u, k))
                        pe.matmul(bank[:, :], wa[:, at + off:at + off + E], xt[:, first:first + UT],
                                  start=True, stop=True).then_inc(work_mm, 1)
                    bank = fill(("proj", u, "v"))
                    for t in range(TPU):
                        ins = pe.matmul(bank[:, P * t:P * (t + 1)], xt[:, first + P * t:first + P * (t + 1)],
                                        wa[:, at + 2 * E:at + 3 * E], start=True, stop=True)
                    ins.then_inc(work_mm, 1)
                elif e[0] == "weights":
                    for k in "gl":
                        bank = fill(("w", k))
                        pe.matmul(bank[:, 0:E], wa[:, col("out_" + k)], wa[:, col("f_" + k)], start=True, stop=True
                                  ).then_inc(work_mm, 1)
                    bank = fill(("bias",))
                    pe.wait_ge(w_ready, 2)
                    for n, k in enumerate("gl"):
                        pe.matmul(bank[:, 0:E], wa[:, col("b_out_" + k)], wa[:, col("f_" + k)],
                                  start=(n == 0), stop=False)
                        ins = pe.matmul(bank[:, 0:E], wa[:, col("b_v_" + k)], w_out[k][:, :],
                                        start=False, stop=(n == 1))
                    ins.then_inc(work_mm, 1)
                elif e[0] == "max":
                    _, v, n = e
                    u, b = v // 2, v % 2
                    bank = fill(e)
                    if n == 0:
                        pe.wait_ge(qk_loaded[v % 4], 80 * (v // 4 + 1))
                    q, k = qbd[u % 2], kst[u % 2]
                    qt, g, j, heads = max_step(v, n)
                    at = HT * b + P * qt
                    own = slice(HT * b, HT * (b + 1)) if kind_of(u) == "g" else slice(at, at + P)
                    width = 512 // heads
                    for i in range(heads):
                        ins = pe.matmul(bank[:, width * i:width * (i + 1)], q[:, g, j + i, at:at + P], k[:, g, own],
                                        start=True, stop=True)
                    ins.then_inc(work_mm, 1)
                elif e[0] == "shift":
                    v = e[1]
                    bank = fill(e)
                    pe.wait_ge(ml_ready, v + 1)
                    for t in range(2):
                        src = ml[:, AJ * t:AJ * (t + 1), :, :].rearrange("p j r g -> p (j r g)").bitcast(F32)
                        ins = pe.transpose(bank[0:32, P * t:P * (t + 1)], src, ln.ident)
                    ins.then_inc(work_mm, 1)
                elif e[0] == "st":
                    scores(e[1], e[2])
                elif e[0] == "pv":
                    outputs(e[1], e[2])
                elif e[0] == "fuse":
                    p = e[1]
                    bank = fill(e)
                    pe.wait_ge(o_scaled, 2 * p + 2)
                    for t in range(TPU):
                        for i, k in enumerate(KINDS):
                            ins = pe.matmul(bank[:, P * t:P * (t + 1)], o_nrm[k][:, P * t:P * (t + 1)],
                                            w_out[k][:, :], start=(i == 0), stop=(i == 1))
                    ins.then_inc(work_mm, 1)


def coupled_stage(nc, mem, tag, out):
    CYCLES, PAIRS = 3, UNITS // 2
    with ExitStack() as ctx:
        def sb(name, shape):
            return ctx.enter_context(nc.sbuf_tensor(f"{tag}_{name}", shape, F32))

        def ps(name, shape):
            return ctx.enter_context(nc.psum_tensor(f"{tag}_{name}", shape, F32))

        def sem(name):
            return ctx.enter_context(nc.semaphore(f"{tag}_{name}"))

        x_res, w, const = mem["x_res"], mem["w_rest"], mem["const"]
        wcol = lambda name: w[:, W_REST[name][0]:sum(W_REST[name])]
        each = lambda name, shape=(P, UT): [sb(f"{name}{t}", list(shape)) for t in range(UNITS)]
        a_sb, b_sb, h_sb, g_sb, t_sb = each("a"), each("b"), each("h"), each("g"), each("t")
        g1 = each("g1")
        g2 = [sb(f"g2{i}", [P, UT]) for i in range(PAIRS)]
        g3 = [sb(f"g3{i}", [64, UT]) for i in range(PAIRS)]
        cc = [each(f"c{n}_") for n in range(CYCLES)]
        txn = sb("txn", [P, TILES, E])
        c1s = sb("c1s", [P, E])
        ctx_sum, gh1, gh2 = sb("ctx", [P, BATCH]), sb("gh1", [64, BATCH]), sb("gh2", [32, BATCH])
        tg, k0 = sb("tg", [P, BATCH]), sb("k0", [P, BATCH])
        k1, k7, hb4, hg3 = sb("k1", [P, 1]), sb("k7", [P, 1]), sb("hb4", [P, 1]), sb("hg3", [P, 1])
        ct = [sb(f"ct{i}", [P, CYCLES, 2 * TPU]) for i in range(PAIRS)]
        ab = [sb(f"ab{i}", [P, 6, 2 * TPU]) for i in range(PAIRS)]
        pa = [ps(f"pa{t}", [P, UT]) for t in range(UNITS)]
        p2 = [ps(f"p2{i}", [P, UT]) for i in range(PAIRS)]
        p3 = [ps(f"p3{i}", [P, UT]) for i in range(PAIRS)]
        pb = [p2[0], p3[0], p2[1], p3[1]]
        ln = LayerNorm(nc, ctx, mem, tag, pa)

        small_ready = sem("small_ready")
        ctx_ready = sem("ctx_ready")
        glob_mm = sem("glob_mm")
        glob_act = sem("glob_act")
        k0_ready = sem("k0_ready")
        a_mm, b_mm = sem("a_mm"), sem("b_mm")
        a_ready, b_ready = sem("a_ready"), sem("b_ready")
        g1_ready = sem("g1_ready")
        l2_mm, l3_mm = sem("l2_mm"), sem("l3_mm")
        g2_ready, g3_ready = sem("g2_ready"), sem("g3_ready")
        z_mm = sem("z_mm")
        t_ready = sem("t_ready")
        c_ready = sem("c_ready")
        h_ready = sem("h_ready")
        g_ready = sem("g_ready")
        txn_ready = sem("txn_ready")
        ct_mm, ct_ready = sem("ct_mm"), sem("ct_ready")
        x_done = sem("x_done")
        stored = sem("stored")
        dve_chain, pool_chain = sem("dve_chain"), sem("pool_chain")
        block = ctx.enter_context(nc.Block())

        if out is not None:
            @block.sync
            def _(sp):
                for i in range(PAIRS):
                    sp.wait_ge(x_done, i + 1)
                    tiles = slice(2 * TPU * i, 2 * TPU * (i + 1))
                    sp.dma_start(out.rearrange("(i p) e -> p i e", p=P)[:, tiles, :], x_res[:, tiles, :]
                                 ).then_inc(stored, 16)
                sp.wait_ge(stored, 16 * PAIRS)

        @block.gpsimd
        def _(pool):
            ln.on_pool()
            chain = Chain(pool, pool_chain)
            pool.wait_ge(mem["rest_loaded"], 16)
            for t in range(UNITS):
                pool.wait_ge(c_ready, t + 1)
                pool.wait_ge(a_ready, t + 1)
                pool.wait_ge(b_ready, t + 1)
                chain.after(nc.gpsimd.tensor_tensor(g_sb[t][:, :], cc[0][t][:, :], a_sb[t][:, :], ALU.mult))
                nc.gpsimd.tensor_tensor(g_sb[t][:, :], b_sb[t][:, :], g_sb[t][:, :], ALU.subtract
                                        ).then_inc(g_ready, 1)
            for block_out, (block_in, sign) in enumerate([(2, 1.0), (3, -1.0), (0, -1.0), (1, 1.0)]):
                ins = nc.gpsimd.tensor_scalar(txn[:, :, 32 * block_out:32 * block_out + 32],
                                              ln.xn[:, :, 32 * block_in:32 * block_in + 32],
                                              sign, None, ALU.mult)
                ins.then_inc(txn_ready, 1)

        @block.vector
        def _(dve):
            chain = Chain(dve, dve_chain)
            dve.wait_ge(mem["rest_loaded"], 16)
            for dst, src, by in ((k1, "range", 0.3), (k7, "range", 0.7), (hb4, "b4", 0.5), (hg3, "gb3", 0.5)):
                nc.vector.tensor_scalar(dst[:, :], wcol(src), by, None, ALU.mult)
            nc.vector.tensor_scalar(c1s[:, :], wcol("c1p"), const[:, CONST["sign"][0]:CONST["sign"][0] + 1],
                                    None, ALU.mult).then_inc(small_ready, 1)
            ln.on_vector(dve, chain)
            for t in range(UNITS):
                dve.wait_ge(ln.xt_ready, t + 1)
                ins = nc.vector.tensor_reduce(ctx_sum[:, 2 * t:2 * t + 2],
                                              ln.xt[:, UT * t:UT * (t + 1)].rearrange("p (b t) -> p b t", b=2),
                                              AX_X, ALU.add)
            ins.then_inc(ctx_ready, 1)
            for t in range(UNITS):
                dve.wait_ge(g1_ready, t + 1)
                nc.vector.tensor_copy(a_sb[t][:, :], pa[t][:, :]).then_inc(a_ready, 1)
            dve.wait_ge(glob_act, 3)
            nc.vector.tensor_scalar(k0[:, :], tg[:, :], k7[:, 0:1], 0.1, ALU.mult, ALU.add).then_inc(k0_ready, 1)
            dve.wait_ge(k0_ready, 1)
            for n in range(CYCLES):
                for t in range(UNITS):
                    dve.wait_ge(t_ready, UNITS * n + t + 1)
                    for b in range(2):
                        cols = slice(SEQ * b, SEQ * (b + 1))
                        ins = nc.vector.tensor_scalar(cc[n][t][:, cols], t_sb[t][:, cols], k1[:, 0:1],
                                                      k0[:, 2 * t + b:2 * t + b + 1], ALU.mult, ALU.add)
                    ins.then_inc(c_ready, 1)
                    if n < CYCLES - 1:
                        dve.wait_ge(c_ready, UNITS * n + t + 1)
                        if n == 0:
                            dve.wait_ge(b_ready, t + 1)
                            dve.wait_ge(a_ready, t + 1)
                        else:
                            dve.wait_ge(g_ready, t + 1)
                        step, base = (b_sb, a_sb) if n == 0 else (g_sb, h_sb)
                        chain.after(nc.vector.tensor_tensor(t_sb[t][:, :], cc[n][t][:, :], step[t][:, :], ALU.mult))
                        nc.vector.tensor_tensor(h_sb[t][:, :], t_sb[t][:, :], base[t][:, :], ALU.add
                                                ).then_inc(h_ready, 1)
            dve.wait_ge(txn_ready, 4)
            for i in range(PAIRS):
                c, s = ct[i], ab[i]
                dve.wait_ge(ct_mm, i + 1)
                nc.vector.tensor_copy(c[:, :, :].rearrange("p n t -> p (n t)"),
                                      p2[i][:, 0:CYCLES * 2 * TPU]).then_inc(ct_ready, 1)
                dve.wait_ge(ct_ready, i + 1)
                TT, TS = nc.vector.tensor_tensor, nc.vector.tensor_scalar
                TT(s[:, 0, :], c[:, 0, :], c[:, 1, :], ALU.mult)
                chain.after(TT(s[:, 1, :], c[:, 0, :], c[:, 1, :], ALU.add))
                chain.after(TS(s[:, 2, :], s[:, 0, :], -1.0, 1.0, ALU.mult, ALU.add))
                TT(s[:, 3, :], c[:, 2, :], s[:, 1, :], ALU.mult)
                chain.after(TT(s[:, 0, :], c[:, 2, :], s[:, 2, :], ALU.mult))
                TT(s[:, 4, :], s[:, 2, :], s[:, 3, :], ALU.subtract)
                chain.after(TT(s[:, 5, :], s[:, 1, :], s[:, 0, :], ALU.add))
                for src, k in ((ln.xn, 4), (txn, 5)):
                    for t in range(2 * TPU):
                        n = 2 * TPU * i + t
                        ins = nc.vector.scalar_tensor_tensor(
                            out=x_res[:, n, :], in0=src[:, n, :], scalar=s[:, k, t:t + 1], in1=x_res[:, n, :],
                            op0=ALU.mult, op1=ALU.add)
                    if k == 4:
                        chain.after(ins)
                ins.then_inc(x_done, 1)

        @block.scalar
        def _(act):
            ln.on_scalar(act)
            act.wait_ge(mem["rest_loaded"], 16)
            act.wait_ge(small_ready, 1)
            for t in range(UNITS):
                ln.copy(act, t)
            gelu = lambda dst, src, bias, scale=1.0: nc.scalar.activation(dst, src, ACT.Gelu, bias=bias, scale=scale)
            for t in range(UNITS):
                act.wait_ge(a_mm, t + 1)
                gelu(g1[t][:, :], pa[t][:, :], wcol("b1")).then_inc(g1_ready, 1)
                act.wait_ge(b_mm, t + 1)
                nc.scalar.copy(b_sb[t][:, :], pb[t][:, :]).then_inc(b_ready, 1)
            for n in range(CYCLES):
                if n > 0:
                    for t in range(UNITS):
                        act.wait_ge(h_ready, UNITS * (n - 1) + t + 1)
                        gelu(g1[t][:, :], h_sb[t][:, :], wcol("b1")).then_inc(g1_ready, 1)
                for i in range(PAIRS):
                    act.wait_ge(l2_mm, PAIRS * n + i + 1)
                    gelu(g2[i][:, :], p2[i][:, :], wcol("b2")).then_inc(g2_ready, 1)
                for i in range(PAIRS):
                    act.wait_ge(l3_mm, PAIRS * n + i + 1)
                    gelu(g3[i][:, :], p3[i][0:64, :], wcol("b3")[0:64]).then_inc(g3_ready, 1)
                if n == 0:
                    act.wait_ge(glob_mm, 1)
                    gelu(gh1[:, :], p3[0][0:64, 0:BATCH], wcol("gb1")[0:64], 1.0 / SEQ).then_inc(glob_act, 1)
                    act.wait_ge(glob_mm, 2)
                    gelu(gh2[:, :], p3[0][0:32, BATCH:2 * BATCH], wcol("gb2")[0:32]).then_inc(glob_act, 1)
                    act.wait_ge(glob_mm, 3)
                    nc.scalar.activation(tg[:, :], p3[0][:, 2 * BATCH:3 * BATCH], ACT.Tanh, bias=hg3[:, 0:1],
                                         scale=0.5).then_inc(glob_act, 1)
                for t in range(UNITS):
                    act.wait_ge(z_mm, UNITS * n + t + 1)
                    if n > 0:
                        act.wait_ge(h_ready, UNITS * (n - 1) + t + 1)
                    nc.scalar.activation(t_sb[t][:, :], pa[t][:, :], ACT.Tanh, bias=hb4[:, 0:1], scale=0.5
                                         ).then_inc(t_ready, 1)

        @block.tensor
        def _(pe):
            for t in range(UNITS):
                ln.turn(pe, t)
            pe.wait_ge(mem["rest_loaded"], 16)
            pe.wait_ge(small_ready, 1)
            for t in range(UNITS):
                cols = slice(UT * t, UT * (t + 1))
                pe.wait_ge(ln.xt_ready, t + 1)
                pe.matmul(pa[t][:, :], wcol("c1"), ln.xt[:, cols], start=True, stop=True).then_inc(a_mm, 1)
                pe.matmul(pb[t][:, :], c1s[:, :], ln.xt[:, cols], start=True, stop=True).then_inc(b_mm, 1)
            for n in range(CYCLES):
                for i in range(PAIRS):
                    pe.wait_ge(g1_ready, UNITS * n + 2 * i + 2)
                    pe.wait_ge(b_ready, 2 * i + 2)
                    if n > 0:
                        pe.wait_ge(g2_ready, PAIRS * (n - 1) + i + 1)
                    for e in range(2):
                        ins = pe.matmul(p2[i][64 * e:64 * e + 64, :], wcol("c2"), g1[2 * i + e][:, :],
                                        start=True, stop=True)
                    ins.then_inc(l2_mm, 1)
                for i in range(PAIRS):
                    pe.wait_ge(g2_ready, PAIRS * n + i + 1)
                    pe.matmul(p3[i][0:64, :], wcol("c3"), g2[i][:, :], start=True, stop=True).then_inc(l3_mm, 1)
                if n == 0:
                    pe.wait_ge(ctx_ready, 1)
                    pe.wait_ge(g3_ready, 2)
                    pe.matmul(p3[0][0:64, 0:BATCH], wcol("g1"), ctx_sum[:, :], start=True, stop=True).then_inc(glob_mm, 1)
                    pe.wait_ge(glob_act, 1)
                    pe.matmul(p3[0][0:32, BATCH:2 * BATCH], wcol("g2")[0:64], gh1[:, :], start=True, stop=True
                              ).then_inc(glob_mm, 1)
                    pe.wait_ge(glob_act, 2)
                    pe.matmul(p3[0][:, 2 * BATCH:3 * BATCH], wcol("g3r")[0:32], gh2[:, :], start=True, stop=True
                              ).then_inc(glob_mm, 1)
                for t in range(UNITS):
                    pe.wait_ge(g3_ready, PAIRS * n + t // 2 + 1)
                    pe.wait_ge(a_ready, t + 1)
                    pe.matmul(pa[t][:, :], wcol("c4r")[0:64, P * (t % 2):P * (t % 2 + 1)], g3[t // 2][:, :],
                              start=True, stop=True).then_inc(z_mm, 1)
            for i in range(PAIRS):
                pe.wait_ge(c_ready, UNITS * (CYCLES - 1) + 2 * i + 2)
                for n in range(CYCLES):
                    for t in range(2 * TPU):
                        col = 2 * TPU * n + t
                        src = cc[n][2 * i + t // TPU][0:1, P * (t % TPU):P * (t % TPU + 1)]
                        ins = pe.transpose(p2[i][:, col:col + 1], src, ln.ident[0:1, 0:1])
                ins.then_inc(ct_mm, 1)


def retention_stage(nc, mem):
    HG = 2
    with ExitStack() as ctx:
        def sb(name, shape):
            return ctx.enter_context(nc.sbuf_tensor(f"r_{name}", shape, F32))

        def ps(name, shape):
            return ctx.enter_context(nc.psum_tensor(f"r_{name}", shape, F32))

        def sem(name):
            return ctx.enter_context(nc.semaphore(f"r_{name}"))

        x_res, w, const = mem["x_res"], mem["w_rest"], mem["const"]
        wcol = lambda name: w[:, W_REST[name][0]:sum(W_REST[name])]
        ccol = lambda name: const[:, CONST[name][0]:sum(CONST[name])]

        def again(ap, n):
            return bass.AP(ap.tensor, ap.offset, [list(ap.ap[0]), [0, n], list(ap.ap[1])])

        rot = {k: sb(f"{k}r", [P, TOK]) for k in "qk"}
        turned = [[sb(f"{k}{i}", [P, UT]) for i in range(2)] for k in "qk"]
        qbd = [sb(f"qbd{i}", [P, RH, UT]) for i in range(2)]
        val = sb("val", [P, TILES, 2 * E])
        gate = sb("gate", [P, HG, TOK])
        ktok = [sb(f"ktok{i}", [P, 2, P]) for i in range(2)]
        kv = [sb(f"kv{i}", [P, 2, 2 * E]) for i in range(2)]
        masked = [sb(f"masked{i}", [P, 4, P]) for i in range(4)]
        o_sb = [sb(f"o{i}", [P, UT]) for i in range(HG)]
        cen = [sb(f"cen{i}", [P, UT]) for i in range(HG)]
        sq = [sb(f"sq{i}", [P, UT]) for i in range(HG)]
        std = [sb(f"sd{i}", [P, UT]) for i in range(HG)]
        gated = [sb(f"gated{i}", [P, UT]) for i in range(HG)]

        work = [ps(f"work{i}", [P, 512]) for i in range(4)]
        s_bank = [ps(f"s{i}", [P, 512]) for i in range(2)]
        o_bank = [ps(f"ob{i}", [P, 512]) for i in range(HG)]
        ln = LayerNorm(nc, ctx, mem, "r", work)

        keys = []
        for u in range(UNITS):
            keys += [(k, u) for k in ("q", "qs", "k", "ks")]
            keys += [("v", u, 0), ("v", u, 1), ("g", u, 0), ("g", u, 1)]
        for u in range(UNITS):
            keys += [("kt", u), ("u", u)]
            keys += [(k, u, hg) for k in ("mean", "var") for hg in range(HG)] + [("proj", u)]
        use = {k: n + UNITS for n, k in enumerate(keys)}

        zeroed = sem("zeroed")
        work_mm = sem("work_mm")
        part_ready = sem("part_ready")
        rot_ready = sem("rot_ready")
        val_ready = sem("val_ready")
        gate_ready = sem("gate_ready")
        qbd_loaded = [sem(f"qbd_loaded{i}") for i in range(2)]
        ktok_ready = sem("ktok_ready")
        kv_ready = sem("kv_ready")
        s_mm = sem("s_mm")
        masked_ready = sem("masked_ready")
        o_mm = sem("o_mm")
        o_ready = sem("o_ready")
        cen_ready = sem("cen_ready")
        sq_ready = sem("sq_ready")
        std_ready = sem("sd_ready")
        norm_ready = sem("norm_ready")
        gated_ready = sem("gated_ready")
        bias_added = sem("bias_added")
        x_done = sem("x_done")
        dve_chain = sem("dve_chain")
        block = ctx.enter_context(nc.Block())

        def in_bank(eng, key):
            eng.wait_ge(work_mm, use[key] - UNITS + 1)
            return work[use[key] % 4]

        def read(n):
            if n < UNITS:
                return ln.xt_ready, n + 1
            key = keys[n - UNITS]
            kind, u = key[0], key[1]
            if kind in ("q", "qs", "k", "ks"):
                return part_ready, 4 * u + ("q", "qs", "k", "ks").index(kind) + 1
            return {"v": lambda: (val_ready, 2 * u + key[2] + 1), "g": lambda: (gate_ready, 2 * u + key[2] + 1),
                    "kt": lambda: (ktok_ready, u + 1), "u": lambda: (kv_ready, u + 1),
                    "mean": lambda: (cen_ready, HG * u + key[2] + 1),
                    "var": lambda: (std_ready, HG * u + key[2] + 1), "proj": lambda: (x_done, u + 1)}[kind]()

        ITEMS = [(t, hg) for t in range(TPU) for hg in range(HG)]

        @block.sync
        def _(sp):
            for u in range(UNITS):
                sp.wait_ge(rot_ready, 2 * u + 1)
                if u < 2:
                    sp.wait_ge(zeroed, u + 1)
                else:
                    sp.wait_ge(s_mm, 8 * (u - 1))
                for h in range(RH):
                    sp.dma_start(qbd[u % 2][RK * h:RK * (h + 1), h, :],
                                 rot["q"][RK * h:RK * (h + 1), UT * u:UT * (u + 1)]).then_inc(qbd_loaded[u % 2], 16)

        @block.gpsimd
        def _(pool):
            ln.on_pool()
            for i in range(2):
                nc.gpsimd.memset(qbd[i][:, :, :], 0.0).then_inc(zeroed, 1)
            for u in range(UNITS):
                for n, k in enumerate("qk"):
                    pool.wait_ge(part_ready, 4 * u + 2 * n + 2)
                    nc.gpsimd.tensor_tensor(rot[k][:, UT * u:UT * (u + 1)], turned[n][0][:, :], turned[n][1][:, :],
                                            ALU.add).then_inc(rot_ready, 1)
            pool.wait_ge(ln.xn_ready, TILES)
            for i in range(TILES):
                ins = nc.gpsimd.tensor_tensor(x_res[:, i, :], x_res[:, i, :], wcol("b_p"), ALU.add)
            ins.then_inc(bias_added, 1)
            for u in range(UNITS):
                for hg in range(HG):
                    n = HG * u + hg + 1
                    pool.wait_ge(cen_ready, n)
                    nc.gpsimd.tensor_tensor(sq[hg][:, :], cen[hg][:, :], cen[hg][:, :], ALU.mult).then_inc(sq_ready, 1)
                for hg in range(HG):
                    n = HG * u + hg + 1
                    pool.wait_ge(norm_ready, n)
                    pool.wait_ge(gate_ready, n)
                    if u > 0:
                        pool.wait_ge(x_done, u)
                    nc.gpsimd.tensor_tensor(gated[hg][:, :], std[hg][:, :], gate[:, hg, UT * u:UT * (u + 1)],
                                            ALU.mult).then_inc(gated_ready, 1)

        @block.vector
        def _(dve):
            chain = Chain(dve, dve_chain)
            ln.on_vector(dve, chain)
            for u in range(UNITS):
                for n, k in enumerate("qk"):
                    if u > 0:
                        dve.wait_ge(rot_ready, 2 * (u - 1) + n + 1)
                    for i, (key, table) in enumerate([(k, "cos_" + k), (k + "s", "sin_" + k)]):
                        bank = in_bank(dve, (key, u))
                        nc.vector.scalar_tensor_tensor(
                            out=turned[n][i][:, :].rearrange("p (b t) -> p b t", b=2),
                            in0=bank[:, :].rearrange("p (b t) -> p b t", b=2), scalar=wcol("b" + key),
                            in1=again(ccol(table), 2), op0=ALU.add, op1=ALU.mult).then_inc(part_ready, 1)
                for half in range(2):
                    bank = in_bank(dve, ("v", u, half))
                    i = TPU * u + 2 * half
                    nc.vector.tensor_tensor(val[:, i:i + 2, :], bank[:, :].rearrange("p (t v) -> p t v", t=2),
                                            again(wcol("b_v"), 2), ALU.add).then_inc(val_ready, 1)
            for u in range(UNITS):
                bank = in_bank(dve, ("u", u))
                if u >= 2:
                    dve.wait_ge(o_mm, 8 * (u - 1))
                nc.vector.tensor_tensor(kv[u % 2][:, :, :], bank[:, :].rearrange("p (t v) -> p t v", t=2),
                                        again(ccol("heads"), 2), ALU.mult).then_inc(kv_ready, 1)
                for i in range(8):
                    n = 8 * u + i
                    dve.wait_ge(s_mm, n + 1)
                    if n >= 4:
                        dve.wait_ge(o_mm, n - 3)
                    nc.vector.tensor_tensor(masked[n % 4][:, :, :], s_bank[n % 2][:, :].rearrange("p (h i) -> p h i", h=4),
                                            again(ccol("causal"), 4), ALU.mult).then_inc(masked_ready, 1)
                for hg in range(HG):
                    n = HG * u + hg + 1
                    bank = in_bank(dve, ("mean", u, hg))
                    if u > 0:
                        dve.wait_ge(norm_ready, n - HG)
                    nc.vector.tensor_tensor(cen[hg][:, :], o_sb[hg][:, :], bank[:, :], ALU.subtract).then_inc(cen_ready, 1)
                for hg in range(HG):
                    n = HG * u + hg + 1
                    dve.wait_ge(std_ready, n)
                    dve.wait_ge(cen_ready, n)
                    chain.after(nc.vector.reciprocal(std[hg][:, :], std[hg][:, :]))
                    nc.vector.tensor_tensor(std[hg][:, :], std[hg][:, :], cen[hg][:, :], ALU.mult).then_inc(norm_ready, 1)
                bank = in_bank(dve, ("proj", u))
                dve.wait_ge(bias_added, 1)
                xs = x_res[:, TPU * u:TPU * (u + 1), :].rearrange("p i e -> p (i e)")
                nc.vector.tensor_tensor(xs, bank[:, :], xs, ALU.add).then_inc(x_done, 1)

        @block.scalar
        def _(act):
            ln.on_scalar(act)
            for u in range(UNITS):
                ln.copy(act, u)
            for u in range(UNITS):
                for hg in range(HG):
                    bank = in_bank(act, ("g", u, hg))
                    at = W_REST["bg"][0] + hg
                    nc.scalar.activation(gate[:, hg, UT * u:UT * (u + 1)], bank[:, :], ACT.Silu, bias=w[:, at:at + 1]
                                         ).then_inc(gate_ready, 1)
            for u in range(UNITS):
                bank = in_bank(act, ("kt", u))
                nc.scalar.copy(ktok[u % 2][:, :, :].rearrange("p a b -> p (a b)"), bank[:, 0:2 * P]).then_inc(ktok_ready, 1)
                for hg in range(HG):
                    act.wait_ge(o_mm, 8 * (u + 1) - (1 - hg))
                    if u > 0:
                        act.wait_ge(cen_ready, HG * (u - 1) + hg + 1)
                    nc.scalar.copy(o_sb[hg][:, :], o_bank[hg][:, :]).then_inc(o_ready, 1)
                for hg in range(HG):
                    bank = in_bank(act, ("var", u, hg))
                    if u > 0:
                        act.wait_ge(gated_ready, HG * (u - 1) + hg + 1)
                    nc.scalar.activation(std[hg][:, :], bank[:, :], ACT.Sqrt, bias=ln.eps[:, 0:1]).then_inc(std_ready, 1)

        @block.tensor
        def _(pe):
            def fill(key):
                pe.wait_ge(*read(use[key] - 4))
                return work[use[key] % 4]

            for u in range(UNITS):
                ln.turn(pe, u)
            for u in range(UNITS):
                cols = slice(UT * u, UT * (u + 1))
                pe.wait_ge(ln.xt_ready, u + 1)
                for k in ("q", "qs", "k", "ks"):
                    pe.matmul(fill((k, u))[:, :], wcol(k), ln.xt[:, cols], start=True, stop=True).then_inc(work_mm, 1)
                for half in range(2):
                    bank = fill(("v", u, half))
                    for t in range(2):
                        at = UT * u + P * (2 * half + t)
                        ins = pe.matmul(bank[:, 2 * E * t:2 * E * (t + 1)], ln.xt[:, at:at + P], wcol("v"),
                                        start=True, stop=True)
                    ins.then_inc(work_mm, 1)
                for hg in range(HG):
                    pe.matmul(fill(("g", u, hg))[:, :], wcol("gate")[:, P * hg:P * (hg + 1)], ln.xt[:, cols],
                              start=True, stop=True).then_inc(work_mm, 1)
            for u in range(UNITS):
                pe.wait_ge(rot_ready, 2 * u + 2)
                bank = fill(("kt", u))
                for b in range(2):
                    at = UT * u + SEQ * b
                    ins = pe.transpose(bank[:, P * b:P * (b + 1)], rot["k"][:, at:at + P], ln.ident)
                ins.then_inc(work_mm, 1)

                def scores(i):
                    n = 8 * u + i
                    t, hg = ITEMS[i]
                    if n >= 2:
                        pe.wait_ge(masked_ready, n - 1)
                    at = UT * u + P * t
                    pe.matmul(s_bank[n % 2][:, :].rearrange("p (h i) -> p h i", h=4), rot["k"][:, at:at + P],
                              qbd[u % 2][:, 4 * hg:4 * hg + 4, P * t:P * (t + 1)], start=True, stop=True
                              ).then_inc(s_mm, 1)

                pe.wait_ge(qbd_loaded[u % 2], 16 * RH * (u // 2 + 1))
                scores(0)
                bank = fill(("u", u))
                pe.wait_ge(ktok_ready, u + 1)
                pe.wait_ge(val_ready, 2 * u + 2)
                for b in range(2):
                    ins = pe.matmul(bank[:, 2 * E * b:2 * E * (b + 1)], ktok[u % 2][:, b, :], val[:, TPU * u + 2 * b, :],
                                    start=True, stop=True)
                ins.then_inc(work_mm, 1)
                for i, (t, hg) in enumerate(ITEMS):
                    if i + 1 < 8:
                        scores(i + 1)
                    out = o_bank[hg][:, P * t:P * (t + 1)]
                    if i < 2 and u > 0:
                        pe.wait_ge(o_ready, HG * (u - 1) + hg + 1)
                    if t % 2 == 1:
                        pe.wait_ge(kv_ready, u + 1)
                        at = UT * u + P * t
                        pe.matmul(out, kv[u % 2][:, t // 2, P * hg:P * (hg + 1)], rot["q"][:, at:at + P],
                                  start=True, stop=False)
                    pe.wait_ge(masked_ready, 8 * u + i + 1)
                    for j in range(4):
                        h = 4 * hg + j
                        ins = pe.matmul(out[32 * j:32 * j + 32, :], val[:, TPU * u + t, RV * h:RV * (h + 1)],
                                        masked[(8 * u + i) % 4][:, j, :], start=(t % 2 == 0), stop=True)
                    ins.then_inc(o_mm, 1)
                for hg in range(HG):
                    bank = fill(("mean", u, hg))
                    pe.wait_ge(o_ready, HG * u + hg + 1)
                    pe.matmul(bank[:, :], ccol("mean"), o_sb[hg][:, :], start=True, stop=True).then_inc(work_mm, 1)
                for hg in range(HG):
                    bank = fill(("var", u, hg))
                    pe.wait_ge(sq_ready, HG * u + hg + 1)
                    pe.matmul(bank[:, :], ccol("mean"), sq[hg][:, :], start=True, stop=True).then_inc(work_mm, 1)
                bank = fill(("proj", u))
                pe.wait_ge(gated_ready, HG * (u + 1))
                for t in range(TPU):
                    for hg in range(HG):
                        ins = pe.matmul(bank[:, P * t:P * (t + 1)], gated[hg][:, P * t:P * (t + 1)], wcol(f"p{hg}"),
                                        start=(hg == 0), stop=(hg == HG - 1))
                ins.then_inc(work_mm, 1)


def build(nc, ins, out):
    parts = nc.dram_tensor("scratch_parts", (2, 2, AH * 32, UT), F32, kind="Internal").ap()
    dram = dict(ins)
    dram["parts"] = [[parts[kind, which] for which in range(2)] for kind in range(2)]
    dram["o"] = nc.dram_tensor("scratch_o", (2, P, UT), F32, kind="Internal").ap()
    with ExitStack() as ctx:
        mem = {
            "x_res": ctx.enter_context(nc.sbuf_tensor("x_res", [P, TILES, E], F32)),
            "w_att": ctx.enter_context(nc.sbuf_tensor("w_att", [P, W_ATT_N], F32)),
            "w_rest": ctx.enter_context(nc.sbuf_tensor("w_rest", [P, W_REST_N], F32)),
            "const": ctx.enter_context(nc.sbuf_tensor("const", [P, CONST_N], F32)),
            "rest_loaded": ctx.enter_context(nc.semaphore("rest_loaded")),
        }
        attention_stage(nc, mem, dram, ins["x"])
        coupled_stage(nc, mem, "f0", None)
        retention_stage(nc, mem)
        coupled_stage(nc, mem, "f1", out)


def _constants():
    import numpy as np

    aux = np.zeros((2, 2, 8, UT), np.float32)
    aux[:, 0, 0:2] = 1.0
    window = np.arange(UT) % P // WIN
    for bit in range(3):
        on = (window >> bit & 1).astype(np.float32)
        aux[0, 1, 2 + 2 * bit], aux[0, 1, 3 + 2 * bit] = on, 1 - on
        aux[0, 0, 2 + 2 * bit], aux[0, 0, 3 + 2 * bit] = -FAR * (1 - on), -FAR * on

    f32 = np.float32
    pos = np.arange(SEQ, dtype=f32)
    half = E // 2
    scale_vec = (np.arange(0, E, 2, dtype=f32) + f32(0.4 * E)) / f32(1.4 * E)
    scale = scale_vec[None, :].astype(np.float64) ** (pos[:, None].astype(np.float64) / 512.0)
    inv_freq = (f32(1.0) / f32(10000.0) ** (np.arange(half, dtype=f32) / f32(half))).astype(f32)
    angle = (pos[:, None] * inv_freq[None, :]).astype(f32).astype(np.float64)
    gamma = f32(1.0) - np.exp(np.linspace(np.log(1 / 32), np.log(1 / 512), RH).astype(f32)).astype(f32)
    log_decay = np.log(gamma).astype(f32).astype(np.float64)
    decay = np.exp(log_decay[:, None, None] * np.maximum(pos[:, None] - pos[None, :], 0.0))
    norm = np.sqrt((decay * (pos[:, None] >= pos[None, :])).sum(-1))
    head = np.arange(E) // RK
    q_side = np.exp(log_decay[head][:, None] * pos[None, :]) / norm[head] * RK ** -0.5
    k_side = np.exp(-log_decay[head][:, None] * pos[None, :])
    sign = np.where(np.arange(E) % 2 == 0, -1.0, 1.0)[:, None]
    wide = lambda a: np.repeat(a, 2, axis=1).T
    const = np.zeros((P, CONST_N), np.float32)

    def put(name, a):
        at, n = CONST[name]
        const[:, at:at + n] = a

    put("ident", np.eye(P))
    put("cos_q", wide(np.cos(angle) * scale) * q_side)
    put("sin_q", wide(np.sin(angle) * scale) * q_side * sign)
    put("cos_k", wide(np.cos(angle) / scale) * k_side)
    put("sin_k", wide(np.sin(angle) / scale) * k_side * sign)
    put("heads", head[:, None] == (np.arange(2 * E) // RV)[None, :])
    put("causal", np.arange(P)[:, None] <= np.arange(P)[None, :])
    put("mean", (np.arange(P)[:, None] // RV == np.arange(P)[None, :] // RV) / RV)
    blocks = np.arange(P) // 32
    put("sign", np.where((blocks == 0) | (blocks == 3), -1.0, 1.0)[:, None])
    return aux, const


def _pack(spec, total, blocks):
    import numpy as np

    out = np.zeros((P, total), np.float32)
    for name, a in blocks.items():
        at, n = spec[name]
        a = np.asarray(a)
        out[:a.shape[0], at:at + n] = a
    return out


def kernel(**inputs):
    import numpy as np
    import concourse.bacc as _bacc
    from concourse.bass_utils import run_bass_kernel_spmd as _run

    a = {k.replace("L0_attn_a_", "a_").replace("L0_attn_b_", "r_").replace("L0_ffn_", "f_"): np.asarray(v)
         for k, v in inputs.items()}
    column = lambda v: v.reshape(-1, P).T
    down = lambda v: np.broadcast_to(v[:, None], (v.shape[0], P))
    spread = lambda v: np.broadcast_to(v[None, :], (P, v.shape[0]))
    order = np.arange(E).reshape(AG, AJ, AD)
    rows = np.concatenate([order[:3].transpose(1, 0, 2).reshape(-1), order[3].reshape(-1)])
    att = _pack(W_ATT, W_ATT_N, {
        "in_g": a["a_w_in_g"].T, "in_l": a["a_w_in_l"].T,
        "out_g": a["a_w_out_g"][:, rows], "out_l": a["a_w_out_l"][:, rows],
        "f_g": a["a_w_f"].T[:E], "f_l": a["a_w_f"].T[E:],
        "b_in_g": column(a["a_b_in_g"][:2 * E]), "b_in_l": column(a["a_b_in_l"][:2 * E]),
        "b_v_g": down(a["a_b_in_g"][2 * E:][rows]), "b_v_l": down(a["a_b_in_l"][2 * E:][rows]),
        "b_out_g": down(a["a_b_out_g"]), "b_out_l": down(a["a_b_out_l"]), "b_f": spread(a["a_b_f"])})

    swap = np.arange(E) ^ 1
    turn = (np.arange(E) + 64) % E
    w1 = a["f_cn_w1"]
    w_q, w_k, w_v = a["r_w_qkv"][:, :E], a["r_w_qkv"][:, E:2 * E], a["r_w_qkv"][:, 2 * E:]
    b_q, b_k, b_v = a["r_b_qkv"][:E], a["r_b_qkv"][E:2 * E], a["r_b_qkv"][2 * E:]
    c3 = np.zeros((P, E // 2), np.float32)
    c3[:64, :32], c3[64:, 32:] = a["f_cn_w3"], a["f_cn_w3"]
    c4 = np.zeros((64, 2 * E), np.float32)
    c4[:32, :E], c4[32:, E:] = a["f_cn_w4"], a["f_cn_w4"]
    tile = lambda v, n: np.concatenate([v] * n)[:, None]
    rest = _pack(W_REST, W_REST_N, {
        "c1": w1, "c1p": w1[turn], "c2": a["f_cn_w2"], "c3": c3, "c4r": c4,
        "b1": column(a["f_cn_b1"]), "b2": tile(a["f_cn_b2"], 2), "b3": tile(a["f_cn_b3"], 4),
        "b4": tile(a["f_cn_b4"], P), "range": tile(a["f_adaptive_range"], P),
        "g1": a["f_gc_w1"], "g2": a["f_gc_w2"], "g3r": np.broadcast_to(a["f_gc_w3"], (32, P)),
        "gb1": a["f_gc_b1"][:, None], "gb2": a["f_gc_b2"][:, None], "gb3": tile(a["f_gc_b3"], P),
        "q": w_q, "k": w_k, "qs": w_q[:, swap], "ks": w_k[:, swap], "v": w_v, "gate": a["r_w_g"],
        "p0": a["r_w_p"][:P], "p1": a["r_w_p"][P:],
        "bq": column(b_q), "bk": column(b_k), "bqs": column(b_q[swap]), "bks": column(b_k[swap]),
        "bg": column(a["r_b_g"]), "b_v": spread(b_v), "b_p": spread(a["r_b_p"])})
    aux, const = _constants()

    nc = _bacc.Bacc("TRN2", target_bir_lowering=False, num_devices=1)
    arrays = {"x": a["a_x"].reshape(TOK, E), "w_att": att, "w_rest": rest, "aux": aux, "const": const}
    ins = {n: nc.dram_tensor("in_" + n, v.shape, F32, kind="ExternalInput").ap() for n, v in arrays.items()}
    out = nc.dram_tensor("out_0", (TOK, E), F32, kind="ExternalOutput").ap()
    build(nc, ins, out)
    r = _run(nc, [{"in_" + n: np.ascontiguousarray(v) for n, v in arrays.items()}], core_ids=[0])
    return np.asarray(r.results[0]["out_0"]).reshape(a["a_x"].shape)
```

```python
from contextlib import ExitStack

import concourse.bass as bass
from concourse import mybir

F32 = mybir.dt.float32
F32R = mybir.dt.float32r
ALU = mybir.AluOpType
ACT = mybir.ActivationFunctionType
AX_X = mybir.AxisListType.X

P = 128
BATCH, SEQ, E = 8, 256, 128
TOK = BATCH * SEQ
TILES = TOK // P
UT = 512
UNITS = TOK // UT
TPU = UT // P
EPS = 1e-5

AH, AD = 16, 8
AG, AJ = 4, 4
WIN = 16
A_SCALE = float(AD) ** -0.5
FAR = 2.0 ** 100

RH, RK, RV = 8, 16, 32


def columns(spec):
    at, out = 0, {}
    for name, width in spec:
        out[name] = (at, width)
        at += width
    return out, at


W_ATT, W_ATT_N = columns([
    ("in_l", 3 * E), ("in_g", 3 * E), ("b_in_l", 2), ("b_in_g", 2),
    ("out_g", E), ("out_l", E), ("f_g", E), ("f_l", E), ("b_v_g", P), ("b_v_l", P), ("b_out_g", P), ("b_out_l", P), ("b_f", E)])
W_REST, W_REST_N = columns([
    ("c1", E), ("c1p", E), ("c2", E // 2), ("c3", E // 2), ("c4r", 2 * E),
    ("b1", 1), ("b2", 1), ("b3", 1), ("b4", 1), ("range", 1),
    ("g1", E // 2), ("g2", E // 4), ("g3r", E), ("gb1", 1), ("gb2", 1), ("gb3", 1),
    ("q", E), ("k", E), ("qs", E), ("ks", E), ("vt", 2 * E), ("gate", 2 * E), ("p0", E), ("p1", E),
    ("bq", 1), ("bk", 1), ("bqs", 1), ("bks", 1), ("bg", 2), ("b_v", 2 * E), ("b_p", E)])
CONST, CONST_N = columns([
    ("ident", P), ("cos_q", SEQ), ("sin_q", SEQ), ("cos_k", SEQ), ("sin_k", SEQ),
    ("heads", 2 * E), ("causal", P), ("mean", 32), ("spread", 4 * P), ("centre", P), ("sign", 1)])


class Chain:

    def __init__(self, eng, sem):
        self.eng, self.sem, self.n = eng, sem, 0

    def after(self, ins):
        self.n += 1
        ins.then_inc(self.sem, 1)
        self.eng.wait_ge(self.sem, self.n)


def layernorm_buffers(nc, ctx):
    sb = lambda name, shape: ctx.enter_context(nc.sbuf_tensor(f"ln_{name}", shape, F32))
    return {"xn": sb("xn", [P, TILES, E]), "xt": sb("xt", [P, TOK]), "stats": sb("stats", [P, TILES, 6]),
            "mv": sb("mv", [P, TILES, 2]), "std": sb("std", [P, TILES]), "rstd": sb("rstd", [P, TILES]),
            "shift": sb("shift", [P, TILES]),
            "eps": sb("eps", [P, 1])}


class LayerNorm:

    def __init__(self, nc, ctx, mem, tag):
        def sem(name):
            return ctx.enter_context(nc.semaphore(f"{tag}_{name}"))

        self.nc, self.x_res, self.bank = nc, mem["x_res"], None
        self.ident = mem["const"][:, CONST["ident"][0]:CONST["ident"][0] + P]
        ln = mem["ln"]
        self.xn, self.xt, self.stats, self.mv = ln["xn"], ln["xt"], ln["stats"], ln["mv"]
        self.std, self.rstd, self.shift, self.eps = ln["std"], ln["rstd"], ln["shift"], ln["eps"]
        self.var_ready = sem("var_ready")
        self.std_ready = sem("std_ready")
        self.rstd_ready = sem("rstd_ready")
        self.xn_ready = sem("xn_ready")
        self.turned = sem("turned")
        self.xt_ready = sem("xt_ready")

    def statistics(self, chain, u):
        nc = self.nc
        for i in range(TPU * u, TPU * (u + 1)):
            last = nc.vector.bn_stats(self.stats[:, i, :], self.x_res[:, i, :])
        chain.after(last)
        for i in range(TPU * u, TPU * (u + 1)):
            last = nc.vector.bn_aggr(self.mv[:, i, :], self.stats[:, i, :])
        last.then_inc(self.var_ready, 1)

    def reciprocals(self, dve, chain, u):
        nc = self.nc
        tiles = slice(TPU * u, TPU * (u + 1))
        dve.wait_ge(self.std_ready, u + 1)
        chain.after(nc.vector.reciprocal(self.rstd[:, tiles], self.std[:, tiles]))
        nc.vector.scalar_tensor_tensor(out=self.shift[:, tiles], in0=self.mv[:, tiles, 0], scalar=-1.0,
                                       in1=self.rstd[:, tiles], op0=ALU.mult, op1=ALU.mult
                                       ).then_inc(self.rstd_ready, 1)

    def normalise(self, act, u):
        act.wait_ge(self.rstd_ready, u + 1)
        for i in range(TPU * u, TPU * (u + 1)):
            self.nc.scalar.activation(self.xn[:, i, :], self.x_res[:, i, :], ACT.Identity,
                                      scale=self.rstd[:, i:i + 1], bias=self.shift[:, i:i + 1]
                                      ).then_inc(self.xn_ready, 1)

    def normalise_on_vector(self, dve, chain, u):
        nc = self.nc
        tiles = slice(TPU * u, TPU * (u + 1))
        dve.wait_ge(self.std_ready, u + 1)
        chain.after(nc.vector.reciprocal(self.rstd[:, tiles], self.std[:, tiles]))
        for i in range(TPU * u, TPU * (u + 1)):
            nc.vector.tensor_scalar(self.xn[:, i, :], self.x_res[:, i, :], self.mv[:, i, 0:1],
                                    self.rstd[:, i:i + 1], ALU.subtract, ALU.mult).then_inc(self.xn_ready, 1)

    def deviation(self, act, u):
        tiles = slice(TPU * u, TPU * (u + 1))
        act.wait_ge(self.var_ready, u + 1)
        self.nc.scalar.activation(self.std[:, tiles], self.mv[:, tiles, 1], ACT.Sqrt, bias=self.eps[:, 0:1]
                                  ).then_inc(self.std_ready, 1)

    def turn(self, pe, u):
        pe.wait_ge(self.xn_ready, TPU * (u + 1))
        for t in range(TPU):
            ins = pe.transpose(self.bank(u)[:, P * t:P * (t + 1)], self.xn[:, TPU * u + t, :], self.ident)
        ins.then_inc(self.turned, 1)

    def copy(self, act, u):
        act.wait_ge(self.turned, u + 1)
        self.nc.scalar.copy(self.xt[:, UT * u:UT * (u + 1)], self.bank(u)[:, :]).then_inc(self.xt_ready, 1)


KINDS = "lg"
A_UNITS = 2 * UNITS
BATCHES = TOK // SEQ
HALVES = 2 * BATCHES
HT = UT // 2


EARLY = ("proj",)


def unit_of(v):
    return 2 * (v // 4) + v % 2


def kind_of(v):
    return KINDS[v % 2]


def attention_events():
    chunks = [8 if kind_of(v) == "g" else 4 for v in range(HALVES)]
    banks = [16 if kind_of(v) == "g" else 8 for v in range(HALVES)]
    maxima = lambda v: [("max", v, n) for n in range(banks[v])]
    more = {}
    add = lambda v, c, *ev: more.setdefault((v, c), []).extend(ev)
    for p in range(1, UNITS):
        add(p - 1, 0, ("normalise", p), ("xt", p))
        for n, part in enumerate("kqv"):
            add(4 * (p - 1), 1 + n, ("proj", 2 * p, part))
            add(4 * (p - 1) + 1, 3 + n, ("proj", 2 * p + 1, part))
    add(1, 4, ("weights",))
    add(3, 2, ("biases",))
    for v in range(HALVES):
        add(v + 1, 1, ("evac", v))
    for b in range(BATCHES):
        add(2 * b + 2, 1, ("o_store", b))
        add(2 * b + 2, 3, ("o_load", b))
        add(2 * b + 3, 2, ("r_store", b))
        add(2 * b + 3, 4, ("r_load", b))
        add(2 * b + 3, 6, ("scale", b))
        add(2 * b + 4, 2, ("fuse", b))

    ev = [("xt", 0)] + [("proj", 0, part) for part in "kqv"] + [("load", 0)]
    ev += [("proj", 1, part) for part in "kqv"] + [("load", 1), ("load", 2)]
    ev += maxima(0) + [("minus", 0), ("shift", 0)] + maxima(1) + [("minus", 1), ("shift", 1)]
    for v in range(HALVES):
        spread = maxima(v + 2) if v + 2 < HALVES else []
        if v + 3 < HALVES:
            ev.append(("load", v + 3))
        ev += [("st", v, 0, 0), ("st", v, 0, 1)]
        for c in range(chunks[v]):
            ev += [("exp", v, c, 0), ("exp", v, c, 1)]
            ahead = spread[c * len(spread) // chunks[v]:(c + 1) * len(spread) // chunks[v]]
            if c + 1 < chunks[v]:
                ahead = ahead[:1] + [("st", v, c + 1, 0)] + ahead[1:] + [("st", v, c + 1, 1)]
            ev += ahead
            extra = more.pop((v, c), [])
            ev += [e for e in extra if e[0] in EARLY]
            ev.append(("pv", v, c))
            ev += [e for e in extra if e[0] not in EARLY]
        if spread:
            ev.append(("minus", v + 2))
            more.setdefault((v + 1, 0), []).insert(0, ("shift", v + 2))
    tail = [ev_ for key in sorted(more) for ev_ in more[key]]
    last = UNITS - 1
    early = [("next_stats", p) for p in range(last)] + [("next_norm", p) for p in range(last)]
    early += [("next_xt", p) for p in range(last)]
    at = tail.index(("evac", HALVES - 1)) + 1
    ev += tail[:at] + early + tail[at:] + [("next_stats", last), ("next_norm", last), ("next_xt", last)]
    return ev, chunks, banks


def attention_stage(nc, mem, dram, x_in, ln, ln_next):
    events, chunks, banks = attention_events()
    first_chunk = [sum(chunks[:v]) for v in range(HALVES + 1)]
    first_bank = [sum(banks[:v]) for v in range(HALVES + 1)]

    keys = []
    for e in events:
        if e[0] == "weights":
            keys += [("w", "g"), ("w", "l"), ("bias",)]
        elif e[0] in ("xt", "proj", "max", "shift", "fuse", "next_xt"):
            keys.append(e)
    use = {key: n for n, key in enumerate(keys)}
    mine = [key for key in keys if key[0] not in ("xt", "next_xt")]
    filled = {key: n + 1 for n, key in enumerate(mine)}

    with ExitStack() as ctx:
        def sb(name, shape, dt=F32):
            return ctx.enter_context(nc.sbuf_tensor(name, shape, dt))

        def ps(name, shape):
            return ctx.enter_context(nc.psum_tensor(name, shape, F32))

        def sem(name):
            return ctx.enter_context(nc.semaphore(name))

        x_res, wa, const = mem["x_res"], mem["w_att"], mem["const"]
        qbd = [sb(f"a_qbd{i}", [P, AG, AJ, UT], F32R) for i in range(2)]
        kst = [sb(f"a_kst{i}", [P, AG, UT], F32R) for i in range(2)]
        vx = [sb(f"a_vx{i}", [P, TPU, AH, 32]) for i in range(4)]
        probs = [sb(f"a_probs{i}", [P, 1024]) for i in range(4)]
        hi = {k: sb(f"a_{k}hi", [P, UT], F32R) for k in "kq"}
        lo = {k: sb(f"a_{k}lo", [P, UT], F32R) for k in "kq"}
        mx = sb("a_mx", [P, 2 * AJ, AG])
        ml = sb("a_ml", [P, 2 * AJ, 2, AG], F32R)
        mrow = sb("a_mrow", [32, HT], F32R)
        o_raw = sb("a_o_raw", [P, 2, UT])
        o_val = sb("a_o_val", [P, UT])
        den = sb("a_den", [P, AH * UT // P])
        rec = sb("a_rec", [P, AH * UT // P])
        o_rec = sb("a_o_rec", [P, UT])
        o_nrm = [sb(f"a_o_nrm{i}", [P, UT]) for i in range(2)]
        w_out = {k: sb(f"a_w_out_{k}", [P, E]) for k in KINDS}
        bias = sb("a_bias", [P, E])

        st = [ps(f"a_st{i}", [P, 512]) for i in range(3)]
        work = [ps(f"a_work{i}", [P, 512]) for i in range(3)]
        pv_bank = [ps(f"a_pv{i}", [P, 512]) for i in range(2)]
        ln.bank = lambda u: work[use[("xt", u)] % 3]
        ln_next.bank = lambda u: work[use[("next_xt", u)] % 3]
        xt = ln.xt

        x_loaded = [sem(f"x_loaded{p}") for p in range(UNITS)]
        ident_loaded, w_loaded, w_out_loaded, aux_set = (
            sem(n) for n in ("ident_loaded", "w_loaded", "w_out_loaded", "aux_set"))
        eps_set = sem("eps_set")
        zeroed = sem("zeroed")
        zeroed_too = sem("zeroed_too")
        w_ready = sem("w_ready")
        bias_ready = sem("bias_ready")
        bias_added = sem("bias_added")
        work_mm = sem("work_mm")
        max_done = sem("max_done")
        hi_ready, lo_ready = sem("hi_ready"), sem("lo_ready")
        parts_stored = sem("parts_stored")
        qk_loaded = [sem(f"qk_loaded{i}") for i in range(4)]
        v_ready = sem("v_ready")
        ml_ready = sem("ml_ready")
        mrow_ready = sem("mrow_ready")
        mrow_placed = sem("mrow_placed")
        st_ready = sem("st_ready")
        probs_ready = sem("probs_ready")
        pv_done = sem("pv_done")
        o_evacuated = sem("o_evacuated")
        o_stored, r_stored = sem("o_stored"), sem("r_stored")
        val_loaded, den_loaded, rec_loaded = sem("val_loaded"), sem("den_loaded"), sem("rec_loaded")
        rec_ready = sem("rec_ready")
        o_scaled = sem("o_scaled")
        x_done = sem("x_done")
        dve_chain, pool_chain = sem("a_dve_chain"), sem("a_pool_chain")

        block = ctx.enter_context(nc.Block())
        col = lambda name: slice(W_ATT[name][0], sum(W_ATT[name]))

        def in_bank(eng, key):
            eng.wait_ge(work_mm, filled[key])
            return work[use[key] % 3]

        def read(key):
            kind = key[0]
            if kind == "proj":
                _, u, part = key
                return {"k": (lo_ready, 2 * u + 1), "q": (lo_ready, 2 * u + 2), "v": (v_ready, u + 1)}[part]
            if kind == "w":
                return w_ready, 1 + "gl".index(key[1])
            if kind == "bias":
                return bias_ready, 1
            if kind == "max":
                return max_done, first_bank[key[1]] + key[2] + 1
            return {"xt": ln.xt_ready, "next_xt": ln_next.xt_ready, "shift": mrow_ready, "fuse": x_done}[kind], key[1] + 1

        def max_step(v, n):
            if kind_of(v) == "g":
                return n // 8, n % 8 // 2, 2 * (n % 2), 2
            return n // AG, n % AG, 0, 4

        @block.sync
        def _(sp):
            x_tiles = x_in.rearrange("(i p) e -> p i e", p=P)
            load_x = lambda p: sp.dma_start(x_res[:, TPU * p:TPU * (p + 1), :], x_tiles[:, TPU * p:TPU * (p + 1), :]
                                            ).then_inc(x_loaded[p], 16)
            load_x(0)
            sp.dma_start(const[:, 0:P], dram["const"][:, 0:P]).then_inc(ident_loaded, 16)
            first = W_ATT["out_g"][0]
            sp.dma_start(wa[:, 0:first], dram["w_att"][:, 0:first]).then_inc(w_loaded, 16)
            for p in range(1, UNITS):
                load_x(p)
            for kind in range(2):
                for which in range(2):
                    dst = dram["parts"][kind][which].rearrange("(h r) t -> h r t", r=32)[:, 24:32, :]
                    src = dram["aux"][kind, which]
                    sp.dma_start(dst, bass.AP(src.tensor, src.offset, [[0, AH], [UT, 8], [1, UT]])
                                 ).then_inc(aux_set, 16)
            for e in events:
                if e[0] == "proj" and e[2] != "v":
                    _, u, k = e
                    n = "kq".index(k)
                    if u >= 2 and n == 0:
                        for b in range(2):
                            sp.wait_ge(qk_loaded[2 * b + u % 2], 80 * (u // 2))
                    sp.wait_ge(hi_ready, 2 * u + n + 1)
                    sp.wait_ge(lo_ready, 2 * u + n + 1)
                    scratch = dram["parts"][u % 2][n].rearrange("(h r) t -> h r t", r=32)
                    for part, r in zip((("hi", "lo", "hi"), ("hi", "hi", "lo"))[n], range(3)):
                        src = (hi if part == "hi" else lo)[k]
                        sp.dma_start(scratch[:, 8 * r:8 * r + 8, :], src[:, :].bitcast(F32)
                                     ).then_inc(parts_stored, 16)
                elif e[0] == "load":
                    v = e[1]
                    u, b = unit_of(v), v // 2 % 2
                    cols = slice(HT * b, HT * (b + 1))
                    sp.wait_ge(parts_stored, 96 * (u + 1))
                    if v < 4:
                        sp.wait_ge(aux_set, 64)
                        sp.wait_ge(zeroed, 2 if u else 1)
                        sp.wait_ge(zeroed_too, 1)
                    else:
                        sp.wait_ge(st_ready, 2 * first_chunk[v - 3])
                    sp.dma_start(kst[u % 2][:, :, cols].bitcast(F32),
                                 dram["parts"][u % 2][0].rearrange("(g p) t -> p g t", p=P)[:, :, cols]
                                 ).then_inc(qk_loaded[v % 4], 16)
                    queries = dram["parts"][u % 2][1].rearrange("(g j r) t -> j r g t", g=AG, j=AJ)
                    for j in range(AJ):
                        sp.dma_start(qbd[u % 2][32 * j:32 * j + 32, :, j, cols].bitcast(F32),
                                     queries[j][:, :, cols]).then_inc(qk_loaded[v % 4], 16)
                    if v == 2:
                        sp.dma_start(wa[:, first:], dram["w_att"][:, first:]).then_inc(w_out_loaded, 16)
                        sp.dma_start(const[:, P:], dram["const"][:, P:]).then_inc(mem["rest_loaded"], 16)
                        sp.dma_start(mem["w_rest"][:, :], dram["w_rest"]).then_inc(mem["rest_loaded"], 16)
                elif e[0] == "shift":
                    v = e[1]
                    cols = slice(HT * (v // 2 % 2), HT * (v // 2 % 2 + 1))
                    sp.wait_ge(mrow_ready, v + 1)
                    for j in range(AJ):
                        sp.dma_start(qbd[v % 2][32 * j + 24:32 * j + 26, :, j, cols].bitcast(F32),
                                     mrow[8 * j:8 * j + 8, :].bitcast(F32)).then_inc(mrow_placed, 16)
                elif e[0] == "o_store":
                    b = e[1]
                    sp.wait_ge(o_evacuated, 2 * b + 2)
                    if b >= 1:
                        sp.wait_ge(val_loaded, 32 * b)
                        sp.wait_ge(den_loaded, 32 * b)
                    sp.dma_start(dram["o"].rearrange("a p t -> p a t"), o_raw[:, :, :]).then_inc(o_stored, 16)
                elif e[0] == "o_load":
                    b = e[1]
                    sp.wait_ge(o_stored, 16 * (b + 1))
                    if b >= 1:
                        sp.wait_ge(o_scaled, b)
                    o, part = dram["o"].tensor, UT // 8
                    for dst, at, rows in ((den[0:96, :], 24 * UT, [[32 * UT, AJ], [UT, 3], [1, UT]]),
                                          (den[96:P, :], (P + 27) * UT, [[32 * UT, AJ], [part, 8], [1, part]])):
                        sp.dma_start(dst, bass.AP(o, at, rows)).then_inc(den_loaded, 16)
                    for dst, at, n in ((o_val[0:96, :], 0, 24), (o_val[96:P, :], P * UT, 8)):
                        sp.dma_start(dst, bass.AP(o, at, [[32 * UT, AJ], [UT, n], [1, UT]])).then_inc(val_loaded, 16)
                elif e[0] == "r_store":
                    b = e[1]
                    sp.wait_ge(rec_ready, b + 1)
                    if b >= 1:
                        sp.wait_ge(rec_loaded, 16 * b)
                    sp.dma_start(dram["r"], rec[:, :]).then_inc(r_stored, 16)
                elif e[0] == "r_load":
                    b = e[1]
                    sp.wait_ge(r_stored, 16 * (b + 1))
                    sp.dma_start(o_rec[:, :], bass.AP(dram["r"].tensor, 0, [[UT, AH], [0, 8], [1, UT]])
                                 ).then_inc(rec_loaded, 16)

        @block.gpsimd
        def _(pool):
            nc.gpsimd.memset(ln.eps[:, :], EPS).then_inc(eps_set, 1)
            nc.gpsimd.memset(qbd[0][:, 2:4, :, :].bitcast(F32), 0.0).then_inc(zeroed, 1)
            nc.gpsimd.memset(qbd[1][:, :, :, :].bitcast(F32), 0.0).then_inc(zeroed, 1)
            for i in range(4):
                nc.gpsimd.memset(vx[i][:, :, :, :], 0.0).then_inc(pool_chain, 1)
                pool.wait_ge(pool_chain, 1 + i)
                for g in range(AG):
                    last = nc.gpsimd.memset(vx[i][:, :, 4 * g:4 * g + 4, 24 + g], 1.0)
                last.then_inc(zeroed, 1)
            for e in events:
                if e[0] == "biases":
                    pool.wait_ge(bias_ready, 1)
                    pool.wait_ge(ln.xn_ready, TILES)
                    for i in range(TILES):
                        ins = nc.gpsimd.tensor_tensor(x_res[:, i, :], x_res[:, i, :], bias[:, :], ALU.add)
                    ins.then_inc(bias_added, 1)
                elif e[0] == "scale":
                    b = e[1]
                    pool.wait_ge(val_loaded, 32 * (b + 1))
                    pool.wait_ge(rec_loaded, 16 * (b + 1))
                    if b >= 2:
                        pool.wait_ge(work_mm, filled[("fuse", b - 2)])
                    nc.gpsimd.tensor_tensor(o_nrm[b % 2][:, :], o_val[:, :], o_rec[:, :], ALU.mult
                                            ).then_inc(o_scaled, 1)

        @block.vector
        def _(dve):
            chain = Chain(dve, dve_chain)
            nc.vector.memset(qbd[0][:, 0:2, :, :].bitcast(F32), 0.0).then_inc(zeroed_too, 1)
            for p in range(UNITS):
                dve.wait_ge(x_loaded[p], 16)
                ln.statistics(chain, p)
                if p == 1:
                    ln.normalise_on_vector(dve, chain, 0)
            for e in events:
                if e[0] == "normalise":
                    ln.normalise_on_vector(dve, chain, e[1])
                elif e[0] == "next_stats":
                    dve.wait_ge(x_done, 2 * e[1] + 2)
                    ln_next.statistics(chain, e[1])
                elif e[0] == "next_norm":
                    ln_next.normalise_on_vector(dve, chain, e[1])
                elif e[0] == "proj" and e[2] != "v":
                    _, u, k = e
                    bank = in_bank(dve, e)
                    dve.wait_ge(hi_ready, 2 * u + "kq".index(k) + 1)
                    if u >= 1:
                        dve.wait_ge(parts_stored, 96 * u)
                    at = W_ATT["b_in_" + kind_of(u)][0] + (1 if k == "k" else 0)
                    nc.vector.scalar_tensor_tensor(
                        out=lo[k][:, :], in0=bank[:, :], scalar=wa[:, at:at + 1],
                        in1=hi[k][:, :].bitcast(F32), op0=ALU.add, op1=ALU.subtract).then_inc(lo_ready, 1)
                elif e[0] == "weights":
                    bank = in_bank(dve, ("bias",))
                    dve.wait_ge(w_out_loaded, 16)
                    nc.vector.tensor_tensor(bias[:, :], bank[:, 0:E], wa[:, col("b_f")], ALU.add).then_inc(bias_ready, 1)
                elif e[0] == "max":
                    _, v, n = e
                    bank = in_bank(dve, e)
                    qt, g, j, heads = max_step(v, n)
                    nc.vector.tensor_reduce(mx[:, AJ * qt + j:AJ * qt + j + heads, g],
                                            bank[:, :].rearrange("p (h k) -> p h k", h=heads), AX_X, ALU.max
                                            ).then_inc(max_done, 1)
                elif e[0] == "minus":
                    v = e[1]
                    dve.wait_ge(max_done, first_bank[v + 1])
                    if v >= 1:
                        dve.wait_ge(mrow_ready, v)
                    chain.after(nc.vector.tensor_scalar(ml[:, :, 0, :], mx[:, :, :], -1.0, None, ALU.mult))
                    nc.vector.scalar_tensor_tensor(out=ml[:, :, 1, :], in0=mx[:, :, :], scalar=-1.0,
                                                   in1=ml[:, :, 0, :].bitcast(F32), op0=ALU.mult,
                                                   op1=ALU.subtract).then_inc(ml_ready, 1)
                    dve.wait_ge(ml_ready, v + 1)
                elif e[0] == "r_store":
                    b = e[1]
                    dve.wait_ge(den_loaded, 32 * (b + 1))
                    if b >= 1:
                        dve.wait_ge(r_stored, 16 * b)
                    nc.vector.reciprocal(rec[:, :], den[:, :]).then_inc(rec_ready, 1)
                elif e[0] == "fuse":
                    b = e[1]
                    bank = in_bank(dve, e)
                    dve.wait_ge(bias_added, 1)
                    xs = x_res[:, 2 * b:2 * b + 2, :].rearrange("p i e -> p (i e)")
                    nc.vector.tensor_tensor(xs, bank[:, 0:SEQ], xs, ALU.add).then_inc(x_done, 1)

        @block.scalar
        def _(act):
            act.wait_ge(eps_set, 1)
            for u in range(UNITS):
                ln.deviation(act, u)
            for e in events:
                if e[0] == "xt":
                    ln.copy(act, e[1])
                elif e[0] == "next_norm":
                    ln_next.deviation(act, e[1])
                elif e[0] == "next_xt":
                    ln_next.copy(act, e[1])
                elif e[0] == "proj" and e[2] != "v":
                    _, u, k = e
                    bank = in_bank(act, e)
                    if u == 0:
                        act.wait_ge(w_loaded, 16)
                    else:
                        act.wait_ge(parts_stored, 96 * u)
                        act.wait_ge(lo_ready, 2 * u)
                    at = W_ATT["b_in_" + kind_of(u)][0] + (1 if k == "k" else 0)
                    nc.scalar.activation(hi[k][:, :], bank[:, :], ACT.Identity, bias=wa[:, at:at + 1]
                                         ).then_inc(hi_ready, 1)
                elif e[0] == "proj":
                    u = e[1]
                    bank = in_bank(act, e)
                    act.wait_ge(zeroed, 3 + u % 4)
                    if u >= 4:
                        act.wait_ge(pv_done, first_chunk[4 * (u // 2 - 2) + 2 + u % 2 + 1])
                    for g in range(AG):
                        off = 8 * (g % 3)
                        ins = nc.scalar.copy(
                            vx[u % 4][:, :, 4 * g:4 * g + 4, off:off + 8],
                            bank[:, :].rearrange("p (t g j d) -> p t g j d", t=TPU, g=AG, j=AJ)[:, :, g, :, :])
                    ins.then_inc(v_ready, 1)
                elif e[0] == "weights":
                    for n, k in enumerate("gl"):
                        bank = in_bank(act, ("w", k))
                        nc.scalar.copy(w_out[k][:, :], bank[:, 0:E]).then_inc(w_ready, 1)
                elif e[0] == "shift":
                    v = e[1]
                    bank = in_bank(act, e)
                    if v >= 1:
                        act.wait_ge(mrow_placed, 64 * v)
                    nc.scalar.copy(mrow[:, :], bank[0:32, 0:HT]).then_inc(mrow_ready, 1)
                elif e[0] == "exp":
                    _, v, c, half = e
                    n = first_chunk[v] + c
                    m = 2 * n + half
                    act.wait_ge(st_ready, m + 1)
                    if n >= 4:
                        act.wait_ge(pv_done, n - 3)
                    nc.scalar.activation(probs[n % 4][:, 512 * half:512 * (half + 1)], st[m % 3][:, :],
                                         ACT.Exp, scale=A_SCALE).then_inc(probs_ready, 1)
                elif e[0] == "evac":
                    v = e[1]
                    at = HT * (v % 2)
                    act.wait_ge(pv_done, first_chunk[v + 1])
                    if v >= 2:
                        act.wait_ge(o_stored, 16 * (v // 2))
                    nc.scalar.copy(o_raw[:, :, at:at + HT], pv_bank[v % 2][:, :].rearrange("p (a t) -> p a t", a=2)
                                   ).then_inc(o_evacuated, 1)

        @block.tensor
        def _(pe):
            def fill(key):
                n = use[key]
                if n >= 3:
                    pe.wait_ge(*read(keys[n - 3]))
                return work[n % 3]

            def scores(v, c, half):
                u, b = unit_of(v), v // 2 % 2
                m = 2 * (first_chunk[v] + c) + half
                if c == 0 and half == 0:
                    pe.wait_ge(mrow_placed, 64 * (v + 1))
                if m >= 3:
                    pe.wait_ge(probs_ready, m - 2)
                q, k, out = qbd[u % 2], kst[u % 2], st[m % 3]
                if kind_of(v) == "g":
                    g, kt = c // 2, c % 2
                    at = HT * b + P * kt
                    pairs = q[:, g, 2 * half:2 * half + 2, HT * b:HT * (b + 1)]
                    ins = pe.matmul(out[:, :].rearrange("p (j q) -> p j q", j=2), k[:, g, at:at + P], pairs,
                                    start=True, stop=True)
                else:
                    g, at = 2 * (c % 2) + half, HT * b + P * (c // 2)
                    ins = pe.matmul(out[:, :].rearrange("p (j q) -> p j q", j=4), k[:, g, at:at + P],
                                    q[:, g, :, at:at + P], start=True, stop=True)
                ins.then_inc(st_ready, 1)

            def outputs(v, c):
                u, b = unit_of(v), v // 2 % 2
                n = first_chunk[v] + c
                pe.wait_ge(probs_ready, 2 * n + 2)
                if c == 0:
                    pe.wait_ge(v_ready, u + 1)
                    if v >= 2:
                        pe.wait_ge(o_evacuated, v - 1)
                pr, val = probs[n % 4], vx[u % 4]
                if kind_of(u) == "g":
                    g, kt = c // 2, c % 2
                    for j in range(AJ):
                        ins = pe.matmul(pv_bank[1][32 * j:32 * j + 32, HT * (g // 3):HT * (g // 3 + 1)],
                                        val[:, 2 * b + kt, 4 * g + j, :], pr[:, HT * j:HT * (j + 1)],
                                        start=(kt == 0 and g in (0, 3)), stop=(kt == 1 and g in (2, 3)))
                else:
                    t = 2 * b + c // 2
                    for half in range(2):
                        g = 2 * (c % 2) + half
                        out = HT * (g // 3) + P * (c // 2)
                        for j in range(AJ):
                            at = 512 * half + P * j
                            ins = pe.matmul(pv_bank[0][32 * j:32 * j + 32, out:out + P],
                                            val[:, t, 4 * g + j, :], pr[:, at:at + P],
                                            start=(g in (0, 3)), stop=(g in (2, 3)))
                ins.then_inc(pv_done, 1)

            pe.wait_ge(ident_loaded, 16)
            for e in events:
                if e[0] == "xt":
                    fill(e)
                    ln.turn(pe, e[1])
                elif e[0] == "next_xt":
                    fill(e)
                    ln_next.turn(pe, e[1])
                elif e[0] == "proj":
                    _, u, part = e
                    at = W_ATT["in_" + kind_of(u)][0] + E * "qkv".index(part)
                    pe.wait_ge(w_loaded, 16)
                    pe.wait_ge(ln.xt_ready, u // 2 + 1)
                    first = UT * (u // 2)
                    bank = fill(e)
                    if part == "v":
                        for t in range(TPU):
                            ins = pe.matmul(bank[:, P * t:P * (t + 1)], xt[:, first + P * t:first + P * (t + 1)],
                                            wa[:, at:at + E], start=True, stop=True)
                    else:
                        ins = pe.matmul(bank[:, :], wa[:, at:at + E], xt[:, first:first + UT], start=True, stop=True)
                    ins.then_inc(work_mm, 1)
                elif e[0] == "weights":
                    pe.wait_ge(w_out_loaded, 16)
                    for k in "gl":
                        bank = fill(("w", k))
                        pe.matmul(bank[:, 0:E], wa[:, col("out_" + k)], wa[:, col("f_" + k)], start=True, stop=True
                                  ).then_inc(work_mm, 1)
                    bank = fill(("bias",))
                    pe.wait_ge(w_ready, 2)
                    for n, k in enumerate("gl"):
                        pe.matmul(bank[:, 0:E], wa[:, col("b_out_" + k)], wa[:, col("f_" + k)],
                                  start=(n == 0), stop=False)
                        ins = pe.matmul(bank[:, 0:E], wa[:, col("b_v_" + k)], w_out[k][:, :],
                                        start=False, stop=(n == 1))
                    ins.then_inc(work_mm, 1)
                elif e[0] == "max":
                    _, v, n = e
                    u, b = unit_of(v), v // 2 % 2
                    bank = fill(e)
                    if n == 0:
                        pe.wait_ge(qk_loaded[v % 4], 80 * (v // 4 + 1))
                    q, k = qbd[u % 2], kst[u % 2]
                    qt, g, j, heads = max_step(v, n)
                    at = HT * b + P * qt
                    own = slice(HT * b, HT * (b + 1)) if kind_of(u) == "g" else slice(at, at + P)
                    width = 512 // heads
                    for i in range(heads):
                        ins = pe.matmul(bank[:, width * i:width * (i + 1)], q[:, g, j + i, at:at + P], k[:, g, own],
                                        start=True, stop=True)
                    ins.then_inc(work_mm, 1)
                elif e[0] == "shift":
                    v = e[1]
                    bank = fill(e)
                    pe.wait_ge(ml_ready, v + 1)
                    for t in range(2):
                        src = ml[:, AJ * t:AJ * (t + 1), :, :].rearrange("p j r g -> p (j r g)").bitcast(F32)
                        ins = pe.transpose(bank[0:32, P * t:P * (t + 1)], src, ln.ident)
                    ins.then_inc(work_mm, 1)
                elif e[0] == "st":
                    scores(e[1], e[2], e[3])
                elif e[0] == "pv":
                    outputs(e[1], e[2])
                elif e[0] == "fuse":
                    b = e[1]
                    bank = fill(e)
                    pe.wait_ge(o_scaled, b + 1)
                    for t in range(2):
                        for i, k in enumerate(KINDS):
                            at = HT * i + P * t
                            ins = pe.matmul(bank[:, P * t:P * (t + 1)], o_nrm[b % 2][:, at:at + P],
                                            w_out[k][:, :], start=(i == 0), stop=(i == 1))
                    ins.then_inc(work_mm, 1)


CYCLES, PAIRS = 3, UNITS // 2
FILL = 128


def coupled_events():
    def slot(i, n, k, m):
        c, d = 2 * k, 2 * k + 1
        first, second = 0 <= n < CYCLES, 0 <= m < CYCLES
        ev = []
        ev += [("g3", k, m), ("z", c, m)] if second else []
        ev += [("g1", 2 * i, n), ("g1", 2 * i + 1, n)] if first and n > 0 else []
        ev += [("z", d, m), ("tanh", c, m), ("c", c, m)] if second else []
        ev += [("l2", i, n)] if first else []
        ev += [("tanh", d, m), ("c", d, m)] if second else []
        ev += [("g2", i, n), ("l3", i, n)] if first else []
        return ev

    ev = [("ab", 0), ("g1", 0, 0), ("glob", 0), ("ab", 1), ("g1", 1, 0), ("glob", 1), ("ab", 2), ("glob", 2),
          ("l2", 0, 0), ("ab", 3), ("g2", 0, 0), ("g1", 2, 0), ("l3", 0, 0), ("g1", 3, 0)]
    for n in range(CYCLES - 1):
        ev += slot(1, n, 0, n) + slot(0, n + 1, 1, n)
    ev += [("twist",)] + slot(1, CYCLES - 1, 0, CYCLES - 1)
    last = slot(None, CYCLES, 1, CYCLES - 1)
    ev += last[:3] + [("turn", 0)] + last[3:] + [("turn", 1), ("poly", 0), ("alpha", 0), ("alpha", 1)]
    ev += [("beta", 0), ("beta", 1), ("add", 0), ("add", 1), ("poly", 1), ("alpha", 2), ("alpha", 3), ("stats", 0), ("stats", 1),
           ("beta", 2), ("norm", 0), ("add", 2), ("beta", 3), ("norm", 1), ("add", 3), ("xt", 0), ("xt", 1),
           ("stats", 2), ("stats", 3), ("norm", 2), ("norm", 3), ("xt", 2), ("xt", 3)]
    return ev


def coupled_stage(nc, mem, tag, out, ln, ln_next):
    events = coupled_events()
    done, seen = {}, {}
    for e in events:
        seen[e[0]] = seen.get(e[0], 0) + 1
        done[e] = seen[e[0]]

    with ExitStack() as ctx:
        def sb(name, shape):
            return ctx.enter_context(nc.sbuf_tensor(f"{tag}_{name}", shape, F32))

        def ps(name, shape):
            return ctx.enter_context(nc.psum_tensor(f"{tag}_{name}", shape, F32))

        def sem(name):
            return ctx.enter_context(nc.semaphore(f"{tag}_{name}"))

        x_res, w, const = mem["x_res"], mem["w_rest"], mem["const"]
        wcol = lambda name: w[:, W_REST[name][0]:sum(W_REST[name])]
        each = lambda name, shape=(P, UT): [sb(f"{name}{t}", list(shape)) for t in range(UNITS)]
        a_sb, b_sb, h_sb, g_sb, t_sb = each("a"), each("b"), each("h"), each("g"), each("t")
        g1 = each("g1")
        g2 = [sb(f"g2{i}", [P, UT]) for i in range(PAIRS)]
        g3 = sb("gelu3", [P, UT])
        cc = [each(f"c{n}_") for n in range(CYCLES)]
        txn, axn = sb("txn", [P, TILES, E]), sb("axn", [P, TILES, E])
        c1s = sb("c1s", [P, E])
        ctx_sum, gh1, gh2 = sb("ctx", [P, BATCH]), sb("gh1", [64, BATCH]), sb("gh2", [32, BATCH])
        tg, k0 = sb("tg", [P, BATCH]), sb("k0", [P, BATCH])
        k1, k7, hb4, hg3 = sb("k1", [P, 1]), sb("k7", [P, 1]), sb("hb4", [P, 1]), sb("hg3", [P, 1])
        ct = [sb(f"ct{i}", [P, CYCLES, 2 * TPU]) for i in range(PAIRS)]
        ab = [sb(f"ab{i}", [P, 6, 2 * TPU]) for i in range(PAIRS)]
        pa = [ps(f"pa{t}", [P, UT]) for t in range(UNITS)]
        p2 = [ps(f"p2{i}", [P, UT]) for i in range(PAIRS)]
        p3, spare = ps("p3", [P, UT]), ps("spare", [P, UT])
        pb = [p2[0], p3, p2[1], spare]
        pg = spare
        if ln_next is not None:
            ln_next.bank = lambda u: pa[u]

        small_ready = sem("small_ready")
        ctx_ready = sem("ctx_ready")
        glob_mm = sem("glob_mm")
        glob_act = sem("glob_act")
        k0_ready = sem("k0_ready")
        a_mm, b_mm = sem("a_mm"), sem("b_mm")
        a_ready, b_ready = sem("a_ready"), sem("b_ready")
        g1_ready = sem("g1_ready")
        l2_mm, l3_mm = sem("l2_mm"), sem("l3_mm")
        g2_ready, g3_ready = sem("g2_ready"), sem("g3_ready")
        z_mm = sem("z_mm")
        t_ready = sem("t_ready")
        c_ready = sem("c_ready")
        h_ready = sem("h_ready")
        g_ready = sem("g_ready")
        txn_ready = sem("txn_ready")
        ct_mm, ct_ready = sem("ct_mm"), sem("ct_ready")
        ab_ready = sem("ab_ready")
        axn_ready = sem("axn_ready")
        beta_added = sem("beta_added")
        x_done = sem("x_done")
        stored = sem("stored")
        dve_chain, pool_chain = sem("dve_chain"), sem("pool_chain")
        block = ctx.enter_context(nc.Block())

        if out is not None:
            @block.sync
            def _(sp):
                for u in range(UNITS):
                    sp.wait_ge(x_done, u + 1)
                    tiles = slice(TPU * u, TPU * (u + 1))
                    sp.dma_start(out.rearrange("(i p) e -> p i e", p=P)[:, tiles, :], x_res[:, tiles, :]
                                 ).then_inc(stored, 16)
                sp.wait_ge(stored, 16 * UNITS)

        @block.gpsimd
        def _(pool):
            chain = Chain(pool, pool_chain)
            pool.wait_ge(mem["rest_loaded"], 32)
            for e in events:
                if e[0] == "c" and e[2] == 0:
                    t = e[1]
                    pool.wait_ge(c_ready, done[e])
                    pool.wait_ge(a_ready, t + 1)
                    pool.wait_ge(b_ready, t + 1)
                    chain.after(nc.gpsimd.tensor_tensor(g_sb[t][:, :], cc[0][t][:, :], a_sb[t][:, :], ALU.mult))
                    nc.gpsimd.tensor_tensor(g_sb[t][:, :], b_sb[t][:, :], g_sb[t][:, :], ALU.subtract
                                            ).then_inc(g_ready, 1)
                elif e[0] == "twist":
                    for block_out, (block_in, sign) in enumerate([(2, 1.0), (3, -1.0), (0, -1.0), (1, 1.0)]):
                        ins = nc.gpsimd.tensor_scalar(txn[:, :, 32 * block_out:32 * block_out + 32],
                                                      ln.xn[:, :, 32 * block_in:32 * block_in + 32],
                                                      sign, None, ALU.mult)
                        ins.then_inc(txn_ready, 1)

        @block.vector
        def _(dve):
            chain = Chain(dve, dve_chain)
            TT, TS = nc.vector.tensor_tensor, nc.vector.tensor_scalar
            dve.wait_ge(mem["rest_loaded"], 32)
            for dst, src, by in ((k1, "range", 0.3), (k7, "range", 0.7), (hb4, "b4", 0.5), (hg3, "gb3", 0.5)):
                TS(dst[:, :], wcol(src), by, None, ALU.mult)
            TS(c1s[:, :], wcol("c1p"), const[:, CONST["sign"][0]:CONST["sign"][0] + 1], None, ALU.mult
               ).then_inc(small_ready, 1)
            ins = nc.vector.tensor_reduce(ctx_sum[:, :], ln.xt[:, :].rearrange("p (b t) -> p b t", b=BATCH), AX_X, ALU.add)
            ins.then_inc(ctx_ready, 1)
            for e in events:
                if e[0] == "g1" and e[2] == 0:
                    t = e[1]
                    dve.wait_ge(g1_ready, done[e])
                    nc.vector.tensor_copy(a_sb[t][:, :], pa[t][:, :]).then_inc(a_ready, 1)
                elif e == ("c", 0, 0):
                    dve.wait_ge(glob_act, 3)
                    TS(k0[:, :], tg[:, :], k7[:, 0:1], 0.1, ALU.mult, ALU.add).then_inc(k0_ready, 1)
                    dve.wait_ge(k0_ready, 1)
                if e[0] == "c":
                    _, t, n = e
                    dve.wait_ge(t_ready, done[("tanh", t, n)])
                    for b in range(2):
                        cols = slice(SEQ * b, SEQ * (b + 1))
                        ins = TS(cc[n][t][:, cols], t_sb[t][:, cols], k1[:, 0:1], k0[:, 2 * t + b:2 * t + b + 1],
                                 ALU.mult, ALU.add)
                    ins.then_inc(c_ready, 1)
                    if n < CYCLES - 1:
                        dve.wait_ge(c_ready, done[e])
                        if n == 0:
                            dve.wait_ge(b_ready, t + 1)
                            dve.wait_ge(a_ready, t + 1)
                        else:
                            dve.wait_ge(g_ready, t + 1)
                        step, base = (b_sb, a_sb) if n == 0 else (g_sb, h_sb)
                        chain.after(TT(t_sb[t][:, :], cc[n][t][:, :], step[t][:, :], ALU.mult))
                        TT(h_sb[t][:, :], t_sb[t][:, :], base[t][:, :], ALU.add).then_inc(h_ready, 1)
                elif e[0] == "poly":
                    i = e[1]
                    c, s = ct[i], ab[i]
                    dve.wait_ge(ct_mm, i + 1)
                    nc.vector.tensor_copy(c[:, :, :].rearrange("p n t -> p (n t)"),
                                          p2[i][:, 0:CYCLES * 2 * TPU]).then_inc(ct_ready, 1)
                    dve.wait_ge(ct_ready, i + 1)
                    TT(s[:, 0, :], c[:, 0, :], c[:, 1, :], ALU.mult)
                    chain.after(TT(s[:, 1, :], c[:, 0, :], c[:, 1, :], ALU.add))
                    chain.after(TS(s[:, 2, :], s[:, 0, :], -1.0, 1.0, ALU.mult, ALU.add))
                    TT(s[:, 3, :], c[:, 2, :], s[:, 1, :], ALU.mult)
                    chain.after(TT(s[:, 0, :], c[:, 2, :], s[:, 2, :], ALU.mult))
                    TT(s[:, 4, :], s[:, 2, :], s[:, 3, :], ALU.subtract)
                    TT(s[:, 5, :], s[:, 1, :], s[:, 0, :], ALU.add).then_inc(ab_ready, 1)
                elif e[0] == "beta":
                    u = e[1]
                    dve.wait_ge(ab_ready, u // 2 + 1)
                    dve.wait_ge(txn_ready, 4)
                    for k in range(TPU):
                        n, t = TPU * u + k, TPU * (u % 2) + k
                        ins = nc.vector.scalar_tensor_tensor(
                            out=x_res[:, n, :], in0=txn[:, n, :], scalar=ab[u // 2][:, 5, t:t + 1], in1=x_res[:, n, :],
                            op0=ALU.mult, op1=ALU.add)
                    ins.then_inc(beta_added, 1)
                elif e[0] == "add":
                    u = e[1]
                    dve.wait_ge(beta_added, u + 1)
                    dve.wait_ge(axn_ready, u + 1)
                    tiles = slice(TPU * u, TPU * (u + 1))
                    TT(x_res[:, tiles, :], x_res[:, tiles, :], axn[:, tiles, :], ALU.add).then_inc(x_done, 1)
                elif e[0] == "stats" and ln_next is not None:
                    dve.wait_ge(x_done, e[1] + 1)
                    ln_next.statistics(chain, e[1])
                elif e[0] == "norm" and ln_next is not None:
                    ln_next.reciprocals(dve, chain, e[1])

        @block.scalar
        def _(act):
            act.wait_ge(mem["rest_loaded"], 32)
            act.wait_ge(small_ready, 1)
            gelu = lambda dst, src, bias, scale=1.0: nc.scalar.activation(dst, src, ACT.Gelu, bias=bias, scale=scale)
            for e in events:
                if e[0] == "g1":
                    _, t, n = e
                    if n == 0:
                        act.wait_ge(a_mm, t + 1)
                        gelu(g1[t][:, :], pa[t][:, :], wcol("b1")).then_inc(g1_ready, 1)
                        act.wait_ge(b_mm, t + 1)
                        nc.scalar.copy(b_sb[t][:, :], pb[t][:, :]).then_inc(b_ready, 1)
                    else:
                        act.wait_ge(h_ready, done[("c", t, n - 1)])
                        gelu(g1[t][:, :], h_sb[t][:, :], wcol("b1")).then_inc(g1_ready, 1)
                elif e[0] == "g2":
                    _, i, n = e
                    act.wait_ge(l2_mm, done[("l2", i, n)])
                    gelu(g2[i][:, :], p2[i][:, :], wcol("b2")).then_inc(g2_ready, 1)
                elif e[0] == "g3":
                    _, i, n = e
                    act.wait_ge(l3_mm, done[("l3", i, n)])
                    half = slice(64 * i, 64 * i + 64)
                    gelu(g3[half, :], p3[half, :], wcol("b3")[half]).then_inc(g3_ready, 1)
                elif e[0] == "glob":
                    act.wait_ge(glob_mm, e[1] + 1)
                    if e[1] == 0:
                        gelu(gh1[:, :], pg[0:64, 0:BATCH], wcol("gb1")[0:64], 1.0 / SEQ).then_inc(glob_act, 1)
                    elif e[1] == 1:
                        gelu(gh2[:, :], pg[0:32, BATCH:2 * BATCH], wcol("gb2")[0:32]).then_inc(glob_act, 1)
                    else:
                        nc.scalar.activation(tg[:, :], pg[:, 2 * BATCH:3 * BATCH], ACT.Tanh, bias=hg3[:, 0:1],
                                             scale=0.5).then_inc(glob_act, 1)
                elif e[0] == "tanh":
                    _, t, n = e
                    act.wait_ge(z_mm, done[("z", t, n)])
                    if n > 0:
                        act.wait_ge(h_ready, done[("c", t, n - 1)])
                    nc.scalar.activation(t_sb[t][:, :], pa[t][:, :], ACT.Tanh, bias=hb4[:, 0:1], scale=0.5
                                         ).then_inc(t_ready, 1)
                elif e[0] == "alpha":
                    u = e[1]
                    act.wait_ge(ab_ready, u // 2 + 1)
                    for k in range(TPU):
                        n, t = TPU * u + k, TPU * (u % 2) + k
                        ins = nc.scalar.activation(axn[:, n, :], ln.xn[:, n, :], ACT.Copy,
                                                   scale=ab[u // 2][:, 4, t:t + 1])
                    ins.then_inc(axn_ready, 1)
                elif e[0] == "norm" and ln_next is not None:
                    ln_next.deviation(act, e[1])
                    ln_next.normalise(act, e[1])
                elif e[0] == "xt" and ln_next is not None:
                    ln_next.copy(act, e[1])

        @block.tensor
        def _(pe):
            def keep_awake():
                pe.matmul(spare[:, 0:FILL], wcol("c1"), ln.xt[:, 0:FILL], start=True, stop=True)

            pe.wait_ge(mem["rest_loaded"], 32)
            pe.wait_ge(small_ready, 1)
            for e in events:
                if e[0] in ("l2", "l3", "z") and e[2] + e[1] > 0:
                    if e == ("z", 0, 0) or e[0] != "z" and e[1:] == (1, 0):
                        pe.wait_ge(b_ready, UNITS)
                    keep_awake()
                if e[0] == "ab":
                    t = e[1]
                    cols = slice(UT * t, UT * (t + 1))
                    pe.matmul(pa[t][:, :], wcol("c1"), ln.xt[:, cols], start=True, stop=True).then_inc(a_mm, 1)
                    if pb[t] is pg:
                        pe.wait_ge(glob_act, 3)
                    pe.matmul(pb[t][:, :], c1s[:, :], ln.xt[:, cols], start=True, stop=True).then_inc(b_mm, 1)
                elif e[0] == "glob":
                    if e[1] == 0:
                        pe.wait_ge(ctx_ready, 1)
                        pe.matmul(pg[0:64, 0:BATCH], wcol("g1"), ctx_sum[:, :], start=True, stop=True
                                  ).then_inc(glob_mm, 1)
                    elif e[1] == 1:
                        pe.wait_ge(glob_act, 1)
                        pe.matmul(pg[0:32, BATCH:2 * BATCH], wcol("g2")[0:64], gh1[:, :], start=True, stop=True
                                  ).then_inc(glob_mm, 1)
                    else:
                        pe.wait_ge(glob_act, 2)
                        pe.matmul(pg[:, 2 * BATCH:3 * BATCH], wcol("g3r")[0:32], gh2[:, :], start=True, stop=True
                                  ).then_inc(glob_mm, 1)
                elif e[0] == "l2":
                    _, i, n = e
                    pe.wait_ge(g1_ready, done[("g1", 2 * i + 1, n)])
                    if n == 0:
                        pe.wait_ge(b_ready, 2 * i + 1)
                    else:
                        pe.wait_ge(g2_ready, done[("g2", i, n - 1)])
                    for k in range(2):
                        ins = pe.matmul(p2[i][64 * k:64 * k + 64, :], wcol("c2"), g1[2 * i + k][:, :],
                                        start=True, stop=True)
                    ins.then_inc(l2_mm, 1)
                elif e[0] == "l3":
                    _, i, n = e
                    pe.wait_ge(g2_ready, done[("g2", i, n)])
                    if n == 0:
                        pe.wait_ge(b_ready, 2)
                    pe.matmul(p3[64 * i:64 * i + 64, :], wcol("c3"), g2[i][:, :], start=True, stop=True).then_inc(l3_mm, 1)
                elif e[0] == "z":
                    _, t, n = e
                    pe.wait_ge(g3_ready, done[("g3", t // 2, n)])
                    pe.wait_ge(a_ready, t + 1)
                    half = slice(64 * (t // 2), 64 * (t // 2) + 64)
                    pe.matmul(pa[t][:, :], wcol("c4r")[half, P * (t % 2):P * (t % 2 + 1)], g3[half, :],
                              start=True, stop=True).then_inc(z_mm, 1)
                elif e[0] == "turn":
                    i = e[1]
                    pe.wait_ge(c_ready, done[("c", 2 * i + 1, CYCLES - 1)])
                    for n in range(CYCLES):
                        for t in range(2 * TPU):
                            col = 2 * TPU * n + t
                            src = cc[n][2 * i + t // TPU][0:1, P * (t % TPU):P * (t % TPU + 1)]
                            ins = pe.transpose(p2[i][:, col:col + 1], src, ln.ident[0:1, 0:1])
                    ins.then_inc(ct_mm, 1)
                elif e[0] == "xt" and ln_next is not None:
                    u = e[1]
                    pe.wait_ge(t_ready, done[("tanh", u, CYCLES - 1)])
                    ln_next.turn(pe, u)


PROJ = ("q", "qs", "k", "ks", "v0", "v1", "g0", "g1")
HG = 2
ITEMS = [(t, hg) for t in range(TPU) for hg in range(HG)]


def retention_events():
    ev = []
    for u in range(UNITS + 1):
        after = {}
        if u > 0:
            after = {1: [("var", u - 1)], 2: [("rec", u - 1)],
                     5: [("spread", u - 1, hg) for hg in range(HG)], 7: [("proj", u - 1)]}
            if u > 1:
                after[3] = [("next_xt", u - 2)]
        if u < UNITS:
            ev += [("kt", u), ("s", u, 0), ("u", u)]
            for i in range(len(ITEMS)):
                if i + 1 < len(ITEMS):
                    ev.append(("s", u, i + 1))
                ev.append(("o", u, i))
                ev += after.get(i, [])
            ev += [("evac", u, hg) for hg in range(HG)]
        else:
            for i in sorted(after):
                ev += after[i]
    ev.append(("next_xt", UNITS - 1))
    return ev


def retention_stage(nc, mem, ln, ln_next):
    with ExitStack() as ctx:
        def sb(name, shape):
            return ctx.enter_context(nc.sbuf_tensor(f"r_{name}", shape, F32))

        def ps(name, shape):
            return ctx.enter_context(nc.psum_tensor(f"r_{name}", shape, F32))

        def sem(name):
            return ctx.enter_context(nc.semaphore(f"r_{name}"))

        x_res, w, const = mem["x_res"], mem["w_rest"], mem["const"]
        wcol = lambda name: w[:, W_REST[name][0]:sum(W_REST[name])]
        ccol = lambda name: const[:, CONST[name][0]:sum(CONST[name])]

        def again(ap, n):
            return bass.AP(ap.tensor, ap.offset, [list(ap.ap[0]), [0, n], list(ap.ap[1])])

        rot = {k: sb(f"{k}r", [P, TOK]) for k in "qk"}
        turned = [[sb(f"{k}{i}", [P, UT]) for i in range(2)] for k in "qk"]
        qbd = [sb(f"qbd{i}", [P, RH, UT]) for i in range(2)]
        w_v, b_v = sb("w_v", [P, 2 * E]), sb("b_v", [P, 2 * E])
        val = sb("val", [P, TILES, 2 * E])
        gate = sb("gate", [P, HG, TOK])
        ktok = [sb(f"ktok{i}", [P, 2, P]) for i in range(2)]
        kv = [sb(f"kv{i}", [P, 2, 2 * E]) for i in range(2)]
        masked = [sb(f"masked{i}", [P, 4, P]) for i in range(4)]
        o_sb = [sb(f"o{i}", [P, UT]) for i in range(HG)]
        sq = [sb(f"sq{i}", [P, UT]) for i in range(HG)]
        std, rec = sb("sd", [P, SEQ]), sb("rec", [P, SEQ])
        gated = [sb(f"gated{i}", [P, UT]) for i in range(HG)]

        work = [ps(f"work{i}", [P, 512]) for i in range(3)]
        s_bank = [ps(f"s{i}", [P, 512]) for i in range(2)]
        o_bank = [ps(f"ob{i}", [P, 512]) for i in range(3)]
        events = retention_events()

        keys = [("w_v",), ("b_v",)] + [(k, u) for u in range(UNITS) for k in PROJ]
        keys += [e for e in events if e[0] in ("kt", "u", "var", "spread", "proj", "next_xt")]
        use = {k: n for n, k in enumerate(keys)}
        mine = [key for key in keys if key[0] != "next_xt"]
        filled = {key: n + 1 for n, key in enumerate(mine)}
        ln_next.bank = lambda u: work[use[("next_xt", u)] % 3]

        centred = sem("centred")
        zeroed = sem("zeroed")
        work_mm = sem("work_mm")
        part_ready = sem("part_ready")
        rot_ready = sem("rot_ready")
        val_ready = sem("val_ready")
        gate_ready = sem("gate_ready")
        qbd_loaded = [sem(f"qbd_loaded{i}") for i in range(2)]
        ktok_ready = sem("ktok_ready")
        kv_ready = sem("kv_ready")
        s_mm = sem("s_mm")
        masked_ready = sem("masked_ready")
        o_mm = sem("o_mm")
        o_ready = sem("o_ready")
        sq_ready = sem("sq_ready")
        std_ready = sem("sd_ready")
        rec_ready = sem("rec_ready")
        swish_ready = sem("swish_ready")
        gated_ready = sem("gated_ready")
        bias_added = sem("bias_added")
        x_done = sem("x_done")
        dve_chain = sem("dve_chain")
        block = ctx.enter_context(nc.Block())

        def in_bank(eng, key):
            eng.wait_ge(work_mm, filled[key])
            return work[use[key] % 3]

        def read(key):
            kind = key[0]
            if kind in ("w_v", "b_v"):
                return centred, 1 + ("w_v", "b_v").index(kind)
            u = key[1]
            if kind in ("q", "qs", "k", "ks"):
                return part_ready, 4 * u + PROJ.index(kind) + 1
            if kind[0] in "vg" and len(kind) == 2:
                return (val_ready if kind[0] == "v" else gate_ready), 2 * u + int(kind[1]) + 1
            if kind == "spread":
                return gated_ready, HG * u + key[2] + 1
            return {"var": std_ready, "kt": ktok_ready, "u": kv_ready, "proj": x_done, "next_xt": ln_next.xt_ready}[kind], u + 1

        @block.sync
        def _(sp):
            for u in range(UNITS):
                sp.wait_ge(rot_ready, 2 * u + 1)
                if u < 2:
                    sp.wait_ge(zeroed, u + 1)
                else:
                    sp.wait_ge(s_mm, 8 * (u - 1))
                for h in range(RH):
                    sp.dma_start(qbd[u % 2][RK * h:RK * (h + 1), h, :],
                                 rot["q"][RK * h:RK * (h + 1), UT * u:UT * (u + 1)]).then_inc(qbd_loaded[u % 2], 16)

        @block.gpsimd
        def _(pool):
            nc.gpsimd.memset(qbd[0][:, :, :], 0.0).then_inc(zeroed, 1)
            for u in range(UNITS):
                for n, k in enumerate("qk"):
                    pool.wait_ge(part_ready, 4 * u + 2 * n + 2)
                    nc.gpsimd.tensor_tensor(rot[k][:, UT * u:UT * (u + 1)], turned[n][0][:, :], turned[n][1][:, :],
                                            ALU.add).then_inc(rot_ready, 1)
                if u == 0:
                    nc.gpsimd.memset(qbd[1][:, :, :], 0.0).then_inc(zeroed, 1)
            for i in range(TILES):
                ins = nc.gpsimd.tensor_tensor(x_res[:, i, :], x_res[:, i, :], wcol("b_p"), ALU.add)
            ins.then_inc(bias_added, 1)
            for e in events:
                if e[0] == "evac":
                    _, u, hg = e
                    n = HG * u + hg + 1
                    pool.wait_ge(o_ready, n)
                    pool.wait_ge(gate_ready, n)
                    if u > 0:
                        pool.wait_ge(work_mm, filled[("proj", u - 1)])
                    nc.gpsimd.tensor_tensor(gated[hg][:, :], o_sb[hg][:, :], gate[:, hg, UT * u:UT * (u + 1)],
                                            ALU.mult).then_inc(swish_ready, 1)

        @block.vector
        def _(dve):
            chain = Chain(dve, dve_chain)
            for dst, key in ((w_v, ("w_v",)), (b_v, ("b_v",))):
                bank = in_bank(dve, key)
                nc.vector.tensor_copy(dst[:, :], bank[:, 0:2 * E]).then_inc(centred, 1)
            for u in range(UNITS):
                for n, k in enumerate("qk"):
                    if u > 0:
                        dve.wait_ge(rot_ready, 2 * (u - 1) + n + 1)
                    for i, (key, table) in enumerate([(k, "cos_" + k), (k + "s", "sin_" + k)]):
                        bank = in_bank(dve, (key, u))
                        nc.vector.scalar_tensor_tensor(
                            out=turned[n][i][:, :].rearrange("p (b t) -> p b t", b=2),
                            in0=bank[:, :].rearrange("p (b t) -> p b t", b=2), scalar=wcol("b" + key),
                            in1=again(ccol(table), 2), op0=ALU.add, op1=ALU.mult).then_inc(part_ready, 1)
                for half in range(2):
                    bank = in_bank(dve, (f"v{half}", u))
                    i = TPU * u + 2 * half
                    dve.wait_ge(centred, 2)
                    nc.vector.tensor_tensor(val[:, i:i + 2, :], bank[:, :].rearrange("p (t v) -> p t v", t=2),
                                            again(b_v[:, :], 2), ALU.add).then_inc(val_ready, 1)
            for e in events:
                if e[0] == "u":
                    u = e[1]
                    bank = in_bank(dve, e)
                    if u >= 2:
                        dve.wait_ge(o_mm, 8 * (u - 1))
                    nc.vector.tensor_tensor(kv[u % 2][:, :, :], bank[:, :].rearrange("p (t v) -> p t v", t=2),
                                            again(ccol("heads"), 2), ALU.mult).then_inc(kv_ready, 1)
                elif e[0] == "s":
                    n = 8 * e[1] + e[2]
                    dve.wait_ge(s_mm, n + 1)
                    if n >= 4:
                        dve.wait_ge(o_mm, n - 3)
                    nc.vector.tensor_tensor(masked[n % 4][:, :, :],
                                            s_bank[n % 2][:, :].rearrange("p (h i) -> p h i", h=4),
                                            again(ccol("causal"), 4), ALU.mult).then_inc(masked_ready, 1)
                elif e[0] == "rec":
                    u = e[1]
                    dve.wait_ge(std_ready, u + 1)
                    if u > 0:
                        dve.wait_ge(work_mm, filled[("spread", u - 1, 1)])
                    nc.vector.reciprocal(rec[:, :], std[:, :]).then_inc(rec_ready, 1)
                elif e[0] == "spread":
                    _, u, hg = e
                    bank = in_bank(dve, e)
                    dve.wait_ge(swish_ready, HG * u + hg + 1)
                    nc.vector.tensor_tensor(gated[hg][:, :], bank[:, :], gated[hg][:, :], ALU.mult
                                            ).then_inc(gated_ready, 1)
                elif e[0] == "proj":
                    u = e[1]
                    bank = in_bank(dve, e)
                    dve.wait_ge(bias_added, 1)
                    xs = x_res[:, TPU * u:TPU * (u + 1), :].rearrange("p i e -> p (i e)")
                    nc.vector.tensor_tensor(xs, bank[:, :], xs, ALU.add).then_inc(x_done, 1)
                    dve.wait_ge(x_done, u + 1)
                    ln_next.statistics(chain, u)
                elif e[0] == "next_xt":
                    ln_next.normalise_on_vector(dve, chain, e[1])

        @block.scalar
        def _(act):
            for u in range(UNITS):
                for hg in range(HG):
                    bank = in_bank(act, (f"g{hg}", u))
                    at = W_REST["bg"][0] + hg
                    nc.scalar.activation(gate[:, hg, UT * u:UT * (u + 1)], bank[:, :], ACT.Silu, bias=w[:, at:at + 1]
                                         ).then_inc(gate_ready, 1)
            for e in events:
                if e[0] == "kt":
                    bank = in_bank(act, e)
                    if e[1] >= 2:
                        act.wait_ge(work_mm, filled[("u", e[1] - 2)])
                    nc.scalar.copy(ktok[e[1] % 2][:, :, :].rearrange("p a b -> p (a b)"), bank[:, 0:2 * P]
                                   ).then_inc(ktok_ready, 1)
                elif e[0] == "evac":
                    _, u, hg = e
                    n = HG * u + hg
                    act.wait_ge(o_mm, 8 * (u + 1) - (1 - hg))
                    if u > 0:
                        act.wait_ge(swish_ready, n - 1)
                        act.wait_ge(work_mm, filled[("var", u - 1)])
                    nc.scalar.activation(sq[hg][:, :], o_bank[n % 3][:, :], ACT.Square).then_inc(sq_ready, 1)
                    nc.scalar.copy(o_sb[hg][:, :], o_bank[n % 3][:, :]).then_inc(o_ready, 1)
                elif e[0] == "var":
                    u = e[1]
                    bank = in_bank(act, e)
                    if u > 0:
                        act.wait_ge(rec_ready, u)
                    nc.scalar.activation(std[:, :], bank[:, 0:SEQ], ACT.Sqrt, bias=ln.eps[:, 0:1]).then_inc(std_ready, 1)
                elif e[0] == "next_xt":
                    ln_next.deviation(act, e[1])
                    ln_next.copy(act, e[1])

        @block.tensor
        def _(pe):
            def fill(key):
                if use[key] >= 3:
                    pe.wait_ge(*read(keys[use[key] - 3]))
                return work[use[key] % 3]

            for key, src in ((("w_v",), "vt"), (("b_v",), "b_v")):
                bank = fill(key)
                for hg in range(HG):
                    ins = pe.matmul(bank[:, P * hg:P * (hg + 1)], wcol(src)[:, P * hg:P * (hg + 1)], ccol("centre"),
                                    start=True, stop=True)
                ins.then_inc(work_mm, 1)
            for u in range(UNITS):
                cols = slice(UT * u, UT * (u + 1))
                for k in ("q", "qs", "k", "ks"):
                    pe.matmul(fill((k, u))[:, :], wcol(k), ln.xt[:, cols], start=True, stop=True).then_inc(work_mm, 1)
                pe.wait_ge(centred, 1)
                for half in range(2):
                    bank = fill((f"v{half}", u))
                    for t in range(2):
                        at = UT * u + P * (2 * half + t)
                        ins = pe.matmul(bank[:, 2 * E * t:2 * E * (t + 1)], ln.xt[:, at:at + P], w_v[:, :],
                                        start=True, stop=True)
                    ins.then_inc(work_mm, 1)
                for hg in range(HG):
                    pe.matmul(fill((f"g{hg}", u))[:, :], wcol("gate")[:, P * hg:P * (hg + 1)], ln.xt[:, cols],
                              start=True, stop=True).then_inc(work_mm, 1)
            for e in events:
                if e[0] == "kt":
                    u = e[1]
                    pe.wait_ge(rot_ready, 2 * u + 2)
                    bank = fill(e)
                    for b in range(2):
                        at = UT * u + SEQ * b
                        ins = pe.transpose(bank[:, P * b:P * (b + 1)], rot["k"][:, at:at + P], ln.ident)
                    ins.then_inc(work_mm, 1)
                elif e[0] == "s":
                    _, u, i = e
                    n, (t, hg) = 8 * u + i, ITEMS[i]
                    if i == 0:
                        pe.wait_ge(qbd_loaded[u % 2], 16 * RH * (u // 2 + 1))
                    if n >= 2:
                        pe.wait_ge(masked_ready, n - 1)
                    at = UT * u + P * t
                    pe.matmul(s_bank[n % 2][:, :].rearrange("p (h i) -> p h i", h=4), rot["k"][:, at:at + P],
                              qbd[u % 2][:, 4 * hg:4 * hg + 4, P * t:P * (t + 1)], start=True, stop=True
                              ).then_inc(s_mm, 1)
                elif e[0] == "u":
                    u = e[1]
                    bank = fill(e)
                    pe.wait_ge(ktok_ready, u + 1)
                    pe.wait_ge(val_ready, 2 * u + 2)
                    for b in range(2):
                        ins = pe.matmul(bank[:, 2 * E * b:2 * E * (b + 1)], ktok[u % 2][:, b, :],
                                        val[:, TPU * u + 2 * b, :], start=True, stop=True)
                    ins.then_inc(work_mm, 1)
                elif e[0] == "o":
                    _, u, i = e
                    n, (t, hg) = 8 * u + i, ITEMS[i]
                    m = HG * u + hg
                    out = o_bank[m % 3][:, P * t:P * (t + 1)]
                    if i < 2 and m >= 3:
                        pe.wait_ge(o_ready, m - 2)
                    if t % 2 == 1:
                        pe.wait_ge(kv_ready, u + 1)
                        at = UT * u + P * t
                        pe.matmul(out, kv[u % 2][:, t // 2, P * hg:P * (hg + 1)], rot["q"][:, at:at + P],
                                  start=True, stop=False)
                    pe.wait_ge(masked_ready, n + 1)
                    for j in range(4):
                        h = 4 * hg + j
                        ins = pe.matmul(out[32 * j:32 * j + 32, :], val[:, TPU * u + t, RV * h:RV * (h + 1)],
                                        masked[n % 4][:, j, :], start=(t % 2 == 0), stop=True)
                    ins.then_inc(o_mm, 1)
                elif e[0] == "var":
                    u = e[1]
                    bank = fill(e)
                    pe.wait_ge(sq_ready, HG * (u + 1))
                    for hg in range(HG):
                        for b in range(2):
                            at = 32 * (2 * hg + b)
                            ins = pe.matmul(bank[at:at + 32, 0:SEQ], ccol("mean"), sq[hg][:, SEQ * b:SEQ * (b + 1)],
                                            start=True, stop=True)
                    ins.then_inc(work_mm, 1)
                elif e[0] == "spread":
                    _, u, hg = e
                    bank = fill(e)
                    pe.wait_ge(rec_ready, u + 1)
                    for b in range(2):
                        at = P * (2 * hg + b)
                        ins = pe.matmul(bank[:, SEQ * b:SEQ * (b + 1)], ccol("spread")[:, at:at + P], rec[:, :],
                                        start=True, stop=True)
                    ins.then_inc(work_mm, 1)
                elif e[0] == "proj":
                    u = e[1]
                    bank = fill(e)
                    pe.wait_ge(gated_ready, HG * (u + 1))
                    for t in range(TPU):
                        for hg in range(HG):
                            ins = pe.matmul(bank[:, P * t:P * (t + 1)], gated[hg][:, P * t:P * (t + 1)],
                                            wcol(f"p{hg}"), start=(hg == 0), stop=(hg == HG - 1))
                    ins.then_inc(work_mm, 1)
                elif e[0] == "next_xt":
                    fill(e)
                    ln_next.turn(pe, e[1])


def build(nc, ins, out):
    parts = nc.dram_tensor("scratch_parts", (2, 2, AH * 32, UT), F32, kind="Internal").ap()
    dram = dict(ins)
    dram["parts"] = [[parts[kind, which] for which in range(2)] for kind in range(2)]
    dram["o"] = nc.dram_tensor("scratch_o", (2, P, UT), F32, kind="Internal").ap()
    dram["r"] = nc.dram_tensor("scratch_r", (P, AH * UT // P), F32, kind="Internal").ap()
    with ExitStack() as ctx:
        mem = {
            "x_res": ctx.enter_context(nc.sbuf_tensor("x_res", [P, TILES, E], F32)),
            "w_att": ctx.enter_context(nc.sbuf_tensor("w_att", [P, W_ATT_N], F32)),
            "w_rest": ctx.enter_context(nc.sbuf_tensor("w_rest", [P, W_REST_N], F32)),
            "const": ctx.enter_context(nc.sbuf_tensor("const", [P, CONST_N], F32)),
            "rest_loaded": ctx.enter_context(nc.semaphore("rest_loaded")),
        }
        mem["ln"] = layernorm_buffers(nc, ctx)
        ln = [LayerNorm(nc, ctx, mem, f"ln{i}") for i in range(4)]
        attention_stage(nc, mem, dram, ins["x"], ln[0], ln[1])
        coupled_stage(nc, mem, "f0", None, ln[1], ln[2])
        retention_stage(nc, mem, ln[2], ln[3])
        coupled_stage(nc, mem, "f1", out, ln[3], None)


def _constants():
    import numpy as np

    aux = np.zeros((2, 2, 8, UT), np.float32)
    aux[:, 0, 0:2] = 1.0
    window = np.arange(UT) % P // WIN
    for bit in range(3):
        on = (window >> bit & 1).astype(np.float32)
        aux[0, 1, 2 + 2 * bit], aux[0, 1, 3 + 2 * bit] = on, 1 - on
        aux[0, 0, 2 + 2 * bit], aux[0, 0, 3 + 2 * bit] = -FAR * (1 - on), -FAR * on

    f32 = np.float32
    pos = np.arange(SEQ, dtype=f32)
    half = E // 2
    scale_vec = (np.arange(0, E, 2, dtype=f32) + f32(0.4 * E)) / f32(1.4 * E)
    scale = scale_vec[None, :].astype(np.float64) ** (pos[:, None].astype(np.float64) / 512.0)
    inv_freq = (f32(1.0) / f32(10000.0) ** (np.arange(half, dtype=f32) / f32(half))).astype(f32)
    angle = (pos[:, None] * inv_freq[None, :]).astype(f32).astype(np.float64)
    gamma = f32(1.0) - np.exp(np.linspace(np.log(1 / 32), np.log(1 / 512), RH).astype(f32)).astype(f32)
    log_decay = np.log(gamma).astype(f32).astype(np.float64)
    decay = np.exp(log_decay[:, None, None] * np.maximum(pos[:, None] - pos[None, :], 0.0))
    norm = np.sqrt((decay * (pos[:, None] >= pos[None, :])).sum(-1))
    head = np.arange(E) // RK
    q_side = np.exp(log_decay[head][:, None] * pos[None, :]) / norm[head] * RK ** -0.5
    k_side = np.exp(-log_decay[head][:, None] * pos[None, :])
    sign = np.where(np.arange(E) % 2 == 0, -1.0, 1.0)[:, None]
    wide = lambda a: np.repeat(a, 2, axis=1).T
    const = np.zeros((P, CONST_N), np.float32)

    def put(name, a):
        at, n = CONST[name]
        const[:, at:at + n] = a

    put("ident", np.eye(P))
    put("cos_q", wide(np.cos(angle) * scale) * q_side)
    put("sin_q", wide(np.sin(angle) * scale) * q_side * sign)
    put("cos_k", wide(np.cos(angle) / scale) * k_side)
    put("sin_k", wide(np.sin(angle) / scale) * k_side * sign)
    put("heads", head[:, None] == (np.arange(2 * E) // RV)[None, :])
    put("causal", np.arange(P)[:, None] <= np.arange(P)[None, :])
    put("mean", (np.arange(P)[:, None] // RV == np.arange(32)[None, :] // 8) / RV)
    quadrants = np.arange(4)[None, :, None] * 32 + np.arange(P)[None, None, :] // RV * 8
    put("spread", (np.arange(P)[:, None, None] == quadrants).reshape(P, -1))
    put("centre", np.eye(P) - (np.arange(P)[:, None] // RV == np.arange(P)[None, :] // RV) / RV)
    blocks = np.arange(P) // 32
    put("sign", np.where((blocks == 0) | (blocks == 3), -1.0, 1.0)[:, None])
    return aux, const


def _pack(spec, total, blocks):
    import numpy as np

    out = np.zeros((P, total), np.float32)
    for name, a in blocks.items():
        at, n = spec[name]
        a = np.asarray(a)
        out[:a.shape[0], at:at + n] = a
    return out


def kernel(**inputs):
    import numpy as np
    import concourse.bacc as _bacc
    from concourse.bass_utils import run_bass_kernel_spmd as _run

    a = {k.replace("L0_attn_a_", "a_").replace("L0_attn_b_", "r_").replace("L0_ffn_", "f_"): np.asarray(v)
         for k, v in inputs.items()}
    column = lambda v: v.reshape(-1, P).T
    down = lambda v: np.broadcast_to(v[:, None], (v.shape[0], P))
    spread = lambda v: np.broadcast_to(v[None, :], (P, v.shape[0]))
    order = np.arange(E).reshape(AG, AJ, AD)
    rows = np.concatenate([order[:3].transpose(1, 0, 2).reshape(-1), order[3].reshape(-1)])
    att = _pack(W_ATT, W_ATT_N, {
        "in_g": a["a_w_in_g"].T, "in_l": a["a_w_in_l"].T,
        "out_g": a["a_w_out_g"][:, rows], "out_l": a["a_w_out_l"][:, rows],
        "f_g": a["a_w_f"].T[:E], "f_l": a["a_w_f"].T[E:],
        "b_in_g": column(a["a_b_in_g"][:2 * E]), "b_in_l": column(a["a_b_in_l"][:2 * E]),
        "b_v_g": down(a["a_b_in_g"][2 * E:][rows]), "b_v_l": down(a["a_b_in_l"][2 * E:][rows]),
        "b_out_g": down(a["a_b_out_g"]), "b_out_l": down(a["a_b_out_l"]), "b_f": spread(a["a_b_f"])})

    swap = np.arange(E) ^ 1
    turn = (np.arange(E) + 64) % E
    w1 = a["f_cn_w1"]
    w_q, w_k, w_v = a["r_w_qkv"][:, :E], a["r_w_qkv"][:, E:2 * E], a["r_w_qkv"][:, 2 * E:]
    b_q, b_k, b_v = a["r_b_qkv"][:E], a["r_b_qkv"][E:2 * E], a["r_b_qkv"][2 * E:]
    c3 = np.zeros((P, E // 2), np.float32)
    c3[:64, :32], c3[64:, 32:] = a["f_cn_w3"], a["f_cn_w3"]
    c4 = np.zeros((P, 2 * E), np.float32)
    for half in range(2):
        c4[64 * half:64 * half + 32, :E], c4[64 * half + 32:64 * half + 64, E:] = a["f_cn_w4"], a["f_cn_w4"]
    tile = lambda v, n: np.concatenate([v] * n)[:, None]
    rest = _pack(W_REST, W_REST_N, {
        "c1": w1, "c1p": w1[turn], "c2": a["f_cn_w2"], "c3": c3, "c4r": c4,
        "b1": column(a["f_cn_b1"]), "b2": tile(a["f_cn_b2"], 2), "b3": tile(a["f_cn_b3"], 4),
        "b4": tile(a["f_cn_b4"], P), "range": tile(a["f_adaptive_range"], P),
        "g1": a["f_gc_w1"], "g2": a["f_gc_w2"], "g3r": np.broadcast_to(a["f_gc_w3"], (32, P)),
        "gb1": a["f_gc_b1"][:, None], "gb2": a["f_gc_b2"][:, None], "gb3": tile(a["f_gc_b3"], P),
        "q": w_q, "k": w_k, "qs": w_q[:, swap], "ks": w_k[:, swap], "vt": w_v.T.reshape(2, P, E).transpose(1, 0, 2).reshape(P, 2 * E), "gate": a["r_w_g"],
        "p0": a["r_w_p"][:P], "p1": a["r_w_p"][P:],
        "bq": column(b_q), "bk": column(b_k), "bqs": column(b_q[swap]), "bks": column(b_k[swap]),
        "bg": column(a["r_b_g"]), "b_v": np.concatenate([down(b_v[:P]), down(b_v[P:])], 1), "b_p": spread(a["r_b_p"])})
    aux, const = _constants()

    nc = _bacc.Bacc("TRN2", target_bir_lowering=False, num_devices=1)
    arrays = {"x": a["a_x"].reshape(TOK, E), "w_att": att, "w_rest": rest, "aux": aux, "const": const}
    ins = {n: nc.dram_tensor("in_" + n, v.shape, F32, kind="ExternalInput").ap() for n, v in arrays.items()}
    out = nc.dram_tensor("out_0", (TOK, E), F32, kind="ExternalOutput").ap()
    build(nc, ins, out)
    r = _run(nc, [{"in_" + n: np.ascontiguousarray(v) for n, v in arrays.items()}], core_ids=[0])
    return np.asarray(r.results[0]["out_0"]).reshape(a["a_x"].shape)
```
